# Optimizing a Trainium2 kernel written in Bass

```python
import numpy as np
import jax
import jax.numpy as jnp

def _softmax(x, axis=-1):
    return jax.nn.softmax(x, axis=axis)

def _gelu(x):
    return jax.nn.gelu(x, approximate=True)

def _silu(x):
    return jax.nn.silu(x)

def _sigmoid(x):
    return jax.nn.sigmoid(x)

def _layernorm(x, axis=-1, eps=1e-05):
    m = jnp.mean(x, axis=axis, keepdims=True)
    v = jnp.var(x, axis=axis, keepdims=True)
    return (x - m) / jnp.sqrt(v + eps)

def _scatter_add(tgt, idx, src, axis=0):
    return tgt.at[idx].add(src)

def _segment_sum(src, seg, n):
    return jax.ops.segment_sum(src, seg, n)
kernel_name = 'mk_xattn_ffn_d4_seqx_r8_90966f'

def setup_inputs(seed: int=0):
    np.random.seed(seed)
    _w = jnp.asarray

    def _rec_inputs():
        import jax
        import jax.numpy as jnp
        _rk = jax.random.key(seed)
        x = 7.22e-05 + 1 * jax.random.normal(jax.random.fold_in(_rk, 1), (1, 1024, 128), jnp.float32)
        _lenS = 1024 - jax.random.randint(jax.random.fold_in(_rk, 7), (1,), 0, max(1, 1024 // 4) + 1, jnp.int32)
        _lenS2 = 6404 - jax.random.randint(jax.random.fold_in(_rk, 8), (1,), 0, max(1, 6404 // 4) + 1, jnp.int32)
        _ctx_768P = jax.random.normal(jax.random.fold_in(_rk, 11), (1, 16, 96), jnp.float32)
        _ctx_768c = jax.random.dirichlet(jax.random.fold_in(_rk, 511), 0.3 * jnp.ones((16,), jnp.float32), (1, 6404))
        _ctx_768t = jnp.einsum('bsk,bkd->bsd', _ctx_768c, _ctx_768P)
        _ctx_768t = _ctx_768t * jax.lax.rsqrt(jnp.mean(jnp.square(_ctx_768t)) + 1e-12) * 0.953939
        ctx_768 = -0.000191848 + 0.999787 * (_ctx_768t + 0.3 * jax.random.normal(jax.random.fold_in(_rk, 611), (1, 6404, 96), jnp.float32))
        return (x, ctx_768)
    x, ctx_768 = _rec_inputs()

    def _L0_xattn_setup():
        import jax, jax.numpy as jnp
        import numpy as np
        NUM_HEADS = 16
        CLAMP = 10000.0
        key = jax.random.key(seed)
        ks = jax.random.split(key, 8)
        B, Nq, Nkv, Cq, Ckv = (4, 256, 256, 128, 96)
        s_q = 1.0 / np.sqrt(Cq)
        s_kv = 1.0 / np.sqrt(Ckv)
        return {'query': jax.random.normal(ks[0], (B, Nq, Cq), jnp.float32), 'key_value': jax.random.normal(ks[1], (B, Nkv, Ckv), jnp.float32), 'Wq': jax.random.normal(ks[2], (Cq, Cq), jnp.float32) * s_q, 'bq': jnp.zeros((Cq,), jnp.float32), 'Wk': jax.random.normal(ks[3], (Ckv, Cq), jnp.float32) * s_kv, 'bk': jnp.zeros((Cq,), jnp.float32), 'Wv': jax.random.normal(ks[4], (Ckv, Cq), jnp.float32) * s_kv, 'bv': jnp.zeros((Cq,), jnp.float32), 'Wo': jax.random.normal(ks[5], (Cq, Cq), jnp.float32) * s_q, 'bo': jnp.zeros((Cq,), jnp.float32)}
    _L0_xattn_all = _L0_xattn_setup()
    _L0_xattn_in = {k: v for k, v in _L0_xattn_all.items() if k in ('Wq', 'bq', 'Wk', 'bk', 'Wv', 'bv', 'Wo', 'bo')}
    del _L0_xattn_all

    def _L0_ffn_setup():
        import jax, jax.numpy as jnp
        import numpy as np
        EPS = 1e-12

        def _l2norm(v):
            n = jnp.sqrt(jnp.sum(v * v, axis=-1, keepdims=True))
            return v / jnp.maximum(n, EPS)
        key = jax.random.key(seed)
        ks = jax.random.split(key, 6)
        B, S, D, F, E = (2, 256, 128, 512, 8)
        std = 0.02
        return {'x': jax.random.normal(ks[0], (B, S, D), jnp.float32), 'Wp': jax.random.normal(ks[1], (D, D), jnp.float32) * (1.0 / np.sqrt(D)), 'sim_matrix': jax.random.normal(ks[2], (E, D), jnp.float32) * std, 'temperature': jnp.asarray(1.0, jnp.float32), 'W1': jax.random.normal(ks[3], (E, D, F), jnp.float32) * (1.0 / np.sqrt(D)), 'b1': jnp.zeros((E, F), jnp.float32), 'W2': jax.random.normal(ks[4], (E, F, D), jnp.float32) * (1.0 / np.sqrt(F)), 'b2': jnp.zeros((E, D), jnp.float32)}
    _L0_ffn_all = _L0_ffn_setup()
    _L0_ffn_in = {k: v for k, v in _L0_ffn_all.items() if k in ('Wp', 'sim_matrix', 'temperature', 'W1', 'b1', 'W2', 'b2')}
    del _L0_ffn_all

    def _L1_xattn_setup():
        import jax, jax.numpy as jnp
        import numpy as np
        HEADS = 16
        DIM_HEAD = 64
        key = jax.random.key(seed)
        ks = jax.random.split(key, 7)
        B, Nq, Dq = (4, 256, 128)
        Nk, Dc = (128, 96)
        inner = HEADS * DIM_HEAD
        sq = 1.0 / np.sqrt(Dq)
        sc = 1.0 / np.sqrt(Dc)
        si = 1.0 / np.sqrt(inner)
        return {'x': jax.random.normal(ks[0], (B, Nq, Dq), dtype=jnp.float32), 'context': jax.random.normal(ks[1], (B, Nk, Dc), dtype=jnp.float32), 'Wq': jax.random.normal(ks[2], (Dq, inner), dtype=jnp.float32) * sq, 'Wk': jax.random.normal(ks[3], (Dc, inner), dtype=jnp.float32) * sc, 'Wv': jax.random.normal(ks[4], (Dc, inner), dtype=jnp.float32) * sc, 'Wo': jax.random.normal(ks[5], (inner, Dq), dtype=jnp.float32) * si, 'bo': jax.random.normal(ks[6], (Dq,), dtype=jnp.float32) * 0.01}
    _L1_xattn_all = _L1_xattn_setup()
    _L1_xattn_in = {k: v for k, v in _L1_xattn_all.items() if k in ('Wq', 'Wk', 'Wv', 'Wo', 'bo')}
    del _L1_xattn_all

    def _L1_ffn_setup():
        import jax, jax.numpy as jnp
        import numpy as np
        FEATURES = 128
        D_IN = 128

        def fp8_gemm_optimized(x, input_scale, kernel, kernel_scale):
            s_in = input_scale[0]
            s_k = kernel_scale[0]
            x_q = (x.astype(jnp.float32) / s_in).astype(jnp.float8_e4m3fn)
            k_q = (kernel.astype(jnp.float32) / s_k).astype(jnp.float8_e4m3fn)
            y = jnp.dot(x_q.astype(jnp.float32), k_q.astype(jnp.float32), preferred_element_type=jnp.float32)
            return y * (s_in * s_k)
        key = jax.random.key(seed)
        kx, kk, kb = jax.random.split(key, 3)
        x = jax.random.normal(kx, (4, 1024, D_IN), dtype=jnp.float32)
        limit = np.sqrt(6.0 / (D_IN + FEATURES)).astype(np.float32)
        kernel = jax.random.uniform(kk, (D_IN, FEATURES), dtype=jnp.float32, minval=-limit, maxval=limit).astype(jnp.bfloat16)
        input_scale = jnp.ones((1,), dtype=jnp.float32)
        kernel_scale = jnp.ones((1,), dtype=jnp.float32)
        bias = jnp.zeros((FEATURES,), dtype=jnp.bfloat16)
        return {'x': x, 'kernel': kernel, 'input_scale': input_scale, 'kernel_scale': kernel_scale, 'bias': bias}
    _L1_ffn_all = _L1_ffn_setup()
    _L1_ffn_in = {k: v for k, v in _L1_ffn_all.items() if k in ('kernel', 'input_scale', 'kernel_scale', 'bias')}
    del _L1_ffn_all

    def _L2_xattn_setup():
        import jax, jax.numpy as jnp
        import numpy as np
        QUERY_DIM = 128
        KEY_DIM = 96
        NUM_HEADS = 16
        HEAD_DIM = QUERY_DIM // NUM_HEADS
        SCALE = HEAD_DIM ** (-0.5)
        key = jax.random.key(seed)
        ks = jax.random.split(key, 11)
        B, Nq, Nk = (4, 512, 128)
        s_q = QUERY_DIM ** (-0.5)
        s_k = KEY_DIM ** (-0.5)
        return {'query': jax.random.normal(ks[0], (B, Nq, QUERY_DIM), jnp.float32), 'key': jax.random.normal(ks[1], (B, Nk, KEY_DIM), jnp.float32), 'value': jax.random.normal(ks[2], (B, Nk, KEY_DIM), jnp.float32), 'Wq': jax.random.normal(ks[3], (QUERY_DIM, QUERY_DIM), jnp.float32) * s_q, 'bq': jnp.zeros((QUERY_DIM,), jnp.float32), 'Wk': jax.random.normal(ks[4], (KEY_DIM, QUERY_DIM), jnp.float32) * s_k, 'bk': jnp.zeros((QUERY_DIM,), jnp.float32), 'Wv': jax.random.normal(ks[5], (KEY_DIM, QUERY_DIM), jnp.float32) * s_k, 'bv': jnp.zeros((QUERY_DIM,), jnp.float32), 'Wo': jax.random.normal(ks[6], (QUERY_DIM, QUERY_DIM), jnp.float32) * s_q, 'bo': jnp.zeros((QUERY_DIM,), jnp.float32)}
    _L2_xattn_all = _L2_xattn_setup()
    _L2_xattn_in = {k: v for k, v in _L2_xattn_all.items() if k in ('Wq', 'bq', 'Wk', 'bk', 'Wv', 'bv', 'Wo', 'bo')}
    del _L2_xattn_all

    def _L2_ffn_setup():
        import jax, jax.numpy as jnp
        import numpy as np
        B, S, H, F, E, K = (4, 512, 128, 512, 8, 2)
        LN_EPS = 1e-05
        key = jax.random.key(seed)
        kx, kr, k1, k2 = jax.random.split(key, 4)
        x = jax.random.normal(kx, (B, S, H), dtype=jnp.float32)
        gamma = jnp.ones((H,), jnp.float32)
        beta = jnp.zeros((H,), jnp.float32)
        Wr = jax.random.normal(kr, (H, E), jnp.float32) * 0.02
        br = jnp.zeros((E,), jnp.float32)
        W1 = jax.random.normal(k1, (E, H, F), jnp.float32) * (1.0 / np.sqrt(H))
        b1 = jnp.zeros((E, F), jnp.float32)
        W2 = jax.random.normal(k2, (E, F, H), jnp.float32) * (1.0 / np.sqrt(F))
        b2 = jnp.zeros((E, H), jnp.float32)
        return {'x': x, 'gamma': gamma, 'beta': beta, 'Wr': Wr, 'br': br, 'W1': W1, 'b1': b1, 'W2': W2, 'b2': b2}
    _L2_ffn_all = _L2_ffn_setup()
    _L2_ffn_in = {k: v for k, v in _L2_ffn_all.items() if k in ('gamma', 'beta', 'Wr', 'br', 'W1', 'b1', 'W2', 'b2')}
    del _L2_ffn_all

    def _L3_xattn_setup():
        import jax, jax.numpy as jnp
        import numpy as np
        EPS = 1e-05
        key = jax.random.key(seed)
        ks = jax.random.split(key, 6)
        B, Nq, Nk, Dq, Dk = (16, 256, 256, 128, 96)
        s = lambda d: 1.0 / np.sqrt(d)
        return {'q': jax.random.normal(ks[0], (B, Nq, Dq), dtype=jnp.float32), 'k': jax.random.normal(ks[1], (B, Nk, Dk), dtype=jnp.float32), 'Wq': jax.random.normal(ks[2], (Dq, Dq), dtype=jnp.float32) * s(Dq), 'Wk': jax.random.normal(ks[3], (Dq, Dk), dtype=jnp.float32) * s(Dk), 'Wv': jax.random.normal(ks[4], (Dq, Dk), dtype=jnp.float32) * s(Dk), 'Wo': jax.random.normal(ks[5], (Dq, Dq), dtype=jnp.float32) * s(Dq)}
    _L3_xattn_all = _L3_xattn_setup()
    _L3_xattn_in = {k: v for k, v in _L3_xattn_all.items() if k in ('Wq', 'Wk', 'Wv', 'Wo')}
    del _L3_xattn_all

    def _L3_ffn_setup():
        import jax, jax.numpy as jnp
        import numpy as np
        B, S, D = (2, 64, 128)
        E, K, I = (16, 8, 128)
        I_SH = 128
        ROUTE_SCALE = 2.826
        key = jax.random.key(seed)
        ks = jax.random.split(key, 8)
        s = 0.02
        return {'x': jax.random.normal(ks[0], (B, S, D), dtype=jnp.float32), 'gate_w': jax.random.normal(ks[1], (E, D), dtype=jnp.float32) * s, 'expert_bias': jnp.zeros((E,), dtype=jnp.float32), 'w_gate': jax.random.normal(ks[2], (E, I, D), dtype=jnp.float32) * s, 'w_up': jax.random.normal(ks[3], (E, I, D), dtype=jnp.float32) * s, 'w_down': jax.random.normal(ks[4], (E, D, I), dtype=jnp.float32) * s, 'shared_gate_w': jax.random.normal(ks[5], (I_SH, D), dtype=jnp.float32) * s, 'shared_up_w': jax.random.normal(ks[6], (I_SH, D), dtype=jnp.float32) * s, 'shared_down_w': jax.random.normal(ks[7], (D, I_SH), dtype=jnp.float32) * s}
    _L3_ffn_all = _L3_ffn_setup()
    _L3_ffn_in = {k: v for k, v in _L3_ffn_all.items() if k in ('gate_w', 'expert_bias', 'w_gate', 'w_up', 'w_down', 'shared_gate_w', 'shared_up_w', 'shared_down_w')}
    del _L3_ffn_all
    return {'x': x, 'ctx_768': ctx_768, 'L0_xattn_Wq': _L0_xattn_in['Wq'], 'L0_xattn_bq': _L0_xattn_in['bq'], 'L0_xattn_Wk': _L0_xattn_in['Wk'], 'L0_xattn_bk': _L0_xattn_in['bk'], 'L0_xattn_Wv': _L0_xattn_in['Wv'], 'L0_xattn_bv': _L0_xattn_in['bv'], 'L0_xattn_Wo': _L0_xattn_in['Wo'], 'L0_xattn_bo': _L0_xattn_in['bo'], 'L0_ffn_Wp': _L0_ffn_in['Wp'], 'L0_ffn_sim_matrix': _L0_ffn_in['sim_matrix'], 'L0_ffn_temperature': _L0_ffn_in['temperature'], 'L0_ffn_W1': _L0_ffn_in['W1'], 'L0_ffn_b1': _L0_ffn_in['b1'], 'L0_ffn_W2': _L0_ffn_in['W2'], 'L0_ffn_b2': _L0_ffn_in['b2'], 'L1_xattn_Wq': _L1_xattn_in['Wq'], 'L1_xattn_Wk': _L1_xattn_in['Wk'], 'L1_xattn_Wv': _L1_xattn_in['Wv'], 'L1_xattn_Wo': _L1_xattn_in['Wo'], 'L1_xattn_bo': _L1_xattn_in['bo'], 'L1_ffn_kernel': _L1_ffn_in['kernel'], 'L1_ffn_input_scale': _L1_ffn_in['input_scale'], 'L1_ffn_kernel_scale': _L1_ffn_in['kernel_scale'], 'L1_ffn_bias': _L1_ffn_in['bias'], 'L2_xattn_Wq': _L2_xattn_in['Wq'], 'L2_xattn_bq': _L2_xattn_in['bq'], 'L2_xattn_Wk': _L2_xattn_in['Wk'], 'L2_xattn_bk': _L2_xattn_in['bk'], 'L2_xattn_Wv': _L2_xattn_in['Wv'], 'L2_xattn_bv': _L2_xattn_in['bv'], 'L2_xattn_Wo': _L2_xattn_in['Wo'], 'L2_xattn_bo': _L2_xattn_in['bo'], 'L2_ffn_gamma': _L2_ffn_in['gamma'], 'L2_ffn_beta': _L2_ffn_in['beta'], 'L2_ffn_Wr': _L2_ffn_in['Wr'], 'L2_ffn_br': _L2_ffn_in['br'], 'L2_ffn_W1': _L2_ffn_in['W1'], 'L2_ffn_b1': _L2_ffn_in['b1'], 'L2_ffn_W2': _L2_ffn_in['W2'], 'L2_ffn_b2': _L2_ffn_in['b2'], 'L3_xattn_Wq': _L3_xattn_in['Wq'], 'L3_xattn_Wk': _L3_xattn_in['Wk'], 'L3_xattn_Wv': _L3_xattn_in['Wv'], 'L3_xattn_Wo': _L3_xattn_in['Wo'], 'L3_ffn_gate_w': _L3_ffn_in['gate_w'], 'L3_ffn_expert_bias': _L3_ffn_in['expert_bias'], 'L3_ffn_w_gate': _L3_ffn_in['w_gate'], 'L3_ffn_w_up': _L3_ffn_in['w_up'], 'L3_ffn_w_down': _L3_ffn_in['w_down'], 'L3_ffn_shared_gate_w': _L3_ffn_in['shared_gate_w'], 'L3_ffn_shared_up_w': _L3_ffn_in['shared_up_w'], 'L3_ffn_shared_down_w': _L3_ffn_in['shared_down_w']}

def reference(x, ctx_768, L0_xattn_Wq, L0_xattn_bq, L0_xattn_Wk, L0_xattn_bk, L0_xattn_Wv, L0_xattn_bv, L0_xattn_Wo, L0_xattn_bo, L0_ffn_Wp, L0_ffn_sim_matrix, L0_ffn_temperature, L0_ffn_W1, L0_ffn_b1, L0_ffn_W2, L0_ffn_b2, L1_xattn_Wq, L1_xattn_Wk, L1_xattn_Wv, L1_xattn_Wo, L1_xattn_bo, L1_ffn_kernel, L1_ffn_input_scale, L1_ffn_kernel_scale, L1_ffn_bias, L2_xattn_Wq, L2_xattn_bq, L2_xattn_Wk, L2_xattn_bk, L2_xattn_Wv, L2_xattn_bv, L2_xattn_Wo, L2_xattn_bo, L2_ffn_gamma, L2_ffn_beta, L2_ffn_Wr, L2_ffn_br, L2_ffn_W1, L2_ffn_b1, L2_ffn_W2, L2_ffn_b2, L3_xattn_Wq, L3_xattn_Wk, L3_xattn_Wv, L3_xattn_Wo, L3_ffn_gate_w, L3_ffn_expert_bias, L3_ffn_w_gate, L3_ffn_w_up, L3_ffn_w_down, L3_ffn_shared_gate_w, L3_ffn_shared_up_w, L3_ffn_shared_down_w):
    import jax
    import jax.numpy as jnp

    def _L0_xattn_ref(query, key_value, Wq, bq, Wk, bk, Wv, bv, Wo, bo):
        import jax, jax.numpy as jnp
        import numpy as np
        NUM_HEADS = 16
        CLAMP = 10000.0
        B, Nq, Cq = query.shape
        Nkv = key_value.shape[1]
        H = NUM_HEADS
        D = Cq // H
        scale = D ** (-0.5)
        q = (query @ Wq + bq).reshape(B, Nq, H, D).transpose(0, 2, 1, 3)
        k = (key_value @ Wk + bk).reshape(B, Nkv, H, D).transpose(0, 2, 1, 3)
        v = (key_value @ Wv + bv).reshape(B, Nkv, H, D).transpose(0, 2, 1, 3)
        attn = jnp.einsum('bhqd,bhkd->bhqk', q, k) * scale
        attn = jnp.clip(attn, -CLAMP, CLAMP)
        attn = jax.nn.softmax(attn, axis=-1)
        attn = jnp.where(jnp.any(jnp.isnan(attn)), jnp.asarray(1.0 / Nkv, attn.dtype), attn)
        x = jnp.einsum('bhqk,bhkd->bqhd', attn, v).reshape(B, Nq, Cq)
        return x @ Wo + bo

    def _L0_ffn_ref(x, Wp, sim_matrix, temperature, W1, b1, W2, b2):
        import jax, jax.numpy as jnp
        import numpy as np
        EPS = 1e-12

        def _l2norm(v):
            n = jnp.sqrt(jnp.sum(v * v, axis=-1, keepdims=True))
            return v / jnp.maximum(n, EPS)
        E = sim_matrix.shape[0]
        top_k = 2
        proj = jnp.einsum('bsd,ed->bse', x, Wp)
        pn = _l2norm(proj)
        sn = _l2norm(sim_matrix)
        gate_scores = jnp.einsum('bsd,ed->bse', pn, sn) / temperature
        top_v, top_i = jax.lax.top_k(gate_scores, top_k)
        gate_probs = jax.nn.softmax(top_v, axis=-1)
        comb = jnp.sum(jax.nn.one_hot(top_i, E, dtype=x.dtype) * gate_probs[..., None], axis=-2)
        h = jax.nn.gelu(jnp.einsum('bsd,edf->ebsf', x, W1) + b1[:, None, None, :], approximate=False)
        eo = jnp.einsum('ebsf,efd->ebsd', h, W2) + b2[:, None, None, :]
        out = jnp.einsum('ebsd,bse->bsd', eo, comb)
        return out

    def _L1_xattn_ref(x, context, Wq, Wk, Wv, Wo, bo):
        import jax, jax.numpy as jnp
        import numpy as np
        HEADS = 16
        DIM_HEAD = 64
        B, Nq, _ = x.shape
        Nk = context.shape[1]
        h, dh = (HEADS, DIM_HEAD)
        q = (x @ Wq).reshape(B, Nq, h, dh)
        k = (context @ Wk).reshape(B, Nk, h, dh)
        v = (context @ Wv).reshape(B, Nk, h, dh)
        scale = 1.0 / jnp.sqrt(jnp.asarray(dh, dtype=x.dtype))
        scores = jnp.einsum('bqhd,bkhd->bhqk', q, k) * scale
        attn = jax.nn.softmax(scores, axis=-1)
        out = jnp.einsum('bhqk,bkhd->bqhd', attn, v).reshape(B, Nq, h * dh)
        return out @ Wo + bo

    def _L1_ffn_ref(x, kernel, input_scale, kernel_scale, bias):
        import jax, jax.numpy as jnp
        import numpy as np
        FEATURES = 128
        D_IN = 128

        def fp8_gemm_optimized(x, input_scale, kernel, kernel_scale):
            s_in = input_scale[0]
            s_k = kernel_scale[0]
            x_q = (x.astype(jnp.float32) / s_in).astype(jnp.float8_e4m3fn)
            k_q = (kernel.astype(jnp.float32) / s_k).astype(jnp.float8_e4m3fn)
            y = jnp.dot(x_q.astype(jnp.float32), k_q.astype(jnp.float32), preferred_element_type=jnp.float32)
            return y * (s_in * s_k)
        dtype = jnp.bfloat16
        x = x.astype(dtype)
        orig_shape = x.shape
        x2 = x.reshape(-1, x.shape[-1])
        y = fp8_gemm_optimized(x2, input_scale, kernel, kernel_scale)
        y = y.astype(dtype) + bias
        return y.reshape(orig_shape[:-1] + (FEATURES,))

    def _L2_xattn_ref(query, key, value, Wq, bq, Wk, bk, Wv, bv, Wo, bo):
        import jax, jax.numpy as jnp
        import numpy as np
        QUERY_DIM = 128
        KEY_DIM = 96
        NUM_HEADS = 16
        HEAD_DIM = QUERY_DIM // NUM_HEADS
        SCALE = HEAD_DIM ** (-0.5)
        B, Nq, _ = query.shape
        Nk = key.shape[1]
        q = (query @ Wq + bq).reshape(B, Nq, NUM_HEADS, HEAD_DIM).transpose(0, 2, 1, 3)
        k = (key @ Wk + bk).reshape(B, Nk, NUM_HEADS, HEAD_DIM).transpose(0, 2, 1, 3)
        v = (value @ Wv + bv).reshape(B, Nk, NUM_HEADS, HEAD_DIM).transpose(0, 2, 1, 3)
        attn = jnp.einsum('bhqd,bhkd->bhqk', q, k) * SCALE
        attn = jax.nn.softmax(attn, axis=-1)
        out = jnp.einsum('bhqk,bhkd->bhqd', attn, v)
        out = out.transpose(0, 2, 1, 3).reshape(B, Nq, QUERY_DIM)
        return out @ Wo + bo

    def _L2_ffn_ref(x, gamma, beta, Wr, br, W1, b1, W2, b2):
        import jax, jax.numpy as jnp
        import numpy as np
        B, S, H, F, E, K = (4, 512, 128, 512, 8, 2)
        LN_EPS = 1e-05
        residual = x
        mu = jnp.mean(x, axis=-1, keepdims=True)
        var = jnp.var(x, axis=-1, keepdims=True)
        xn = (x - mu) * jax.lax.rsqrt(var + LN_EPS) * gamma + beta
        probs = jax.nn.softmax(xn @ Wr + br, axis=-1)
        scores, idx = jax.lax.top_k(probs, K)

        def expert_fn(w):
            W1_e, b1_e, W2_e, b2_e = w
            return jax.nn.relu(xn @ W1_e + b1_e) @ W2_e + b2_e
        full = jax.lax.map(expert_fn, (W1, b1, W2, b2))
        full = jnp.moveaxis(full, 0, 2)
        c = jnp.einsum('ef,efh->eh', jax.nn.relu(b1), W2) + b2
        c_total = c.sum(axis=0)
        sel_full = jnp.take_along_axis(full, idx[..., None], axis=2)
        c_sel = c[idx]
        output = jnp.sum(scores[..., None] * (sel_full - c_sel + c_total), axis=2)
        return residual + output

    def _L3_xattn_ref(q, k, Wq, Wk, Wv, Wo):
        import jax, jax.numpy as jnp
        import numpy as np
        EPS = 1e-05
        query = q @ Wq.T
        key_p = k @ Wk.T
        value = k @ Wv.T
        sim = jnp.einsum('bqd,bkd->bqk', query, key_p)
        mean = jnp.mean(sim, axis=(1, 2), keepdims=True)
        var = jnp.var(sim, axis=(1, 2), keepdims=True)
        sim = (sim - mean) * jax.lax.rsqrt(var + EPS)
        attn = jax.nn.softmax(sim, axis=-1)
        out = jnp.einsum('bqk,bkd->bqd', attn, value)
        return out @ Wo.T

    def _L3_ffn_ref(x, gate_w, expert_bias, w_gate, w_up, w_down, shared_gate_w, shared_up_w, shared_down_w):
        import jax, jax.numpy as jnp
        import numpy as np
        B, S, D = (2, 64, 128)
        E, K, I = (16, 8, 128)
        I_SH = 128
        ROUTE_SCALE = 2.826
        gates = jnp.einsum('bsd,ed->bse', x, gate_w)
        scores = jax.nn.sigmoid(gates.astype(jnp.float32))
        sel_scores = scores + expert_bias
        _, inds = jax.lax.top_k(sel_scores, K)
        selected = jnp.take_along_axis(scores, inds, axis=-1)
        selected = selected / selected.sum(axis=-1, keepdims=True)
        selected = selected * ROUTE_SCALE
        onehot = jax.nn.one_hot(inds, E, dtype=selected.dtype)
        combine = jnp.einsum('bske,bsk->bse', onehot, selected)
        hg = jnp.einsum('bsd,eid->bsei', x, w_gate)
        hu = jnp.einsum('bsd,eid->bsei', x, w_up)
        h = jax.nn.silu(hg) * hu
        ye = jnp.einsum('bsei,edi->bsed', h, w_down)
        y = jnp.einsum('bsed,bse->bsd', ye, combine).astype(x.dtype)
        g = jnp.einsum('bsd,id->bsi', x, shared_gate_w)
        u = jnp.einsum('bsd,id->bsi', x, shared_up_w)
        y = y + jnp.einsum('bsi,di->bsd', jax.nn.silu(g) * u, shared_down_w)
        return y
    x = x + _L0_xattn_ref(_layernorm(x, axis=-1), ctx_768, L0_xattn_Wq, L0_xattn_bq, L0_xattn_Wk, L0_xattn_bk, L0_xattn_Wv, L0_xattn_bv, L0_xattn_Wo, L0_xattn_bo)
    x = x + _L0_ffn_ref(_layernorm(x, axis=-1), L0_ffn_Wp, L0_ffn_sim_matrix, L0_ffn_temperature, L0_ffn_W1, L0_ffn_b1, L0_ffn_W2, L0_ffn_b2)
    x = x + _L1_xattn_ref(_layernorm(x, axis=-1), ctx_768, L1_xattn_Wq, L1_xattn_Wk, L1_xattn_Wv, L1_xattn_Wo, L1_xattn_bo)
    x = x + _L1_ffn_ref(_layernorm(x, axis=-1), L1_ffn_kernel, L1_ffn_input_scale, L1_ffn_kernel_scale, L1_ffn_bias)
    x = x + _L2_xattn_ref(_layernorm(x, axis=-1), ctx_768, ctx_768, L2_xattn_Wq, L2_xattn_bq, L2_xattn_Wk, L2_xattn_bk, L2_xattn_Wv, L2_xattn_bv, L2_xattn_Wo, L2_xattn_bo)
    x = x + _L2_ffn_ref(_layernorm(x, axis=-1), L2_ffn_gamma, L2_ffn_beta, L2_ffn_Wr, L2_ffn_br, L2_ffn_W1, L2_ffn_b1, L2_ffn_W2, L2_ffn_b2)
    x = x + _L3_xattn_ref(_layernorm(x, axis=-1), ctx_768, L3_xattn_Wq, L3_xattn_Wk, L3_xattn_Wv, L3_xattn_Wo)
    x = x + _L3_ffn_ref(_layernorm(x, axis=-1), L3_ffn_gate_w, L3_ffn_expert_bias, L3_ffn_w_gate, L3_ffn_w_up, L3_ffn_w_down, L3_ffn_shared_gate_w, L3_ffn_shared_up_w, L3_ffn_shared_down_w)
    return x

_drawn_inputs = setup_inputs


def setup_inputs(seed=0):
    import zlib

    import numpy as np

    out = dict(_drawn_inputs(seed))
    spreads = {'L0_xattn_bq': (0.0, 0.1),
     'L0_xattn_bk': (0.0, 0.8),
     'L0_xattn_bv': (0.0, 0.1),
     'L0_xattn_bo': (0.0, 0.1),
     'L0_ffn_b1': (0.0, 0.1),
     'L0_ffn_b2': (0.0, 0.1),
     'L2_xattn_bq': (0.0, 0.638),
     'L2_xattn_bk': (0.0, 0.8),
     'L2_xattn_bv': (0.0, 0.1),
     'L2_xattn_bo': (0.0, 0.1),
     'L2_ffn_gamma': (1.0, 0.574),
     'L2_ffn_beta': (0.0, 0.566),
     'L2_ffn_br': (0.0, 0.1),
     'L2_ffn_b1': (0.0, 0.363),
     'L2_ffn_b2': (0.0, 0.1),
     'L3_ffn_expert_bias': (0.0, 0.8)}
    factors = {'L1_xattn_bo': 4.414,
     'L3_ffn_gate_w': 8.0,
     'L3_ffn_w_gate': 8.0,
     'L3_ffn_w_up': 8.0,
     'L3_ffn_w_down': 8.0,
     'L3_ffn_shared_gate_w': 8.0,
     'L3_ffn_shared_up_w': 8.0,
     'L3_ffn_shared_down_w': 8.0}
    for name, (base, spread) in spreads.items():
        noise = np.random.default_rng([zlib.crc32(name.encode()), seed]).standard_normal(out[name].shape)
        drawn = base * np.exp(spread * noise) if base else spread * noise
        out[name] = jnp.asarray(drawn.astype(out[name].dtype))
    for name, factor in factors.items():
        out[name] = (out[name] * factor).astype(out[name].dtype)
    return out
```

```python
from contextlib import ExitStack

import concourse.bass as bass
from concourse import mybir

F32 = mybir.dt.float32
F32R = mybir.dt.float32r
I32 = mybir.dt.int32
BF16 = mybir.dt.bfloat16
ACT = mybir.ActivationFunctionType
ALU = mybir.AluOpType
AX = mybir.AxisListType

P = 128
D = 128
C = 96
T = 1024
NT = T // P
HT = 512
S = 6404
SF = S // P
TAIL = S - SF * P
ST = SF + 1
SP = ST * P
H = 16
CHUNKS = [(c, min(HT, SP - c)) for c in range(0, SP, HT)]
NC = len(CHUNKS)
VG = [(t, min(4, ST - t)) for t in range(0, ST, 4)]
NVG = len(VG)
E8 = 8
F = 512
NF = F // P
E16 = 16
HD8 = D // H
G = 4
NG = H // G
HD64 = 64
NP = H // 2
LN_EPS = 1e-5
TINY = 1e-12
ROUTE_SCALE = 2.826
FP8_MAX = 448.0
LIMIT = 60.0
CLIP = 1e4 * HD8 ** 0.5
HUGE = 3e38
SHRINK = 2.0 ** -20
RING = 3
KP_PIECES = [(0, 2), (2, 2), (4, 2), (6, 2), (8, 2), (10, 2), (12, 1)]

TILES = {0: 0, 1: 2 * NG * ST, 2: 2 * NG * ST + H * ST, 3: 4 * NG * ST + H * ST}
UNITS = {0: 0, 1: 4 * NG * ST, 2: 4 * NG * ST + H * ST, 3: 8 * NG * ST + H * ST}
SUMS = {0: 0, 1: 2 * NG, 2: 2 * NG + H, 3: 4 * NG + H}
CHUNKED = {0: 0, 1: NC, 2: (1 + NP) * NC}
QSPLIT = {0: 0, 1: 2, 2: 2 + 4 * NP}
QPROJ = {0: 0, 1: 1, 2: 1 + 2 * NP}
assert NVG == NC and ST % RING == 0
NCONST = 26
ADDED = {1: 0, 3: H * ST}
NCOLS = 19
WOUT = {0: 0, 1: 1, 2: 1 + NP, 3: 2 + NP}


def build_program(nc, a):
    ctx = ExitStack()
    with ctx:
        def sb(name, shape, dt=F32):
            return ctx.enter_context(nc.sbuf_tensor(name, shape, dt))

        def sem(name):
            return ctx.enter_context(nc.semaphore(name))

        ps = ctx.enter_context(nc.psum_tensor("ps", [P, 8, HT], F32))

        xT = sb("xT", [P, 2, HT])
        work = sb("work", [P, 4, 2, HT])
        z, t1, t2, t3 = (work[:, n] for n in range(4))
        sums = work[:, :, :, :].rearrange("p a h n -> p (a h) n")
        ctxT = sb("ctxT", [P, SP])
        kb = sb("kb", [P, 2, SP], F32R)
        klo = sb("klo", [P, 2, 2 * HT])
        vbuf = sb("vbuf", [P, ST * H * (HD8 + 1)])
        qz = sb("qz", [P, 4 * 2 * HT], F32R)
        qs = sb("qs", [P, 2, 2 * HT])
        probs = sb("probs", [P, RING, 4 * HT])
        kst = sb("kst", [P, RING, P], F32R)
        vst = sb("vst", [P, RING, P])
        cst = sb("cst", [P, RING, P])
        w8 = sb("w8", [P, 2, 3 + NG, P])
        w64 = sb("w64", [P, 6, P])
        wT = sb("wT", [P, 6, P])
        wk3 = sb("wk3", [P, P])
        kernel8 = sb("kernel8", [P, P], BF16)
        cols = sb("cols", [P, 16])
        z8 = sb("z8", [P, 2, HT], BF16)
        kernel8q = sb("kernel8q", [P, P], BF16)
        wr2 = sb("wr2", [P, E8])
        bias8 = sb("bias8", [P, 1], BF16)
        b1c = sb("b1c", [P, 2, E8 * NF])
        rb1 = sb("rb1", [P, 3, E8 * NF])
        b2c = sb("b2c", [P, 2, E8])
        brow = sb("brow", [P, E8])
        ebrow = sb("ebrow", [P, E16])
        ident = sb("ident", [P, P])
        ones = sb("ones", [P, P])
        ones_b = sb("ones_b", [P, P], BF16)
        mean_d = sb("mean_d", [P, P])
        mean_s = sb("mean_s", [P, P])
        dsel = sb("dsel", [P, P])
        before = sb("before", [P, E16, E16])
        ccol = sb("ccol", [P, 2, NT])
        stat = sb("stat", [P, 32])
        cov = sb("cov", [P, P])
        heads = sb("heads", [P, 32], BF16)
        peak = sb("peak", [P, 18])
        bnd = sb("bnd", [P, 8])
        given = sb("given", [P, 26])
        warm = sb("warm", [P, 6])
        cpeak = sb("cpeak", [P, 2])

        csum = t1[:, 0, 0:C]
        shared = vbuf[:, 6 * P:9 * P].rearrange("p (m n) -> p m n", m=3)
        turned = cst
        route = qs[:, :, :].rearrange("p l (m n) -> p (l m) n", m=8)
        xn = probs[:, 0, 0:NT * D].rearrange("p (t d) -> p t d", t=NT)
        wn = probs[:, 1, 0:6 * P].rearrange("p (m n) -> p m n", m=6)
        cn = vbuf[:, 0:ST * C].rearrange("p (t c) -> p t c", t=ST)
        cn_sq = kb[:, 0, 0:ST * C].bitcast(F32).rearrange("p (t c) -> p t c", t=ST)
        cn_len = kb[:, 1, 0:ST].bitcast(F32)
        vx = vbuf[:, :].rearrange("p (t h w) -> p t h w", t=ST, h=H)
        vp = vbuf[:, 0:ST * P]
        qh = qz[:, :].rearrange("p (s j n) -> p s j n", s=2, j=G)
        qp = qz[:, :].rearrange("p (e l h n) -> p e l h n", e=2, l=2, h=2)
        hid = probs[:, 0:2, :].rearrange("p a (f h n) -> p (a f) h n", f=2, h=2)
        flat = probs[:, :, :].rearrange("p a n -> p (a n)")
        kscr = nc.dram_tensor("k_scratch", [2, 2, P, SP], F32, kind="Internal").ap()
        qscr = nc.dram_tensor("q_scratch", [2, 2, P, T], F32, kind="Internal").ap()
        BQ0, BO0, BQ2, BO2, BO1, GAM, BET, TEMP, SIN, SK, EPS, MODE = range(12)
        top = klo[:, :, :].rearrange("p a (b n) -> p (a b) n", n=HT)
        topcol = ccol[:, :, :].rearrange("p a t -> p (a t)")
        wqk1 = vbuf[:, 0:2 * T].rearrange("p (m n) -> p m n", m=2)
        gram = vbuf[:, 2 * T:2 * T + T // 2].bitcast(BF16).rearrange("p (m n) -> p m n", n=P)
        t1b, t2b, t3b = (work[:, n].bitcast(BF16)[:, :, 0:HT] for n in (1, 2, 3))

        ex_w = [vbuf[:, u * 3 * P:(u + 1) * 3 * P].rearrange("p (m n) -> p m n", m=3) for u in range(2)]
        stores = [[n * (NC + 1 - c % 2) // 2 * 1 + c // 2 for c in range(NC)] for n in range(2)]

        def col(n):
            return cols[:, n:n + 1]

        def tok(ap, t):
            return ap[:, t // 4, (t % 4) * P:(t % 4 + 1) * P]

        names = (
            "consts_set pool_step in_x in_ctx0 in_ctx1 in_nat in_cols in_w0 in_w2 x_turned ctx_turned ctx_even "
            "ctx_odd w_turned w_copied sim_sq sim_root sim_ready gate_turned csum_ready cmean_ready ccent_ready "
            "cov_ready cov_copied dve_step act_step x_ready ln_mean ln_cent ln_sq ln_var ln_std z_ready "
            "q_proj q_split q_scr k_proj k_high k_split v_proj v_copied v_ones q_zeroed "
            "staged scores_ready exp_done av_done acc_copied added den_ready o_done wo_ready x_added "
            "p_proj p_ready g_proj n_root comb_ready ccol_ready h_ready hid_ready eo_ready eo_used cb_ready "
            "cb_copied moe_acc sum_ready w1_in k1_high f8_ready f8_done den8 y_ready "
            "q3_proj q3_ready q3_next q3_score s3_ready s3_root v3_copied wt_turned wt_copied hg_ready hg_act "
            "hd_ready ex_w0 ex_w1 moe_w0 moe_w1 k_scr0 k_scr1 k_in0 k_in1 q_in0 q_in1 klo_out0 klo_out1 "
            "out_turned out_ready out_stored in_shared in_wk3 rb_ready route_in route_act rec_ready hm_ready"
        ).split()
        names += ("norm_sq norm_mm norm_max bound_in bound_out mode_set ctx_sq cpeak_in cpeak_out in_qk1 "
                  "gram_ready gram_copied b1_q b1_copied b1_r b1_prod b1_sum b1_max b3_sq b3_sum").split()
        names += [f"{n}{l}" for n in ("max_staged", "max_scores", "max_read", "max_spread", "max_known", "shift_sub", "shifted")
                  for l in range(4)]
        s = {n: sem(n) for n in names}

        def mode_of(engine, layer):
            engine.wait_ge(s["mode_set"], layer + 1)
            return engine.value_load(cols[0:1, MODE + layer:MODE + layer + 1].bitcast(I32), min_val=0, max_val=2)

        block = ctx.enter_context(nc.Block())

        @block.tensor
        def _(pe):
            def layernorm(k):
                src = z if k == 6 else xT[:, :, :]
                if k == 6:
                    pe.wait_ge(s["z_ready"], 6)
                else:
                    pe.wait_ge(s["x_ready"], k + 1 if k < 6 else k)
                for h in range(2):
                    mm = pe.matmul(ps[:, h, :], mean_d[:, :], src[:, h, :], start=True, stop=True)
                mm.then_inc(s["ln_mean"], 1)
                pe.wait_ge(s["ln_sq"], k + 1)
                for h in range(2):
                    mm = pe.matmul(ps[:, 2 + h, :], mean_d[:, :], t2[:, h, :], start=True, stop=True)
                mm.then_inc(s["ln_var"], 1)

            def stream(first, qk, av):
                qk(first, 0)
                for t in range(RING):
                    qk(first + t + 1, (t + 1) % RING)
                    av(first + t, t, t == 0, False)
                with pe.Fori(0, ST // RING - 2) as i:
                    for u in range(RING):
                        qk(first + i * RING + RING + u + 1, (u + 1) % RING)
                        av(first + i * RING + RING + u, u, False, False)
                for t in range(ST - RING, ST):
                    if t + 1 < ST:
                        qk(first + t + 1, (t + 1) % RING)
                    av(first + t, t % RING, False, t + 1 == ST)

            def maxima(layer, count, banks, units, qk):
                with pe.Fori(0, ST) as t:
                    pe.wait_ge(s["exp_done"], UNITS[layer] + RING + count * units)
                    pe.wait_ge(s[f"max_staged{layer}"], count * ST + t + 1)
                    pe.wait_ge(s[f"max_read{layer}"], count * ST + t + 1)
                    qk().then_inc(s[f"max_scores{layer}"], 1)
                pe.wait_ge(s[f"max_read{layer}"], count * ST + ST + 1)
                for b in range(4 * banks):
                    mm = pe.transpose(ps[:, b // 4, (b % 4) * P:(b % 4 + 1) * P],
                                      top[:, b // 4, (b % 4) * P:(b % 4 + 1) * P], ident[:, :])
                mm.then_inc(s[f"max_spread{layer}"], 1)
                pe.wait_ge(s[f"max_known{layer}"], count * 2 + 1)
                for b in range(4 * banks):
                    mm = pe.matmul(ps[:, b // 4, (b % 4) * P:(b % 4 + 1) * P], topcol[:, b:b + 1].to_broadcast([P, P]),
                                   ident[:, :], start=True, stop=True)
                mm.then_inc(s[f"max_spread{layer}"], 1)
                pe.wait_ge(s[f"max_known{layer}"], count * 2 + 2)

            def spread_bound(layer):
                pe.wait_ge(s["bound_in"], layer + 1)
                pe.matmul(ps[:, 2, 0:P], bnd[:, 2 * layer:2 * layer + 1].to_broadcast([P, P]), ident[:, :], start=True, stop=True)
                pe.matmul(ps[:, 2, P:P + 1], ones[:, :], bnd[:, 2 * layer + 1:2 * layer + 2], start=True, stop=True)\
                    .then_inc(s["bound_out"], 1)

            pe.wait_ge(s["consts_set"], NCONST)
            pe.wait_ge(s["in_x"], 16)
            for t in range(NT):
                mm = pe.transpose(ps[:, t // 4, (t % 4) * P:(t % 4 + 1) * P], xn[:, t, :], ident[:, :])
            mm.then_inc(s["x_turned"], 1)
            pe.wait_ge(s["in_ctx0"], 16)
            pe.wait_ge(s["in_ctx1"], 16)
            for g, (t0, n) in enumerate(VG):
                if g >= 4:
                    pe.wait_ge(s["ctx_odd" if g % 2 else "ctx_even"], (g - 4) // 2 + 1)
                for u in range(n):
                    mm = pe.transpose(ps[0:C, 2 + g % 4, u * P:(u + 1) * P], cn[:, t0 + u, :], ident[:, :])
                mm.then_inc(s["ctx_turned"], 1)
            pe.wait_ge(s["in_nat"], 16 * 6)
            for m, w in enumerate((P, P, P, C)):
                mm = pe.transpose(ps[0:w, 6, m * P:(m + 1) * P], wn[:, m, 0:w], ident[:, :])
            mm.then_inc(s["w_turned"], 1)
            pe.wait_ge(s["sim_ready"], 1)
            pe.transpose(ps[:, 7, 0:E16], wn[0:E16, 4, :], ident[0:E16, 0:E16])
            pe.transpose(ps[:, 7, E16:E16 + E8], wn[0:E8, 5, :], ident[0:E8, 0:E8]).then_inc(s["gate_turned"], 1)
            pe.wait_ge(s["csum_ready"], 1)
            pe.wait_ge(s["x_ready"], 1)
            pe.matmul(ps[:, 0, 0:C], mean_s[:, :], csum[:, :], start=True, stop=True)
            pe.matmul(ps[0:C, 0, P:P + 1], csum[:, :], mean_s[:, 0:1], start=True, stop=True).then_inc(s["cmean_ready"], 1)
            pe.wait_ge(s["cpeak_in"], 1)
            pe.matmul(ps[:, 0, 2 * P:3 * P], cpeak[:, 0:1].to_broadcast([P, P]), ident[:, :], start=True, stop=True)\
                .then_inc(s["cpeak_out"], 1)
            pe.wait_ge(s["ccent_ready"], 1)
            for t in range(ST):
                k = P if t < SF else TAIL
                mm = pe.matmul(ps[0:C, 1, 0:C], cn[0:k, t, :], cn[0:k, t, :], start=(t == 0), stop=(t == ST - 1))
            mm.then_inc(s["cov_ready"], 1)

            def attention8(n, layer, ln):
                w = w8[:, n]
                pe.wait_ge(s["in_w2" if n else "in_w0"], 16 * 9)
                pe.wait_ge(s["z_ready"], ln + 1)
                for h in range(2):
                    mm = pe.matmul(ps[:, h, :], w[:, 0, :], z[:, h, :], start=True, stop=True)
                mm.then_inc(s["q_proj"], 1)
                if n == 0:
                    pe.wait_ge(s["w_copied"], 1)
                    pe.wait_ge(s["ctx_even"], (NVG + 1) // 2)
                    pe.wait_ge(s["ctx_odd"], NVG // 2)
                base = n * (NC + 1)

                def norms(c):
                    wd = CHUNKS[c][1]
                    pe.wait_ge(s["norm_sq"], base + c + 2)
                    if c >= 2:
                        pe.wait_ge(s["norm_max"], base + c)
                    mm = pe.matmul(ps[0:32, 2 + c % 2, 0:wd], heads[:, :], t3b[:, c % 2, 0:wd],
                                   start=True, stop=True)
                    if c < NC - 1:
                        if c == 0:
                            pe.wait_ge(s["norm_max"], base + 1)
                        mm = pe.matmul(ps[0:32, 1, 0:wd], heads[:, :], t3b[:, c % 2, 0:wd],
                                       start=(c == 0), stop=(c == NC - 2))
                    mm.then_inc(s["norm_mm"], 1)

                pe.wait_ge(s["norm_sq"], base + 1)
                for h in range(2):
                    mm = pe.matmul(ps[0:32, h, :], heads[:, :], t2b[:, h, :], start=True, stop=True)
                mm.then_inc(s["norm_mm"], 1)
                for c, (c0, wd) in enumerate(CHUNKS):
                    if c >= 1:
                        norms(c - 1)
                    if c >= 2:
                        pe.wait_ge(s["k_split"], CHUNKED[layer] + c - 1)
                    pe.matmul(ps[:, 6 + c % 2, 0:wd], w[:, 1, :], ctxT[:, c0:c0 + wd], start=True, stop=True)\
                        .then_inc(s["k_proj"], 1)
                    t0, m = VG[c]
                    if c >= 2:
                        pe.wait_ge(s["v_copied"], CHUNKED[layer] + c - 1)
                    for u in range(m):
                        mm = pe.matmul(ps[:, 4 + c % 2, u * P:(u + 1) * P], ctxT[:, (t0 + u) * P:(t0 + u + 1) * P],
                                       w[:, 2, :], start=True, stop=True)
                    mm.then_inc(s["v_proj"], 1)

                norms(NC - 1)
                pe.wait_ge(s["norm_max"], base + 1 + NC)
                spread_bound(layer)
                mode = mode_of(pe, layer)

                def group(gi, par):
                    g = gi * 2 + par
                    for half in range(2):
                        def qk_maxima():
                            for j in range(G):
                                mm = pe.matmul(ps[:, j, :], kst[:, 0, :], qh[:, half, j, :], start=True, stop=True)
                            return mm

                        local = (g * 2 + half) * ST
                        pe.wait_ge(s[f"q_in{half}"], g * (32 * G) + 32 * G * (NG * n + 1))

                        def qk(t, r):
                            pe.wait_ge(s["staged"], t * 2 + 2)
                            for b in range(2):
                                buf = (2 * r + b) % RING
                                pe.wait_ge(s["exp_done"], (t - TILES[layer]) * 2 + UNITS[layer] + b + 1)
                                for j in range(2):
                                    mm = pe.matmul(ps[:, 2 * buf + j, :], kst[:, r, :], qh[:, half, 2 * b + j, :],
                                                   start=True, stop=True)
                                mm.then_inc(s["scores_ready"], 1)

                        def av(t, r, start, stop):
                            if start:
                                pe.wait_ge(s["acc_copied"], g * 2 + half + SUMS[layer] + 1)
                            pe.wait_ge(s["exp_done"], (t - TILES[layer]) * 2 + UNITS[layer] + 2 + RING)
                            for j in range(G):
                                mm = pe.matmul(ps[32 * j:32 * j + 32, 6 + half, :], vst[:, r, 32 * j:32 * j + 32],
                                               probs[:, r, j * HT:(j + 1) * HT], start=start, stop=stop)
                            mm.then_inc(s["av_done"], 1)

                        with pe.If(mode >= 1):
                            maxima(layer, g * 2 + half, G, 2 * ST, qk_maxima)
                        stream(local + TILES[layer], qk, av)

                pe.wait_ge(s["v_copied"], CHUNKED[layer] + NVG)
                pe.wait_ge(s["k_split"], CHUNKED[layer] + NC)
                pe.wait_ge(s["q_split"], QSPLIT[layer] + 2)
                with pe.Fori(0, NG // 2) as gi:
                    for par in range(2):
                        group(gi, par)
                for gh in range(2 * NG):
                    pe.wait_ge(s["acc_copied"], SUMS[layer] + 2 + gh + 1)
                    if gh >= 4:
                        pe.wait_ge(s["o_done"], SUMS[layer] + gh - 3)
                    pe.matmul(ps[:, gh % 4, :], dsel[:, :], sums[:, gh, :], start=True, stop=True).then_inc(s["den8"], 1)
                pe.wait_ge(s["o_done"], SUMS[layer] + 2 * NG)
                for half in range(2):
                    for g in range(NG):
                        mm = pe.matmul(ps[:, 4 + half, :], w[:, 3 + g, :], sums[:, 2 * g + half, :],
                                       start=(g == 0), stop=(g == NG - 1))
                mm.then_inc(s["wo_ready"], 1)

            def experts8(m):
                def expert(i, u):
                    e = i * 2 + u
                    n = e + E8 * m
                    wts = vbuf[:, u * 2 * F:(u + 1) * 2 * F]
                    pe.wait_ge(s[f"moe_w{u}"], i * 32 + 32 * (E8 // 2 * m + 1))
                    for f in range(NF):
                        pe.wait_ge(s["hid_ready"], n * NF + f + 1)
                        for h in range(2):
                            mm = pe.matmul(ps[:, 2 * (f % 2) + h, :], wts[:, f * P:(f + 1) * P], z[:, h, :],
                                           start=True, stop=True)
                        mm.then_inc(s["h_ready"], 1)
                    pe.wait_ge(s["ccol_ready"], n + 1)
                    for h in range(2):
                        pe.wait_ge(s["cb_copied"], n * 2 + h + 1)
                        for t in range(4):
                            mm = pe.matmul(ps[:, 6, t * P:(t + 1) * P],
                                           ccol[:, u, 4 * h + t:4 * h + t + 1].to_broadcast([P, P]), ident[:, :],
                                           start=True, stop=True)
                        mm.then_inc(s["cb_ready"], 1)
                        if h == 0:
                            pe.wait_ge(s["eo_used"], n + 1)
                            if m == 1:
                                for f in range(NF):
                                    pe.matmul(ps[:, 7, bass.ds(e, 1)], wts[:, F + f * D:F + (f + 1) * D],
                                              rb1[:, 0, bass.ds(e * NF + f, 1)], start=(f == 0), stop=(f == NF - 1))
                        for f in range(NF):
                            pe.wait_ge(s["hid_ready"], n * NF + f + 3)
                            mm = pe.matmul(ps[:, 4 + h, :], wts[:, F + f * D:F + (f + 1) * D], hid[:, f, h, :],
                                           start=(f == 0), stop=(f == NF - 1))
                    mm.then_inc(s["eo_ready"], 1)

                if m == 1:
                    pe.wait_ge(s["rb_ready"], 1)
                with pe.Fori(0, E8 // 2) as i:
                    for u in range(2):
                        expert(i, u)

            pe.wait_ge(s["cov_copied"], 1)
            layernorm(0)
            attention8(0, 0, 0)

            layernorm(1)
            pe.wait_ge(s["z_ready"], 2)
            for h in range(2):
                mm = pe.matmul(ps[:, h, :], wT[:, 0, :], z[:, h, :], start=True, stop=True)
            mm.then_inc(s["p_proj"], 1)
            pe.wait_ge(s["p_ready"], 1)
            for t in range(NT):
                pe.matmul(ps[:, 2, t * E16:t * E16 + E8], tok(t1, t), wT[:, 5, 0:E8], start=True, stop=True)
                mm = pe.matmul(ps[:, 2, t * E16 + E8:t * E16 + E8 + 1], tok(t2, t), ones[:, 0:1], start=True, stop=True)
            mm.then_inc(s["g_proj"], 1)
            pe.wait_ge(s["comb_ready"], 1)
            experts8(0)

            layernorm(2)
            pe.wait_ge(s["z_ready"], 3)
            pe.wait_ge(s["in_qk1"], 32)
            for p in range(NP):
                cut = slice(p * P, (p + 1) * P)
                mm = pe.matmul(ps[:, 6 + p // 4, (p % 4) * P:(p % 4 + 1) * P], wqk1[0:C, 0, cut], wqk1[0:C, 0, cut],
                               start=True, stop=True)
            mm.then_inc(s["gram_ready"], 1)

            def pair_squares(p):
                pe.wait_ge(s["gram_copied"], 2)
                pe.wait_ge(s["b1_copied"], p + 1)
                pe.wait_ge(s["b1_prod"], p + 1)
                for h in range(2):
                    mm = pe.matmul(ps[:, 4 + h, :], gram[:, p, :],
                                   (t2b, t3b)[p % 2][:, h, :], start=True, stop=True)
                mm.then_inc(s["b1_r"], 1)

            def pair_sums(p):
                pe.wait_ge(s["b1_prod"], p + 2)
                if p:
                    pe.wait_ge(s["b1_max"], p)
                for h in range(2):
                    mm = pe.matmul(ps[:, 6 + h, :], ones_b[:, :], t1b[:, h, :], start=True, stop=True)
                mm.then_inc(s["b1_sum"], 1)

            for p in range(NP):
                if p >= 2:
                    pe.wait_ge(s["b1_copied"], p - 1)
                for h in range(2):
                    mm = pe.matmul(ps[:, 2 * (p % 2) + h, :], wqk1[:, 1, p * P:(p + 1) * P], z[:, h, :], start=True, stop=True)
                mm.then_inc(s["b1_q"], 1)
                if p:
                    pair_squares(p - 1)
                    pair_sums(p - 1)
            pair_squares(NP - 1)
            pair_sums(NP - 1)
            pe.wait_ge(s["b1_copied"], NP)
            spread_bound(1)
            mode1 = mode_of(pe, 1)
            with pe.Fori(0, NP) as p:
                pe.wait_ge(s["w1_in"], p * 96 + 96)
                pe.wait_ge(s["x_added"], p + 1)
                for e in range(2):
                    for h in range(2):
                        mm = pe.matmul(ps[:, 2 * e + h, :], w64[:, e, :], z[:, h, :], start=True, stop=True)
                    mm.then_inc(s["q_proj"], 1)
                for c, (c0, wd) in enumerate(CHUNKS):
                    if c >= 2:
                        pe.wait_ge(s["k_split"], p * NC + CHUNKED[1] + c - 1)
                    pe.matmul(ps[:, 4 + c % 2, 0:wd], w64[:, 2, :], ctxT[:, c0:c0 + wd], start=True, stop=True)\
                        .then_inc(s["k_proj"], 1)
                    t0, m = VG[c]
                    if c >= 2:
                        pe.wait_ge(s["v_copied"], p * NVG + CHUNKED[1] + c - 1)
                    if c == 0:
                        pe.wait_ge(s["o_done"], p * 2 + SUMS[1])
                    for u in range(m):
                        mm = pe.matmul(ps[:, 6 + c % 2, u * P:(u + 1) * P], ctxT[:, (t0 + u) * P:(t0 + u + 1) * P],
                                       w64[:, 3, :], start=True, stop=True)
                    mm.then_inc(s["v_proj"], 1)
                pe.wait_ge(s["q_split"], p * 4 + QSPLIT[1] + 4)
                pe.wait_ge(s["k_split"], p * NC + CHUNKED[1] + NC)
                pe.wait_ge(s["v_copied"], p * NVG + CHUNKED[1] + NVG)
                for e in range(2):
                    def scores(bank, r):
                        for h in range(2):
                            pe.matmul(ps[:, bank + h, :], kst[:, r, :], qp[:, e, 0, h, :], start=True, stop=False)
                            mm = pe.matmul(ps[:, bank + h, :], kst[:, r, :], qp[:, e, 1, h, :], start=False, stop=True)
                        return mm

                    def qk(t, r):
                        pe.wait_ge(s["staged"], t * 2 + 2)
                        pe.wait_ge(s["exp_done"], t - TILES[1] + UNITS[1] + 1)
                        scores(2 * r, r).then_inc(s["scores_ready"], 1)

                    def av(t, r, start, stop):
                        if start:
                            pe.wait_ge(s["acc_copied"], p * 2 + e + SUMS[1] + 2)
                        pe.wait_ge(s["exp_done"], t - TILES[1] + UNITS[1] + 1 + RING)
                        for h in range(2):
                            mm = pe.matmul(ps[64 * h:64 * h + 64, 6, :], vst[:, r, 0:HD64],
                                           probs[:, r, h * HT:(h + 1) * HT], start=start, stop=stop)
                        mm.then_inc(s["av_done"], 1)

                    with pe.If(mode1 >= 1):
                        maxima(1, p * 2 + e, 2, ST, lambda: scores(0, 0))
                    stream((p * 2 + e) * ST + TILES[1], qk, av)
                    pe.wait_ge(s["added"], (p * 2 + e) * ST + ST + RING)
                    if e == 1:
                        pe.wait_ge(s["o_done"], p * 2 + 1 + SUMS[1])
                    for h in range(2):
                        mm = pe.matmul(ps[64 * h:64 * h + 64, 7, :], ones[:, 0:HD64], t3[:, h, :], start=True, stop=True)
                    mm.then_inc(s["den_ready"], 1)
                pe.wait_ge(s["o_done"], p * 2 + 2 + SUMS[1])
                for h in range(2):
                    for e in range(2):
                        mm = pe.matmul(ps[:, h, :], w64[64 * h:64 * h + 64, 4 + e, :], t1[64 * h:64 * h + 64, e, :],
                                       start=(e == 0), stop=(e == 1))
                mm.then_inc(s["wo_ready"], 1)

            layernorm(3)
            pe.wait_ge(s["f8_ready"], 1)
            for h in range(2):
                mm = pe.matmul(ps[:, h, :], kernel8q[:, :], z8[:, h, :], start=True, stop=True)
            mm.then_inc(s["f8_done"], 1)

            layernorm(4)
            attention8(1, 2, 4)
            layernorm(5)
            layernorm(6)
            pe.wait_ge(s["z_ready"], 7)
            for t in range(NT):
                mm = pe.matmul(ps[:, 2, t * E16:t * E16 + E8], tok(z, t), wr2[:, :], start=True, stop=True)
            mm.then_inc(s["g_proj"], 1)
            pe.wait_ge(s["comb_ready"], 2)
            experts8(1)
            pe.wait_ge(s["hid_ready"], 2 + 2 * E8 * NF)
            for t in range(NT):
                mm = pe.matmul(ps[:, t // 4, (t % 4) * P:(t % 4 + 1) * P],
                               stat[:, 16 + t:17 + t].to_broadcast([P, P]), ident[:, :], start=True, stop=True)
            mm.then_inc(s["sum_ready"], 1)

            layernorm(7)
            pe.wait_ge(s["z_ready"], 8)
            for h in range(2):
                mm = pe.matmul(ps[:, h, :], wT[:, 1, :], z[:, h, :], start=True, stop=True)
            mm.then_inc(s["q3_proj"], 1)
            pe.wait_ge(s["q3_ready"], 1)
            pe.wait_ge(s["in_wk3"], 16)
            for h in range(2):
                mm = pe.matmul(ps[:, 2 + h, :], wk3[:, :], t1[:, h, :], start=True, stop=True)
            mm.then_inc(s["q3_proj"], 1)
            pe.wait_ge(s["q3_ready"], 2)
            for h in range(2):
                pe.matmul(ps[:, h, :], cov[:, :], z[:, h, :], start=True, stop=True)
            for h in range(2):
                mm = pe.matmul(ps[:, 4 + h, :], stat[:, 0:1].to_broadcast([P, P]), z[:, h, :], start=True, stop=True)
            mm.then_inc(s["q3_proj"], 1)
            pe.wait_ge(s["q3_next"], 1)
            pe.matmul(ps[:, 2, 0:1], mean_d[:, :], stat[:, 1:2], start=True, stop=True).then_inc(s["q3_score"], 1)
            for g, (t0, m) in enumerate(VG):
                if g >= 2:
                    pe.wait_ge(s["v3_copied"], g - 1)
                for u in range(m):
                    mm = pe.matmul(ps[:, 6 + g % 2, u * P:(u + 1) * P], ctxT[0:C, (t0 + u) * P:(t0 + u + 1) * P],
                                   wT[0:C, 3, :], start=True, stop=True)
                mm.then_inc(s["v_proj"], 1)
            pe.wait_ge(s["v3_copied"], NVG)
            pe.wait_ge(s["s3_ready"], 1)

            def scores3(bank, r):
                for h in range(2):
                    mm = pe.matmul(ps[:, bank + h, :], cst[:, r, :], z[:, h, :], start=True, stop=True)
                return mm

            def qk3(t, r):
                pe.wait_ge(s["staged"], t * 2 + 2)
                pe.wait_ge(s["exp_done"], t - TILES[3] + UNITS[3] + 1)
                scores3(2 * r, r).then_inc(s["scores_ready"], 1)

            def av3(t, r, start, stop):
                pe.wait_ge(s["exp_done"], t - TILES[3] + UNITS[3] + 1 + RING)
                for h in range(2):
                    mm = pe.matmul(ps[:, 6 + h, :], vst[:, r, :], probs[:, r, h * HT:(h + 1) * HT], start=start, stop=stop)
                mm.then_inc(s["av_done"], 1)

            pe.wait_ge(s["b3_sq"], 1)
            for h in range(2):
                mm = pe.matmul(ps[:, h, :], ones_b[:, :], t2b[:, h, :], start=True, stop=True)
            mm.then_inc(s["b3_sum"], 1)
            spread_bound(3)
            mode3 = mode_of(pe, 3)
            with pe.If(mode3 >= 1):
                maxima(3, 0, 2, ST, lambda: scores3(0, 0))
            stream(TILES[3], qk3, av3)
            pe.wait_ge(s["added"], (H + 1) * ST + RING)
            for h in range(2):
                mm = pe.matmul(ps[:, h, :], ones[:, :], t3[:, h, :], start=True, stop=True)
            mm.then_inc(s["den_ready"], 1)
            pe.wait_ge(s["o_done"], SUMS[3] + 1)
            for h in range(2):
                mm = pe.matmul(ps[:, 2 + h, :], wT[:, 2, :], t1[:, h, :], start=True, stop=True)
            mm.then_inc(s["wo_ready"], 1)

            layernorm(8)
            pe.wait_ge(s["z_ready"], 9)
            for t in range(NT):
                mm = pe.matmul(ps[:, 0, t * E16:(t + 1) * E16], tok(z, t), wT[:, 4, 0:E16], start=True, stop=True)
            mm.then_inc(s["g_proj"], 1)
            pe.wait_ge(s["in_shared"], 48)
            pe.wait_ge(s["comb_ready"], 3)

            def expert16(n, wts, u, start, stop, gated):
                if not start:
                    pe.wait_ge(s["hd_ready"], n)
                for m in range(3):
                    mm = pe.transpose(ps[:, 2, m * P:(m + 1) * P], wts[:, m, :], ident[:, :])
                mm.then_inc(s["wt_turned"], 1)
                pe.wait_ge(s["wt_copied"], n + 1)
                for m in range(2):
                    for h in range(2):
                        mm = pe.matmul(ps[:, 2 * m + h, :], turned[:, m, :], z[:, h, :], start=True, stop=True)
                    mm.then_inc(s["hg_ready"], 1)
                if gated:
                    pe.wait_ge(s["ccol_ready"], n + 2 * E8)
                    for t in range(NT):
                        mm = pe.matmul(ps[:, 6 + t // 4, (t % 4) * P:(t % 4 + 1) * P],
                                       ccol[:, u, t:t + 1].to_broadcast([P, P]), ident[:, :], start=True, stop=True)
                    mm.then_inc(s["cb_ready"], 1)
                pe.wait_ge(s["hd_ready"], n + 1)
                for h in range(2):
                    mm = pe.matmul(ps[:, 4 + h, :], turned[:, 2, :], t1[:, h, :], start=start, stop=stop)
                mm.then_inc(s["y_ready"], 1)

            expert16(0, shared, 0, True, False, False)
            with pe.Fori(0, E16 // 2 - 1) as i:
                for u in range(2):
                    pe.wait_ge(s[f"ex_w{u}"], i * 48 + 48)
                    expert16(i * 2 + u + 1, ex_w[u], u, False, False, True)
            for u in range(2):
                pe.wait_ge(s[f"ex_w{u}"], 48 * (E16 // 2))
                expert16(E16 - 2 + u + 1, ex_w[u], u, False, u == 1, True)

            pe.wait_ge(s["x_ready"], 9)
            for t in range(NT):
                mm = pe.transpose(ps[:, t // 4, (t % 4) * P:(t % 4 + 1) * P], tok(xT, t), ident[:, :])
            mm.then_inc(s["out_turned"], 1)

        @block.scalar
        def _(act):
            def load_table(k, func):
                act.activation(warm[:, k:k + 1], ones[:, 0:1], func)

            def layernorm(k):
                act.wait_ge(s["ln_var"], k + 1)
                act.activation(t2, ps[:, 2:4, :], ACT.Sqrt, bias=col(EPS)).then_inc(s["ln_std"], 1)

            def values8(n, layer):
                act.wait_ge(s["q_split"], QSPLIT[layer] + 1)
                act.activation(t2b, t1, ACT.Square, scale=SHRINK).then_inc(s["norm_sq"], 1)
                for g, (t0, m) in enumerate(VG):
                    wd = CHUNKS[g][1]
                    act.wait_ge(s["k_high"], NC * n + g + 1)
                    act.wait_ge(s["norm_mm"], n * (NC + 1) + max(1, g))
                    act.activation(t3b[:, g % 2, 0:wd], klo[:, g % 2, 0:wd], ACT.Square, scale=SHRINK)\
                        .then_inc(s["norm_sq"], 1)
                    act.wait_ge(s["v_proj"], CHUNKED[layer] + g + 1)
                    act.activation(vx[:, t0:t0 + m, :, 0:HD8],
                                   ps[:, 4 + g % 2, 0:m * P].rearrange("p (t h w) -> p t h w", t=m, h=H),
                                   ACT.Copy).then_inc(s["v_copied"], 1)

            def exps8(layer):
                mode = mode_of(act, layer)
                with act.If(mode >= 1):
                    exps8_loop(layer, f"shifted{layer}", 0)
                with act.Else():
                    exps8_loop(layer, "scores_ready", UNITS[layer])

            def exps8_loop(layer, ready, base):
                with act.Fori(0, 2 * NG * ST // RING) as i:
                    for r in range(RING):
                        act.wait_ge(s["av_done"], i * RING + r + TILES[layer] + 1)
                        for b in range(2):
                            buf = (2 * r + b) % RING
                            act.wait_ge(s[ready], i * (2 * RING) + 2 * r + b + base + 1)
                            act.activation(probs[:, r, b * T:(b + 1) * T].rearrange("p (h n) -> p h n", h=2),
                                           ps[:, 2 * buf:2 * buf + 2, :], ACT.Exp,
                                           scale=HD8 ** -0.5).then_inc(s["exp_done"], 1)

            def exps1(layer, mode, first, scale):
                with act.If(mode >= 1):
                    exps1_loop(layer, first, scale, f"shifted{layer}", 0)
                with act.Else():
                    exps1_loop(layer, first, scale, "scores_ready", UNITS[layer])

            def exps1_loop(layer, first, scale, ready, base):
                with act.Fori(0, ST // RING) as i:
                    for r in range(RING):
                        local = first + i * RING + r
                        act.wait_ge(s["av_done"], local + TILES[layer] + 1)
                        act.wait_ge(s["added"], local + ADDED[layer] + 1)
                        act.wait_ge(s[ready], local + base + 1)
                        act.activation(probs[:, r, 0:T].rearrange("p (h n) -> p h n", h=2), ps[:, 2 * r:2 * r + 2, :],
                                       ACT.Exp, scale=scale).then_inc(s["exp_done"], 1)

            def experts8(m):
                with act.Fori(0, E8 // 2) as i:
                    for u in range(2):
                        e = i * 2 + u
                        n = e + E8 * m
                        for f in range(NF):
                            if m == 0:
                                act.wait_ge(s["h_ready"], n * NF + f + 1)
                                if f == 0:
                                    act.wait_ge(s["eo_ready"], n + 2)
                                act.activation(hid[:, f, :, :], ps[:, 2 * (f % 2):2 * (f % 2) + 2, :], ACT.Gelu,
                                               bias=b1c[:, 0, bass.ds(e * NF + f, 1)]).then_inc(s["hid_ready"], 1)
                        for h in range(2):
                            act.wait_ge(s["cb_ready"], n * 2 + h + 1)
                            if h == 0:
                                act.wait_ge(s["eo_used"], n + 1)
                            act.activation(t3[:, h, :], ps[:, 6, :], ACT.Copy).then_inc(s["cb_copied"], 1)

            act.wait_ge(s["consts_set"], NCONST)
            for n, name in ((BQ0, "L0_xattn_bq"), (BO0, "L0_xattn_bo"), (BQ2, "L2_xattn_bq"), (BO2, "L2_xattn_bo"),
                            (BO1, "L1_xattn_bo"), (GAM, "L2_ffn_gamma"), (BET, "L2_ffn_beta")):
                act.dma_start(col(n), a[name].rearrange("(p o) -> p o", o=1)).then_inc(s["in_cols"], 16)
            for n, name in ((TEMP, "L0_ffn_temperature"), (SIN, "L1_ffn_input_scale"), (SK, "L1_ffn_kernel_scale")):
                act.dma_start(col(n), a[name].rearrange("(p o) -> p o", o=1).to_broadcast([P, 1])).then_inc(s["in_cols"], 16)
            act.dma_start(bias8[:, :], a["L1_ffn_bias"].rearrange("(p o) -> p o", o=1)).then_inc(s["in_cols"], 16)
            act.dma_start(kernel8[:, :], a["L1_ffn_kernel"]).then_inc(s["in_cols"], 16)
            act.dma_start(wr2[:, :], a["L2_ffn_Wr"]).then_inc(s["in_cols"], 16)
            act.dma_start(brow[:, :], a["L2_ffn_br"].rearrange("(o e) -> o e", o=1).to_broadcast([P, E8])).then_inc(s["in_cols"], 16)
            act.dma_start(ebrow[:, :], a["L3_ffn_expert_bias"].rearrange("(o e) -> o e", o=1).to_broadcast([P, E16]))\
                .then_inc(s["in_cols"], 16)
            for m, l in enumerate(("L0", "L2")):
                act.dma_start(b1c[:, m, :].rearrange("p (e f) -> p e f", f=NF),
                              a[l + "_ffn_b1"].rearrange("e (f p) -> p e f", p=P), allow_slow_non_contiguous=True).then_inc(s["in_cols"], 16)
                act.dma_start(b2c[:, m, :], a[l + "_ffn_b2"].rearrange("e d -> d e"), allow_slow_non_contiguous=True).then_inc(s["in_cols"], 16)

            for g in range(1, NVG, 2):
                t0, m = VG[g]
                act.wait_ge(s["ctx_turned"], g + 1)
                act.activation(ctxT[0:C, t0 * P:(t0 + m) * P], ps[0:C, 2 + g % 4, 0:m * P], ACT.Copy)\
                    .then_inc(s["ctx_odd"], 1)
            act.wait_ge(s["sim_sq"], 1)
            act.activation(stat[0:E8, 3:4], stat[0:E8, 2:3], ACT.Sqrt).then_inc(s["sim_root"], 1)

            layernorm(0)
            values8(0, 0)
            load_table(0, ACT.Exp)
            exps8(0)
            layernorm(1)
            act.wait_ge(s["g_proj"], 1)
            act.activation(route[:, 0, 0:NT], ps[:, 2, 0:NT * E16].rearrange("p (t e) -> p t e", t=NT)[:, :, E8],
                           ACT.Sqrt).then_inc(s["route_act"], 1)
            act.wait_ge(s["route_in"], 1)
            act.activation(route[:, 2, 0:NT * E8], route[:, 1, 0:NT * E8], ACT.Exp).then_inc(s["route_act"], 1)
            act.wait_ge(s["in_cols"], 16 * NCOLS)
            load_table(1, ACT.Gelu)
            experts8(0)

            layernorm(2)
            act.wait_ge(s["gram_ready"], 1)
            for e in range(2):
                rows = slice(HD64 * e, HD64 * (e + 1))
                act.activation(gram[rows, :, rows],
                               ps[rows, 6:8, :].rearrange("p a (m n) -> p (a m) n", n=P)[:, :, rows], ACT.Copy)\
                    .then_inc(s["gram_copied"], 1)
            for p in range(NP):
                act.wait_ge(s["b1_q"], p + 1)
                if p >= 2:
                    act.wait_ge(s["b1_r"], p - 1)
                act.activation((t2b, t3b)[p % 2], ps[:, 2 * (p % 2):2 * (p % 2) + 2, :], ACT.Copy)\
                    .then_inc(s["b1_copied"], 1)
            load_table(2, ACT.Exp)
            mode1 = mode_of(act, 1)
            with act.Fori(0, NP) as p:
                act.wait_ge(s["staged"], p * (4 * ST) + 2 * TILES[1])
                for c, (c0, wd) in enumerate(CHUNKS):
                    act.wait_ge(s["k_proj"], p * NC + CHUNKED[1] + c + 1)
                    for e in range(2):
                        act.activation(kb[64 * e:64 * e + 64, e, c0:c0 + wd], ps[64 * e:64 * e + 64, 4 + c % 2, 0:wd],
                                       ACT.Copy).then_inc(s["k1_high"], 1)
                    t0, m = VG[c]
                    act.wait_ge(s["v_proj"], p * NVG + CHUNKED[1] + c + 1)
                    act.activation(vp[:, t0 * P:(t0 + m) * P], ps[:, 6 + c % 2, 0:m * P], ACT.Copy)\
                        .then_inc(s["v_copied"], 1)
                for e in range(2):
                    exps1(1, mode1, (p * 2 + e) * ST, HD64 ** -0.5)
            layernorm(3)

            layernorm(4)
            values8(1, 2)
            load_table(3, ACT.Exp)
            exps8(2)
            layernorm(5)
            layernorm(6)
            act.wait_ge(s["route_in"], 2)
            act.activation(route[:, 2, 0:NT * E8], route[:, 1, 0:NT * E8], ACT.Exp).then_inc(s["route_act"], 1)
            experts8(1)

            layernorm(7)
            act.wait_ge(s["s3_ready"], 1)
            act.activation(stat[:, 11:12], stat[:, 10:11], ACT.Sqrt, bias=col(EPS)).then_inc(s["s3_root"], 1)
            for g, (t0, m) in enumerate(VG):
                act.wait_ge(s["v_proj"], (2 + NP) * NVG + g + 1)
                act.activation(vp[:, t0 * P:(t0 + m) * P], ps[:, 6 + g % 2, 0:m * P], ACT.Copy)\
                    .then_inc(s["v3_copied"], 1)
            act.wait_ge(s["s3_ready"], 2)
            load_table(4, ACT.Exp)
            mode3 = mode_of(act, 3)
            exps1(3, mode3, 0, stat[:, 12:13])
            layernorm(8)
            act.wait_ge(s["g_proj"], 3)
            act.activation(route[:, 1, :], ps[:, 0, 0:NT * E16], ACT.Sigmoid).then_inc(s["route_act"], 1)

            def gate(n):
                act.wait_ge(s["hg_ready"], n * 2 + 1)
                act.wait_ge(s["hd_ready"], n)
                act.activation(t2, ps[:, 0:2, :], ACT.Silu).then_inc(s["hg_act"], 1)

            gate(0)
            with act.Fori(1, E16 + 1) as n:
                gate(n)

        @block.gpsimd
        def _(pool):
            done = [0]

            def const(ins):
                done[0] += 1
                ins.then_inc(s["consts_set"], 1)
                pool.wait_ge(s["consts_set"], done[0])

            def diagonal(ap, pattern, base):
                const(pool.affine_select(out=ap, in_=ap, compare_op=ALU.not_equal, fill=1.0, base=base,
                                         pattern=pattern, channel_multiplier=1))

            const(pool.memset(cn[:, SF, :], 0.0))
            const(pool.memset(ident[:, :], 0.0))
            const(pool.memset(dsel[:, :], 0.0))
            const(pool.memset(before[:, :, :], 1.0))
            diagonal(ident[:, :], [[-1, P]], 0)
            diagonal(dsel[:, :].rearrange("p (j w) -> p j w", j=G), [[-32, G], [0, 32]], -HD8)
            const(pool.affine_select(out=before[:, :, :], in_=before[:, :, :], compare_op=ALU.is_gt, fill=0.0, base=0,
                                     pattern=[[1, E16], [-1, E16]], channel_multiplier=0))
            const(pool.memset(ones[:, :], 1.0))
            const(pool.memset(mean_d[:, :], 1.0 / D))
            const(pool.memset(mean_s[:, :], 1.0 / S))
            const(pool.memset(w8[:, :, :, :], 0.0))
            const(pool.memset(w64[:, :, :], 0.0))
            const(pool.memset(wk3[:, :], 0.0))
            const(pool.memset(stat[:, :], 0.0))
            const(pool.memset(cov[:, :], 0.0))
            const(pool.memset(cols[:, EPS:EPS + 1], LN_EPS))
            const(pool.memset(ctxT[C:P, :], 0.0))
            const(pool.memset(vst[:, :, :], 0.0))
            const(pool.memset(qz[:, :].bitcast(F32), 0.0))
            const(pool.memset(ctxT[C:C + 1, 0:S], 1.0))
            const(pool.memset(ones_b[:, :], 1.0))
            const(pool.memset(peak[:, :], 0.0))
            const(pool.memset(bnd[:, :], 0.0))
            const(pool.memset(heads[:, :], 0.0))
            in_head = heads[:, 0:H]
            const(pool.affine_select(out=in_head, in_=in_head, compare_op=ALU.is_gt, fill=1.0, base=0,
                                     pattern=[[HD8, H]], channel_multiplier=-1))
            const(pool.affine_select(out=in_head, in_=in_head, compare_op=ALU.is_gt, fill=0.0, base=HD8,
                                     pattern=[[HD8, H]], channel_multiplier=-1))
            assert done[0] == NCONST
            credits = [("exp_done", RING), ("av_done", RING), ("added", RING), ("acc_copied", 2), ("hid_ready", 2),
                       ("eo_ready", 2), ("x_added", 1), ("cb_copied", 1), ("eo_used", 1), ("moe_acc", 1),
                       ("den_ready", 1), ("klo_out0", 1), ("klo_out1", 1), ("y_ready", 1)]
            credits += [(f"{n}{l}", 1) for n in ("max_scores", "max_read", "shift_sub") for l in range(4)]
            for k, (name, count) in enumerate(credits):
                pool.memset(given[:, k:k + 1], 0.0).then_inc(s[name], count)

            pool.wait_ge(s["in_ctx0"], 16)
            pool.wait_ge(s["in_ctx1"], 16)
            pool.tensor_tensor(cn_sq, cn, cn, ALU.mult).then_inc(s["ctx_sq"], 1)

            def stage_maxima(layer, count, first, out, tile, loads):
                with pool.Fori(0, ST) as t:
                    loads()
                    pool.wait_ge(s["av_done"], first + RING)
                    pool.tensor_copy(out, tile(t)).then_inc(s[f"max_staged{layer}"], 1)
                    pool.wait_ge(s[f"max_scores{layer}"], count * ST + t + 2)

            def stage8(n, layer):
                if n:
                    pool.wait_ge(s["z_ready"], 5)
                    pool.memset(vst[:, :, :], 0.0).then_inc(s["pool_step"], 1)
                    pool.memset(qz[:, :].bitcast(F32), 0.0).then_inc(s["q_zeroed"], 1)
                    pool.wait_ge(s["pool_step"], 1)
                pool.wait_ge(s["v_proj"], CHUNKED[layer] + 1)
                pool.memset(vx[:, 0:SF, :, HD8:HD8 + 1], 1.0).then_inc(s["v_ones"], 1)
                pool.memset(vx[:, SF, :, HD8:HD8 + 1], 0.0).then_inc(s["v_ones"], 1)
                pool.wait_ge(s["v_ones"], 3 * n + 2)
                pool.memset(vx[0:TAIL, SF, :, HD8:HD8 + 1], 1.0).then_inc(s["v_ones"], 1)
                pool.wait_ge(s["v_ones"], 3 * n + 3)
                mode = mode_of(pool, layer)
                with pool.Fori(0, NG // 2) as gi:
                    for par in range(2):
                        g = gi * 2 + par

                        def loads():
                            pool.wait_ge(s["v_copied"], CHUNKED[layer] + NVG)
                            pool.wait_ge(s[f"k_in{par}"], gi * (16 * 2 * G) + 16 * 2 * G * (NG // 2 * n + 1))

                        for half in range(2):
                            with pool.If(mode >= 1):
                                stage_maxima(layer, g * 2 + half, (g * 2 + half) * ST + TILES[layer], kst[:, 0, :],
                                             lambda t: kb[:, par, bass.ds(t * P, P)], loads)
                            with pool.Fori(0, ST // RING) as i:
                                loads()
                                for r in range(RING):
                                    t = i * RING + r
                                    pool.wait_ge(s["av_done"], (g * 2 + half) * ST + t + TILES[layer] + 1)
                                    pool.tensor_copy(kst[:, r, :], kb[:, par, bass.ds(t * P, P)]).then_inc(s["staged"], 1)
                                    pool.tensor_copy(
                                        vst[:, r, :].rearrange("p (j w) -> p j w", j=G)[:, :, 0:HD8 + 1],
                                        vbuf[:, bass.ds(t * (H * (HD8 + 1)) + g * (G * (HD8 + 1)), G * (HD8 + 1))]
                                        .rearrange("p (j w) -> p j w", j=G)).then_inc(s["staged"], 1)

            def weights8(m):
                pool.wait_ge(s["comb_ready"], m + 1)
                with pool.Fori(0, E8 // 2) as i:
                    for u in range(2):
                        n = i * 2 + u + E8 * m
                        pool.wait_ge(s["eo_ready"], n + 1)
                        pool.tensor_copy(ccol[:, u, :],
                                         route[:, 7, 0:NT * E8].rearrange("p (t e) -> p e t", t=NT)[:, bass.ds(i * 2 + u, 1), :]
                                         .rearrange("p o t -> p (o t)")).then_inc(s["ccol_ready"], 1)

            stage8(0, 0)
            weights8(0)
            mode1 = mode_of(pool, 1)
            with pool.Fori(0, NP) as p:
                def loads1():
                    pool.wait_ge(s["klo_out0"], p * 128 + 129)
                    pool.wait_ge(s["klo_out1"], p * 96 + 97)
                    pool.wait_ge(s["k1_high"], p * (2 * NC) + 2 * NC)
                    pool.wait_ge(s["v_copied"], p * NVG + CHUNKED[1] + NVG)

                for e in range(2):
                    with pool.If(mode1 >= 1):
                        stage_maxima(1, p * 2 + e, (p * 2 + e) * ST + TILES[1], kst[:, 0, :],
                                     lambda t: kb[:, e, bass.ds(t * P, P)], loads1)
                    with pool.Fori(0, ST // RING) as i:
                        loads1()
                        for r in range(RING):
                            t = i * RING + r
                            pool.wait_ge(s["av_done"], (p * 2 + e) * ST + t + TILES[1] + 1)
                            pool.tensor_copy(kst[:, r, :], kb[:, e, bass.ds(t * P, P)]).then_inc(s["staged"], 1)
                            pool.tensor_copy(vst[:, r, 0:HD64], vp[:, bass.ds(t * P + e * HD64, HD64)]).then_inc(s["staged"], 1)
            stage8(1, 2)
            weights8(1)
            mode3 = mode_of(pool, 3)
            with pool.If(mode3 >= 1):
                stage_maxima(3, 0, TILES[3], cst[:, 0, :], lambda t: ctxT[:, bass.ds(t * P, P)], lambda: None)
            pool.wait_ge(s["v3_copied"], NVG)
            with pool.Fori(0, ST // RING) as i:
                for r in range(RING):
                    t = i * RING + r
                    pool.wait_ge(s["av_done"], t + TILES[3] + 1)
                    pool.tensor_copy(cst[:, r, :], ctxT[:, bass.ds(t * P, P)]).then_inc(s["staged"], 1)
                    pool.tensor_copy(vst[:, r, :], vp[:, bass.ds(t * P, P)]).then_inc(s["staged"], 1)
            pool.wait_ge(s["comb_ready"], 3)
            with pool.Fori(0, E16 // 2) as i:
                for u in range(2):
                    n = i * 2 + u + 1
                    pool.wait_ge(s["y_ready"], i * 2 + u + 1)
                    pool.tensor_copy(ccol[:, u, :],
                                     route[:, 7, :].rearrange("p (t e) -> p e t", t=NT)[:, bass.ds(i * 2 + u, 1), :]
                                     .rearrange("p o t -> p (o t)")).then_inc(s["ccol_ready"], 1)

        @block.vector
        def _(dve):
            steps = [0]

            def then(ins):
                steps[0] += 1
                ins.then_inc(s["dve_step"], 1)
                dve.wait_ge(s["dve_step"], steps[0])

            def layernorm(k):
                src = z if k == 6 else xT[:, :, :]
                dve.wait_ge(s["ln_mean"], k + 1)
                then(dve.tensor_tensor(t1, src, ps[:, 0:2, :], ALU.subtract))
                dve.tensor_tensor(t2, t1, t1, ALU.mult).then_inc(s["ln_sq"], 1)
                dve.wait_ge(s["ln_std"], k + 1)
                then(dve.reciprocal(t2, t2))
                if k == 6:
                    then(dve.tensor_tensor(z, t1, t2, ALU.mult))
                    dve.wait_ge(s["in_cols"], 16 * NCOLS)
                    dve.tensor_scalar(z, z, col(GAM), col(BET), ALU.mult, ALU.add).then_inc(s["z_ready"], 1)
                else:
                    dve.tensor_tensor(z, t1, t2, ALU.mult).then_inc(s["z_ready"], 1)

            def best(sc, E, K):
                shape = [P, NT, E, E]
                cmp = flat[:, 0:NT * E * E].rearrange("p (t e f) -> p t e f", t=NT, e=E)
                eq = flat[:, 2048:2048 + NT * E * E].rearrange("p (t e f) -> p t e f", t=NT, e=E)
                other = sc.unsqueeze(2).to_broadcast(shape)
                own = sc.unsqueeze(3).to_broadcast(shape)
                earlier = before[:, 0:E, 0:E].unsqueeze(1).to_broadcast(shape)
                dve.tensor_tensor(cmp, other, own, ALU.is_gt)
                then(dve.tensor_tensor(eq, other, own, ALU.is_equal))
                then(dve.tensor_tensor(eq, eq, earlier, ALU.mult))
                then(dve.tensor_tensor(cmp, cmp, eq, ALU.add))
                rank = route[:, 3, 0:NT * E].rearrange("p (t e) -> p t e", t=NT)
                then(dve.reduce_sum(rank, cmp, AX.X))
                sel = route[:, 4, 0:NT * E].rearrange("p (t e) -> p t e", t=NT)
                then(dve.tensor_scalar(sel, rank, K - 0.5, None, ALU.is_lt))
                return sel

            def r8(n):
                return route[:, n, 0:NT * E8].rearrange("p (t e) -> p t e", t=NT)

            def r16(n):
                return route[:, n, :].rearrange("p (t e) -> p t e", t=NT)

            def per_token(n, e):
                return route[:, 5, n * NT:(n + 1) * NT].unsqueeze(2).to_broadcast([P, NT, e])

            def tokens(n):
                return route[:, 5, n * NT:(n + 1) * NT]

            def set_mode(layer, most):
                dve.wait_ge(s["bound_out"], layer + 1)
                low, odd = stat[:, 20:21], stat[:, 21:22]
                then(dve.reduce_max(stat[:, 22:23], ps[:, 2, 0:P], AX.X))
                then(dve.tensor_scalar(low, stat[:, 22:23], most, -1.0, ALU.is_lt, ALU.mult))
                then(dve.tensor_scalar(odd, ps[:, 2, P:P + 1], 0.0, -2.0, ALU.is_equal, ALU.mult))
                then(dve.tensor_scalar(odd, odd, 2.0, None, ALU.add))
                then(dve.scalar_tensor_tensor(out=low, in0=low, scalar=1.0, in1=odd, op0=ALU.add, op1=ALU.max))
                dve.tensor_copy(cols[:, MODE + layer:MODE + layer + 1].bitcast(I32), low).then_inc(s["mode_set"], 1)

            def maxima(layer, count, banks, units, most):
                known, read = s[f"max_known{layer}"], s[f"max_read{layer}"]
                into, scores = top[:, 0:banks, :], ps[:, 0:banks, :]
                dve.wait_ge(s[f"shift_sub{layer}"], count * units + 1)
                dve.wait_ge(s[f"max_scores{layer}"], count * ST + 2)
                dve.tensor_copy(into, scores).then_inc(read, 1)
                with dve.Fori(0, ST - 2) as t:
                    dve.wait_ge(s[f"max_scores{layer}"], count * ST + t + 3)
                    dve.wait_ge(read, count * ST + t + 2)
                    dve.tensor_tensor(into, into, scores, ALU.max).then_inc(read, 1)
                dve.wait_ge(s[f"max_scores{layer}"], count * ST + ST + 1)
                dve.wait_ge(read, count * ST + ST)
                dve.tensor_tensor(into[0:TAIL], into[0:TAIL], scores[0:TAIL], ALU.max).then_inc(read, 1)
                dve.wait_ge(s[f"max_spread{layer}"], count * 2 + 1)
                dve.reduce_max(topcol[:, 0:4 * banks], scores.rearrange("p b (m n) -> p (b m) n", n=P), AX.X).then_inc(known, 1)
                dve.wait_ge(s[f"max_spread{layer}"], count * 2 + 2)
                dve.tensor_scalar(into, scores, most, None, ALU.min).then_inc(known, 1)

            def shift(layer, count, unit, scores, largest, least, mode):
                sub = s[f"shift_sub{layer}"]

                def subtract():
                    dve.wait_ge(s[f"max_known{layer}"], count * 2 + 2)
                    dve.wait_ge(s["scores_ready"], unit + UNITS[layer] + 1)
                    dve.scalar_tensor_tensor(out=scores, in0=scores, scalar=least, in1=largest, op0=ALU.max,
                                             op1=ALU.subtract).then_inc(sub, 1)

                if layer == 0:
                    with dve.If(mode == 2):
                        dve.wait_ge(s["scores_ready"], unit + UNITS[layer] + 1)
                        dve.memset(scores, 0.0).then_inc(sub, 1)
                    with dve.Else():
                        subtract()
                else:
                    subtract()
                dve.wait_ge(sub, unit + 2)
                dve.tensor_scalar(scores, scores, 0.0, None, ALU.min).then_inc(s[f"shifted{layer}"], 1)

            dve.wait_ge(s["x_turned"], 1)
            dve.tensor_copy(xT[:, :, :], ps[:, 0:2, :]).then_inc(s["x_ready"], 1)
            dve.wait_ge(s["in_nat"], 16 * 6)
            then(dve.tensor_tensor(route[0:E8, 0, :], wn[0:E8, 5, :], wn[0:E8, 5, :], ALU.mult))
            dve.wait_ge(s["consts_set"], NCONST)
            dve.reduce_sum(stat[0:E8, 2:3], route[0:E8, 0, :], AX.X).then_inc(s["sim_sq"], 1)
            for g in range(0, NVG, 2):
                t0, m = VG[g]
                dve.wait_ge(s["ctx_turned"], g + 1)
                dve.tensor_copy(ctxT[0:C, t0 * P:(t0 + m) * P], ps[0:C, 2 + g % 4, 0:m * P]).then_inc(s["ctx_even"], 1)
            dve.wait_ge(s["sim_root"], 1)
            then(dve.tensor_scalar(stat[0:E8, 3:4], stat[0:E8, 3:4], TINY, None, ALU.max))
            then(dve.reciprocal(stat[0:E8, 3:4], stat[0:E8, 3:4]))
            dve.tensor_scalar(wn[0:E8, 5, :], wn[0:E8, 5, :], stat[0:E8, 3:4], None, ALU.mult).then_inc(s["sim_ready"], 1)
            dve.reduce_sum(csum[:, :], cn.rearrange("p t c -> p c t"), AX.X).then_inc(s["csum_ready"], 1)
            dve.wait_ge(s["w_turned"], 1)
            dve.tensor_copy(wT[:, 0:3, :], ps[:, 6, 0:3 * P].rearrange("p (m n) -> p m n", m=3))
            dve.tensor_copy(wT[0:C, 3, :], ps[0:C, 6, 3 * P:4 * P])
            dve.wait_ge(s["gate_turned"], 1)
            dve.tensor_copy(wT[:, 4, 0:E16], ps[:, 7, 0:E16])
            dve.tensor_copy(wT[:, 5, 0:E8], ps[:, 7, E16:E16 + E8]).then_inc(s["w_copied"], 1)
            dve.wait_ge(s["ctx_sq"], 1)
            then(dve.reduce_sum(cn_len, cn_sq, AX.X))
            dve.reduce_max(cpeak[:, 0:1], cn_len, AX.X).then_inc(s["cpeak_in"], 1)
            dve.wait_ge(s["cpeak_out"], 1)
            dve.reduce_max(cpeak[:, 1:2], ps[:, 0, 2 * P:3 * P], AX.X)
            dve.wait_ge(s["cmean_ready"], 1)
            dve.tensor_copy(stat[0:C, 0:1], ps[0:C, 0, P:P + 1])
            dve.tensor_tensor(cn[:, 0:SF, :], cn[:, 0:SF, :], ps[:, 0, 0:C].unsqueeze(1).to_broadcast([P, SF, C]), ALU.subtract)
            dve.tensor_tensor(cn[0:TAIL, SF, :], cn[0:TAIL, SF, :], ps[0:TAIL, 0, 0:C], ALU.subtract).then_inc(s["ccent_ready"], 1)
            dve.wait_ge(s["cov_ready"], 1)
            dve.tensor_scalar(cov[0:C, 0:C], ps[0:C, 1, 0:C], 1.0 / S, None, ALU.mult).then_inc(s["cov_copied"], 1)

            def attention8(n, layer, bq, bo):
                dve.wait_ge(s["q_proj"], QPROJ[layer] + 1)
                dve.wait_ge(s["in_cols"], 16 * NCOLS)
                then(dve.tensor_scalar(t1, ps[:, 0:2, :], col(bq), None, ALU.add))
                high = qs[:, 0, :].rearrange("p (h n) -> p h n", h=2)
                low = qs[:, 1, :].rearrange("p (h n) -> p h n", h=2)
                dve.tensor_copy(high.bitcast(F32R), t1).then_inc(s["q_split"], 1)
                dve.wait_ge(s["q_split"], QSPLIT[layer] + 1)
                dve.tensor_tensor(low.bitcast(F32R), t1, high, ALU.subtract).then_inc(s["q_split"], 1)
                base = n * (NC + 1)

                def norms(c):
                    dve.wait_ge(s["norm_mm"], base + c + 2)
                    dve.reduce_max(peak[0:32, c:c + 1], ps[0:32, 2 + c % 2, 0:CHUNKS[c][1]], AX.X).then_inc(s["norm_max"], 1)

                dve.wait_ge(s["norm_mm"], base + 1)
                dve.reduce_max(peak[0:32, NC:NC + 1], ps[0:32, 0:2, :], AX.XY)
                dve.reduce_sum(peak[0:32, NC + 1:NC + 2], ps[0:32, 0:2, :], AX.XY).then_inc(s["norm_max"], 1)
                for c, (c0, wd) in enumerate(CHUNKS):
                    r = c % 2
                    dve.wait_ge(s["k_proj"], CHUNKED[layer] + c + 1)
                    if stores[n][c]:
                        dve.wait_ge(s[f"k_scr{r}"], 16 * stores[n][c])
                    if c >= 2:
                        dve.wait_ge(s["norm_sq"], base + c)
                    high, low = klo[:, r, 0:wd], klo[:, r, HT:HT + wd]
                    dve.tensor_copy(high.bitcast(F32R), ps[:, 6 + r, 0:wd]).then_inc(s["k_high"], 1)
                    dve.wait_ge(s["k_high"], NC * n + c + 1)
                    dve.tensor_tensor(low.bitcast(F32R), ps[:, 6 + r, 0:wd], high, ALU.subtract).then_inc(s["k_split"], 1)
                    if c >= 1:
                        norms(c - 1)
                norms(NC - 1)
                then(dve.reduce_sum(peak[0:32, NC + 2:NC + 3], ps[0:32, 1, :], AX.X))
                then(dve.reduce_sum(peak[0:32, NC + 3:NC + 4], ps[0:32, 2 + (NC - 1) % 2, 0:CHUNKS[-1][1]], AX.X))
                then(dve.reduce_max(peak[0:32, NC + 4:NC + 5], peak[0:32, 0:NC], AX.X))
                then(dve.tensor_tensor(bnd[0:32, 2 * layer:2 * layer + 1], peak[0:32, NC + 4:NC + 5], peak[0:32, NC:NC + 1], ALU.mult))
                then(dve.tensor_scalar(peak[0:32, NC + 1:NC + 4], peak[0:32, NC + 1:NC + 4], 0.0, None, ALU.mult))
                dve.reduce_sum(bnd[0:32, 2 * layer + 1:2 * layer + 2], peak[0:32, NC + 1:NC + 4], AX.X).then_inc(s["bound_in"], 1)
                set_mode(layer, LIMIT ** 2 * HD8 * SHRINK ** 4)
                mode = mode_of(dve, layer)
                with dve.Fori(0, NG) as g:
                    for half in range(2):
                        with dve.If(mode >= 1):
                            maxima(layer, g * 2 + half, G, 2 * ST, CLIP if layer == 0 else HUGE)
                            with dve.Fori(0, 2 * ST // (2 * RING)) as i:
                                for k in range(2 * RING):
                                    buf = k % RING
                                    shift(layer, g * 2 + half, (g * 2 + half) * (2 * ST) + i * (2 * RING) + k,
                                          ps[:, 2 * buf:2 * buf + 2, :], top[:, 2 * (k % 2):2 * (k % 2) + 2, :],
                                          -CLIP if layer == 0 else -HUGE, mode)
                        dve.wait_ge(s["av_done"], (g * 2 + half) * ST + TILES[layer] + RING + ST)
                        dve.tensor_copy(sums[:, bass.ds(g * 2 + half, 1), :], ps[:, 6 + half:7 + half, :])\
                            .then_inc(s["acc_copied"], 1)
                for gh in range(2 * NG):
                    dve.wait_ge(s["den8"], 2 * NG * n + gh + 1)
                    rec = flat[:, gh * HT:(gh + 1) * HT]
                    then(dve.reciprocal(rec, ps[:, gh % 4, :]))
                    dve.tensor_tensor(sums[:, gh, :], sums[:, gh, :], rec, ALU.mult).then_inc(s["o_done"], 1)
                dve.wait_ge(s["wo_ready"], WOUT[layer] + 1)
                dve.scalar_tensor_tensor(out=xT[:, :, :], in0=ps[:, 4:6, :], scalar=col(bo), in1=xT[:, :, :],
                                         op0=ALU.add, op1=ALU.add).then_inc(s["x_ready"], 1)

            def experts8(m):
                then(dve.memset(t2, 0.0))
                with dve.Fori(0, E8 // 2) as i:
                    for u in range(2):
                        e = i * 2 + u
                        n = e + E8 * m
                        if m == 1:
                            for f in range(NF):
                                dve.wait_ge(s["h_ready"], n * NF + f + 1)
                                if f == 0:
                                    dve.wait_ge(s["eo_ready"], n + 2)
                                dve.tensor_scalar(hid[:, f, :, :], ps[:, 2 * (f % 2):2 * (f % 2) + 2, :],
                                                  rb1[:, 1, bass.ds(e * NF + f, 1)], rb1[:, 2, bass.ds(e * NF + f, 1)],
                                                  ALU.add, ALU.max).then_inc(s["hid_ready"], 1)
                        dve.wait_ge(s["moe_acc"], n + 1)
                        dve.wait_ge(s["eo_ready"], n + 3)
                        dve.wait_ge(s["cb_copied"], n * 2 + 3)
                        if m == 0:
                            dve.scalar_tensor_tensor(out=t1, in0=ps[:, 4:6, :], scalar=b2c[:, 0, bass.ds(e, 1)], in1=t3,
                                                     op0=ALU.add, op1=ALU.mult).then_inc(s["eo_used"], 1)
                        else:
                            dve.tensor_tensor(t1, ps[:, 4:6, :], t3, ALU.mult).then_inc(s["eo_used"], 1)
                        dve.wait_ge(s["eo_used"], n + 2)
                        dve.tensor_tensor(t2, t2, t1, ALU.add).then_inc(s["moe_acc"], 1)
                dve.wait_ge(s["moe_acc"], E8 * (m + 1) + 1)

            def sums_of(layer, first, count, mode):
                with dve.If(mode >= 1):
                    maxima(layer, count, 2, ST, HUGE)
                    sums_loop(layer, first, count, mode, True)
                with dve.Else():
                    sums_loop(layer, first, count, mode, False)

            def sums_loop(layer, first, count, mode, general):
                def add(local, r, t):
                    if general:
                        shift(layer, count, local, ps[:, 2 * r:2 * r + 2, :], top[:, 0:2, :], -HUGE, mode)
                    dve.wait_ge(s["exp_done"], local + UNITS[layer] + RING + 1)
                    k = TAIL if t == ST - 1 else P
                    e = probs[0:k, r, 0:T].rearrange("p (h n) -> p h n", h=2)
                    if t == 0:
                        dve.wait_ge(s["den_ready"], count + 1)
                        dve.tensor_copy(t3, e).then_inc(s["added"], 1)
                    else:
                        dve.wait_ge(s["added"], local + ADDED[layer] + RING)
                        dve.tensor_tensor(t3[0:k], t3[0:k], e, ALU.add).then_inc(s["added"], 1)

                for t in range(RING):
                    add(first + t, t, t)
                with dve.Fori(0, ST // RING - 2) as i:
                    for r in range(RING):
                        add(first + i * RING + RING + r, r, RING)
                for t in range(ST - RING, ST):
                    add(first + t, t % RING, t)

            layernorm(0)
            attention8(0, 0, BQ0, BO0)
            layernorm(1)
            dve.wait_ge(s["p_proj"], 1)
            then(dve.tensor_copy(t1, ps[:, 0:2, :]))
            dve.tensor_tensor(t2, t1, t1, ALU.mult).then_inc(s["p_ready"], 1)
            then(dve.reciprocal(stat[:, 4:5], col(TEMP)))
            dve.wait_ge(s["route_act"], 1)
            then(dve.tensor_scalar(tokens(0), route[:, 0, 0:NT], TINY, None, ALU.max))
            then(dve.reciprocal(tokens(0), tokens(0)))
            dots = ps[:, 2, 0:NT * E16].rearrange("p (t e) -> p t e", t=NT)[:, :, 0:E8]
            then(dve.tensor_tensor(r8(0), dots, per_token(0, E8), ALU.mult))
            then(dve.tensor_scalar(r8(0), r8(0), stat[:, 4:5], None, ALU.mult))
            then(dve.reduce_max(tokens(1), r8(0), AX.X))
            dve.tensor_tensor(r8(1), r8(0), per_token(1, E8), ALU.subtract).then_inc(s["route_in"], 1)
            sel = best(r8(0), E8, 2)
            dve.wait_ge(s["route_act"], 2)
            then(dve.tensor_tensor(r8(2), r8(2), sel, ALU.mult))
            then(dve.reduce_sum(tokens(2), r8(2), AX.X))
            then(dve.reciprocal(tokens(2), tokens(2)))
            dve.tensor_tensor(r8(7), r8(2), per_token(2, E8), ALU.mult).then_inc(s["comb_ready"], 1)
            experts8(0)
            dve.tensor_tensor(xT[:, :, :], xT[:, :, :], t2, ALU.add).then_inc(s["x_ready"], 1)

            layernorm(2)
            dve.wait_ge(s["in_qk1"], 32)
            dve.memset(gram[0:HD64, :, HD64:P], 0.0)
            dve.memset(gram[HD64:P, :, 0:HD64], 0.0).then_inc(s["b1_prod"], 1)
            for p in range(NP):
                dve.wait_ge(s["b1_r"], p + 1)
                if p:
                    dve.wait_ge(s["b1_sum"], p)
                dve.tensor_tensor(t1b, ps[:, 4:6, :], (t2b, t3b)[p % 2], ALU.mult).then_inc(s["b1_prod"], 1)
                dve.wait_ge(s["b1_sum"], p + 1)
                dve.reduce_max(peak[:, p:p + 1], ps[:, 6:8, :], AX.XY).then_inc(s["b1_max"], 1)
            dve.wait_ge(s["b1_max"], NP)
            then(dve.reduce_max(stat[:, 19:20], peak[:, 0:NP], AX.X))
            dve.tensor_tensor(bnd[:, 2:3], stat[:, 19:20], cpeak[:, 1:2], ALU.mult).then_inc(s["bound_in"], 1)
            set_mode(1, LIMIT ** 2 * HD64)
            mode1 = mode_of(dve, 1)
            with dve.Fori(0, NP) as p:
                for e in range(2):
                    dve.wait_ge(s["q_proj"], p * 2 + QPROJ[1] + e + 1)
                    dve.tensor_copy(qp[:, e, 0], ps[:, 2 * e:2 * e + 2, :]).then_inc(s["q_split"], 1)
                    dve.wait_ge(s["q_split"], p * 4 + QSPLIT[1] + 2 * e + 1)
                    dve.tensor_tensor(qp[:, e, 1], ps[:, 2 * e:2 * e + 2, :], qp[:, e, 0].bitcast(F32), ALU.subtract)\
                        .then_inc(s["q_split"], 1)
                for n, (first, m) in enumerate(KP_PIECES):
                    dve.wait_ge(s[f"klo_out{n % 2}"], p * (32 * (4 - n % 2)) + 32 * (n // 2) + 1)
                    for c in range(first, first + m):
                        c0, wd = CHUNKS[c]
                        at = (c - first) * HT
                        dve.wait_ge(s["k1_high"], p * (2 * NC) + 2 * (c + 1))
                        for e in range(2):
                            rows = slice(64 * e, 64 * e + 64)
                            ins = dve.tensor_tensor(klo[rows, n % 2, at:at + wd].bitcast(F32R), ps[rows, 4 + c % 2, 0:wd],
                                                    kb[rows, e, c0:c0 + wd].bitcast(F32), ALU.subtract)
                        ins.then_inc(s["k_split"], 1)
                for e in range(2):
                    sums_of(1, (p * 2 + e) * ST, p * 2 + e, mode1)
                    dve.wait_ge(s["av_done"], (p * 2 + e) * ST + TILES[1] + RING + ST)
                    dve.tensor_copy(t1[:, e, :], ps[:, 6, :]).then_inc(s["acc_copied"], 1)
                    dve.wait_ge(s["den_ready"], p * 2 + e + 2)
                    dve.reciprocal(t2[:, e, :], ps[:, 7, :]).then_inc(s["rec_ready"], 1)
                    dve.wait_ge(s["rec_ready"], p * 2 + e + 1)
                    dve.tensor_tensor(t1[:, e, :], t1[:, e, :], t2[:, e, :], ALU.mult).then_inc(s["o_done"], 1)
                dve.wait_ge(s["wo_ready"], p + WOUT[1] + 1)
                dve.wait_ge(s["x_added"], p + 1)
                dve.tensor_tensor(xT[:, :, :], xT[:, :, :], ps[:, 0:2, :], ALU.add).then_inc(s["x_added"], 1)
            dve.wait_ge(s["x_added"], NP + 1)
            dve.tensor_scalar(xT[:, :, :], xT[:, :, :], col(BO1), None, ALU.add).then_inc(s["x_ready"], 1)

            def to_float8(out, v, scale, a, b):
                then(dve.tensor_scalar(a, v, scale, None, ALU.mult))
                then(dve.tensor_scalar(b.bitcast(I32), a.bitcast(I32), 0x7F800000, None, ALU.bitwise_and))
                then(dve.tensor_scalar(b, b, 2.0 ** -6, 1.5 * 2.0 ** 20, ALU.max, ALU.mult))
                then(dve.tensor_tensor(a, a, b, ALU.add))
                then(dve.tensor_tensor(a, a, b, ALU.subtract))
                then(dve.tensor_tensor(b, a, a, ALU.mult))
                then(dve.tensor_scalar(b, b, FP8_MAX ** 2, 3e38, ALU.is_gt, ALU.mult))
                then(dve.tensor_scalar(b, b, 3e38, None, ALU.mult))
                then(dve.tensor_tensor(b, b, b, ALU.subtract))
                return dve.tensor_tensor(out, a, b, ALU.add)

            layernorm(3)
            then(dve.reciprocal(stat[:, 5:6], col(SIN)))
            then(dve.reciprocal(stat[:, 6:7], col(SK)))
            then(dve.tensor_tensor(stat[:, 7:8], col(SIN), col(SK), ALU.mult))
            dve.wait_ge(s["z_ready"], 4)
            then(dve.tensor_copy(z8[:, :, :], z))
            then(to_float8(kernel8q[:, :], kernel8[:, :], stat[:, 6:7], t1[:, 0, 0:P], t2[:, 0, 0:P]))
            to_float8(z8[:, :, :], z8[:, :, :], stat[:, 5:6], t1, t2).then_inc(s["f8_ready"], 1)
            dve.wait_ge(s["f8_done"], 1)
            then(dve.tensor_scalar(z8[:, :, :], ps[:, 0:2, :], stat[:, 7:8], None, ALU.mult))
            then(dve.tensor_scalar(z8[:, :, :], z8[:, :, :], bias8[:, 0:1], None, ALU.add))
            dve.tensor_tensor(xT[:, :, :], xT[:, :, :], z8[:, :, :], ALU.add).then_inc(s["x_ready"], 1)

            layernorm(4)
            attention8(1, 2, BQ2, BO2)
            layernorm(5)
            dve.wait_ge(s["z_ready"], 6)
            then(dve.tensor_tensor(xT[:, :, :], xT[:, :, :], z, ALU.add))
            then(dve.tensor_scalar(rb1[:, 0, :], b1c[:, 1, :], 0.0, None, ALU.max))
            dve.tensor_tensor(rb1[:, 1, :], b1c[:, 1, :], rb1[:, 0, :], ALU.subtract)
            then(dve.tensor_scalar(rb1[:, 2, :], rb1[:, 0, :], -1.0, None, ALU.mult))
            then(dve.reduce_sum(stat[:, 24:25], b2c[:, 1, :], AX.X))
            layernorm(6)
            dve.wait_ge(s["g_proj"], 2)
            logits = ps[:, 2, 0:NT * E16].rearrange("p (t e) -> p t e", t=NT)[:, :, 0:E8]
            then(dve.tensor_tensor(r8(0), logits, brow[:, :].unsqueeze(1).to_broadcast([P, NT, E8]), ALU.add))
            then(dve.reduce_max(tokens(1), r8(0), AX.X))
            dve.tensor_tensor(r8(1), r8(0), per_token(1, E8), ALU.subtract).then_inc(s["route_in"], 1)
            dve.wait_ge(s["route_act"], 3)
            then(dve.reduce_sum(tokens(2), r8(2), AX.X))
            then(dve.reciprocal(tokens(2), tokens(2)))
            then(dve.tensor_tensor(r8(6), r8(2), per_token(2, E8), ALU.mult))
            sel = best(r8(6), E8, 2)
            then(dve.tensor_tensor(r8(7), r8(6), sel, ALU.mult))
            then(dve.reduce_sum(stat[:, 16:16 + NT], r8(7), AX.X))
            dve.memset(stat[:, 13:14], 0.0).then_inc(s["rb_ready"], 1)
            dve.memset(stat[:, 29:30], 0.0).then_inc(s["comb_ready"], 1)
            experts8(1)
            dve.wait_ge(s["sum_ready"], 1)
            then(dve.reduce_sum(stat[:, 25:26], ps[:, 7, 0:E8], AX.X))
            then(dve.tensor_tensor(stat[:, 25:26], stat[:, 25:26], stat[:, 24:25], ALU.add))
            then(dve.scalar_tensor_tensor(out=t2, in0=ps[:, 0:2, :], scalar=stat[:, 25:26], in1=t2, op0=ALU.mult, op1=ALU.add))
            dve.tensor_tensor(xT[:, :, :], xT[:, :, :], t2, ALU.add).then_inc(s["x_ready"], 1)

            layernorm(7)
            dve.wait_ge(s["q3_proj"], 1)
            dve.tensor_copy(t1, ps[:, 0:2, :]).then_inc(s["q3_ready"], 1)
            dve.wait_ge(s["q3_proj"], 2)
            dve.tensor_copy(z, ps[:, 2:4, :]).then_inc(s["q3_ready"], 1)
            dve.wait_ge(s["q3_ready"], 2)
            dve.wait_ge(s["q3_proj"], 3)
            then(dve.tensor_tensor(t2, ps[:, 0:2, :], z, ALU.mult))
            dve.reduce_sum(stat[:, 1:2], t2, AX.XY).then_inc(s["q3_next"], 1)
            then(dve.reduce_sum(stat[:, 8:9], ps[:, 4:6, :], AX.XY))
            then(dve.tensor_scalar(stat[:, 8:9], stat[:, 8:9], 1.0 / T, None, ALU.mult))
            then(dve.tensor_scalar(t2, ps[:, 4:6, :], stat[:, 8:9], None, ALU.subtract))
            then(dve.tensor_tensor(t2, t2, t2, ALU.mult))
            then(dve.reduce_sum(stat[:, 9:10], t2, AX.XY))
            then(dve.tensor_scalar(stat[:, 9:10], stat[:, 9:10], 1.0 / T, None, ALU.mult))
            dve.wait_ge(s["q3_score"], 1)
            dve.scalar_tensor_tensor(out=stat[:, 10:11], in0=ps[:, 2, 0:1], scalar=D / T, in1=stat[:, 9:10],
                                     op0=ALU.mult, op1=ALU.add).then_inc(s["s3_ready"], 1)
            dve.wait_ge(s["s3_root"], 1)
            dve.reciprocal(stat[:, 12:13], stat[:, 11:12]).then_inc(s["s3_ready"], 1)
            dve.tensor_tensor(t2b, z, z, ALU.mult).then_inc(s["b3_sq"], 1)
            dve.wait_ge(s["b3_sum"], 1)
            then(dve.reduce_max(stat[:, 19:20], ps[:, 0:2, :], AX.XY))
            then(dve.tensor_tensor(stat[:, 18:19], stat[:, 12:13], stat[:, 12:13], ALU.mult))
            then(dve.tensor_tensor(stat[:, 18:19], stat[:, 18:19], cpeak[:, 1:2], ALU.mult))
            dve.tensor_tensor(bnd[:, 6:7], stat[:, 19:20], stat[:, 18:19], ALU.mult).then_inc(s["bound_in"], 1)
            set_mode(3, LIMIT ** 2)
            mode3 = mode_of(dve, 3)
            sums_of(3, 0, 0, mode3)
            dve.wait_ge(s["den_ready"], H + 2)
            then(dve.reciprocal(t2, ps[:, 0:2, :]))
            dve.wait_ge(s["av_done"], TILES[3] + RING + ST)
            dve.tensor_tensor(t1, ps[:, 6:8, :], t2, ALU.mult).then_inc(s["o_done"], 1)
            dve.wait_ge(s["wo_ready"], WOUT[3] + 1)
            dve.tensor_tensor(xT[:, :, :], xT[:, :, :], ps[:, 2:4, :], ALU.add).then_inc(s["x_ready"], 1)

            layernorm(8)
            dve.wait_ge(s["route_act"], 4)
            then(dve.tensor_tensor(r16(0), r16(1), ebrow[:, :].unsqueeze(1).to_broadcast([P, NT, E16]), ALU.add))
            sel = best(r16(0), E16, 8)
            then(dve.tensor_tensor(r16(2), r16(1), sel, ALU.mult))
            then(dve.reduce_sum(tokens(2), r16(2), AX.X))
            then(dve.reciprocal(tokens(2), tokens(2)))
            then(dve.tensor_tensor(r16(2), r16(2), per_token(2, E16), ALU.mult))
            dve.tensor_scalar(r16(7), r16(2), ROUTE_SCALE, None, ALU.mult).then_inc(s["comb_ready"], 1)

            def expert16(n, gated):
                dve.wait_ge(s["wt_turned"], n + 1)
                dve.wait_ge(s["y_ready"], n + 1)
                dve.tensor_copy(turned[:, :, :], ps[:, 2, 0:3 * P].rearrange("p (m n) -> p m n", m=3)).then_inc(s["wt_copied"], 1)
                dve.wait_ge(s["hg_act"], n + 1)
                dve.wait_ge(s["hg_ready"], n * 2 + 2)
                if gated:
                    dve.tensor_tensor(t1, t2, ps[:, 2:4, :], ALU.mult).then_inc(s["hm_ready"], 1)
                    dve.wait_ge(s["hm_ready"], n)
                    dve.wait_ge(s["cb_ready"], n + 4 * E8)
                    dve.tensor_tensor(t1, t1, ps[:, 6:8, :], ALU.mult).then_inc(s["hd_ready"], 1)
                else:
                    dve.tensor_tensor(t1, t2, ps[:, 2:4, :], ALU.mult).then_inc(s["hd_ready"], 1)

            expert16(0, False)
            with dve.Fori(1, E16 + 1) as n:
                expert16(n, True)
            dve.wait_ge(s["y_ready"], E16 + 2)
            dve.tensor_tensor(xT[:, :, :], xT[:, :, :], ps[:, 4:6, :], ALU.add).then_inc(s["x_ready"], 1)
            dve.wait_ge(s["out_turned"], 1)
            dve.tensor_copy(probs[:, 0, 0:T].rearrange("p (h n) -> p h n", h=2), ps[:, 0:2, :]).then_inc(s["out_ready"], 1)

        @block.sync
        def _(sp):
            x_rows = a["x"].rearrange("o (p t) d -> (o p) t d", t=NT)
            rows = a["ctx_768"].rearrange("o s c -> (o s) c")
            sp.dma_start(xn, x_rows).then_inc(s["in_x"], 16)
            sp.dma_start(cn[:, 0:SF, :], rows[0:SF * P, :].rearrange("(p t) c -> p t c", t=SF)).then_inc(s["in_ctx0"], 16)
            for m, (name, n, w) in enumerate((("L0_ffn_Wp", P, P), ("L3_xattn_Wq", P, P), ("L3_xattn_Wo", P, P),
                                              ("L3_xattn_Wv", P, C), ("L3_ffn_gate_w", E16, P),
                                              ("L0_ffn_sim_matrix", E8, P))):
                sp.dma_start(wn[0:n, m, 0:w], a[name]).then_inc(s["in_nat"], 16)
            sp.wait_ge(s["consts_set"], NCONST)
            sp.dma_start(cn[0:TAIL, SF, :], rows[SF * P:S, :]).then_inc(s["in_ctx1"], 16)
            for n, l in enumerate(("L0_xattn_", "L2_xattn_")):
                into = s["in_w2" if n else "in_w0"]
                sp.dma_start(w8[:, n, 0, :], a[l + "Wq"]).then_inc(into, 16)
                for m, (w, b) in enumerate((("Wk", "bk"), ("Wv", "bv"))):
                    sp.dma_start(w8[0:C, n, 1 + m, :], a[l + w]).then_inc(into, 16)
                    sp.dma_start(w8[C:C + 1, n, 1 + m, :], a[l + b].rearrange("(o n) -> o n", o=1)).then_inc(into, 16)
                for j in range(G):
                    sp.dma_start(w8[32 * j:32 * j + HD8, n, 3:3 + NG, :],
                                 a[l + "Wo"].rearrange("(g j d) n -> d j g n", g=NG, j=G)[:, j]).then_inc(into, 16)
            sp.dma_start(wk3[:, 0:C], a["L3_xattn_Wk"]).then_inc(s["in_wk3"], 16)

            def attention8(n, layer):
                sp.wait_ge(s["q_split"], QSPLIT[layer] + 2)
                sp.dma_start(qscr[n].rearrange("l p n -> p l n"), qs[:, :, :]).then_inc(s["q_scr"], 16)
                for c, (c0, wd) in enumerate(CHUNKS):
                    sp.wait_ge(s["k_split"], CHUNKED[layer] + c + 1)
                    sp.dma_start(kscr[n].rearrange("l p n -> p l n")[:, :, c0:c0 + wd],
                                 klo[:, c % 2, :].rearrange("p (l n) -> p l n", l=2)[:, :, 0:wd])\
                        .then_inc(s[f"k_scr{c % 2}"], 16)
                sp.wait_ge(s["q_scr"], 16 * (n + 1))
                sp.wait_ge(s["k_scr0"], 16 * ((NC + 1) // 2) * (n + 1))
                sp.wait_ge(s["k_scr1"], 16 * (NC // 2) * (n + 1))
                if n:
                    sp.wait_ge(s["q_zeroed"], 1)
                for g in range(NG):
                    if g >= 2:
                        sp.wait_ge(s["av_done"], TILES[layer] + RING + ST * 2 * (g - 1))
                    for j in range(G):
                        h8 = slice((g * G + j) * HD8, (g * G + j + 1) * HD8)
                        for l in range(2):
                            at = 32 * j + 2 * HD8 * l
                            sp.dma_start(kb[at:at + 2 * HD8, g % 2, :].bitcast(F32),
                                         kscr[n, l, h8, :].unsqueeze(0).to_broadcast([2, HD8, SP]))\
                                .then_inc(s[f"k_in{g % 2}"], 16)
                    for half in range(2):
                        if g:
                            sp.wait_ge(s["av_done"], TILES[layer] + RING + ST * (2 * (g - 1) + half + 1))
                        for j in range(G):
                            h8 = slice((g * G + j) * HD8, (g * G + j + 1) * HD8)
                            for c in range(2):
                                at = 32 * j + 2 * HD8 * c
                                sp.dma_start(qh[at:at + 2 * HD8, half, j, :].bitcast(F32),
                                             qscr[n, :, h8, half * HT:(half + 1) * HT]).then_inc(s[f"q_in{half}"], 16)

            def experts8(m, l, free):
                sp.wait_ge(s["x_ready"], free)
                with sp.Fori(0, E8 // 2) as i:
                    for u in range(2):
                        e = i * 2 + u
                        sp.wait_ge(s["eo_ready"], e + E8 * m + 1)
                        slot = vbuf[:, u * 2 * F:(u + 1) * 2 * F]
                        sp.dma_start(slot[:, 0:F], a[l + "W1"][bass.ds(e, 1), :, :].rearrange("o d f -> (o d) f"))\
                            .then_inc(s[f"moe_w{u}"], 16)
                        sp.dma_start(slot[:, F:2 * F].rearrange("p (f d) -> p f d", f=NF),
                                     a[l + "W2"][bass.ds(e, 1), :, :].rearrange("o (f p) d -> p (o f) d", p=P))\
                            .then_inc(s[f"moe_w{u}"], 16)

            attention8(0, 0)
            experts8(0, "L0_ffn_", 2)
            sp.wait_ge(s["x_ready"], 3)
            for m, (name, rows) in enumerate((("Wk", C), ("Wq", D))):
                sp.dma_start(wqk1[0:rows, m, :], a["L1_xattn_" + name]).then_inc(s["in_qk1"], 16)
            with sp.Fori(0, NP) as p:
                sp.wait_ge(s["wo_ready"], p + WOUT[1])
                cut = bass.ds(p * P, P)
                for e in range(2):
                    sp.dma_start(w64[:, e, :].rearrange("p (c n) -> p c n", c=2),
                                 a["L1_xattn_Wq"][:, bass.ds(p * P + e * HD64, HD64)].unsqueeze(1).to_broadcast([P, 2, HD64]))\
                        .then_inc(s["w1_in"], 16)
                    sp.dma_start(w64[HD64 * e:HD64 * (e + 1), 4:6, :],
                                 a["L1_xattn_Wo"][cut, :].rearrange("(e d) n -> d e n", e=2)).then_inc(s["w1_in"], 16)
                sp.dma_start(w64[0:C, 2, :], a["L1_xattn_Wk"][:, cut]).then_inc(s["w1_in"], 16)
                sp.dma_start(w64[0:C, 3, :], a["L1_xattn_Wv"][:, cut]).then_inc(s["w1_in"], 16)
                for n, (first, m) in enumerate(KP_PIECES):
                    sp.wait_ge(s["k_split"], p * NC + CHUNKED[1] + first + m)
                    c0 = first * HT
                    wd = min(SP, (first + m) * HT) - c0
                    for e in range(2):
                        sp.dma_start(kb[HD64 * (1 - e):HD64 * (2 - e), e, c0:c0 + wd].bitcast(F32),
                                     klo[HD64 * e:HD64 * (e + 1), n % 2, 0:wd]).then_inc(s[f"klo_out{n % 2}"], 16)
            attention8(1, 2)
            experts8(1, "L2_ffn_", 6)
            sp.wait_ge(s["x_ready"], 8)
            for m, name in enumerate(("gate", "up", "down")):
                sp.dma_start(shared[:, m, :], a[f"L3_ffn_shared_{name}_w"]).then_inc(s["in_shared"], 16)
            with sp.Fori(0, E16 // 2) as i:
                for u in range(2):
                    e = i * 2 + u
                    sp.wait_ge(s["y_ready"], e + 1)
                    for m, name in enumerate(("gate", "up", "down")):
                        sp.dma_start(ex_w[u][:, m, :], a[f"L3_ffn_w_{name}"][bass.ds(e, 1), :, :].rearrange("o i d -> (o i) d"))\
                            .then_inc(s[f"ex_w{u}"], 16)
            sp.wait_ge(s["out_ready"], 1)
            sp.dma_start(a["out"].rearrange("o (p t) d -> (o p) t d", t=NT), xn).then_inc(s["out_stored"], 16)
            sp.wait_ge(s["out_stored"], 16)


INPUTS = [
    "x", "ctx_768",
    "L0_xattn_Wq", "L0_xattn_bq", "L0_xattn_Wk", "L0_xattn_bk", "L0_xattn_Wv", "L0_xattn_bv", "L0_xattn_Wo", "L0_xattn_bo",
    "L0_ffn_Wp", "L0_ffn_sim_matrix", "L0_ffn_temperature", "L0_ffn_W1", "L0_ffn_b1", "L0_ffn_W2", "L0_ffn_b2",
    "L1_xattn_Wq", "L1_xattn_Wk", "L1_xattn_Wv", "L1_xattn_Wo", "L1_xattn_bo",
    "L1_ffn_kernel", "L1_ffn_input_scale", "L1_ffn_kernel_scale", "L1_ffn_bias",
    "L2_xattn_Wq", "L2_xattn_bq", "L2_xattn_Wk", "L2_xattn_bk", "L2_xattn_Wv", "L2_xattn_bv", "L2_xattn_Wo", "L2_xattn_bo",
    "L2_ffn_gamma", "L2_ffn_beta", "L2_ffn_Wr", "L2_ffn_br", "L2_ffn_W1", "L2_ffn_b1", "L2_ffn_W2", "L2_ffn_b2",
    "L3_xattn_Wq", "L3_xattn_Wk", "L3_xattn_Wv", "L3_xattn_Wo",
    "L3_ffn_gate_w", "L3_ffn_expert_bias", "L3_ffn_w_gate", "L3_ffn_w_up", "L3_ffn_w_down",
    "L3_ffn_shared_gate_w", "L3_ffn_shared_up_w", "L3_ffn_shared_down_w",
]


def kernel(**inputs):
    import numpy as np
    import concourse.bacc as bacc
    from concourse.bass_utils import run_bass_kernel_spmd

    nc = bacc.Bacc("TRN2", target_bir_lowering=False, num_devices=1)
    arrays, dram = {}, {}
    for name in INPUTS:
        array = np.atleast_1d(np.ascontiguousarray(inputs[name]))
        arrays[f"in_{name}"] = array
        dram[name] = nc.dram_tensor(f"in_{name}", array.shape, mybir.dt.from_np(array.dtype), kind="ExternalInput").ap()
    dram["out"] = nc.dram_tensor("out_x", (1, T, D), F32, kind="ExternalOutput").ap()
    build_program(nc, dram)
    result = run_bass_kernel_spmd(nc, [arrays], core_ids=[0])
    return result.results[0]["out_x"]
```

```python
from contextlib import ExitStack

import concourse.bass as bass
from concourse import mybir

F32 = mybir.dt.float32
F32R = mybir.dt.float32r
I32 = mybir.dt.int32
BF16 = mybir.dt.bfloat16
ACT = mybir.ActivationFunctionType
ALU = mybir.AluOpType
AX = mybir.AxisListType

P = 128
D = 128
C = 96
T = 1024
NT = T // P
HT = 512
S = 6404
SF = S // P
TAIL = S - SF * P
ST = SF + 1
SP = ST * P
H = 16
CHUNKS = [(c, min(HT, SP - c)) for c in range(0, SP, HT)]
NC = len(CHUNKS)
VG = [(t, min(4, ST - t)) for t in range(0, ST, 4)]
NVG = len(VG)
E8 = 8
F = 512
NF = F // P
E16 = 16
HD8 = D // H
G = 4
NG = H // G
HD64 = 64
NP = H // 2
LN_EPS = 1e-5
TINY = 1e-12
ROUTE_SCALE = 2.826
FP8_MAX = 448.0
LIMIT = 60.0
CLIP = 1e4 * HD8 ** 0.5
HUGE = 3e38
SHRINK = 2.0 ** -20
PU = 2 * ST
RING = 3

STAGED = {0: 0, 2: 4 * NG * ST, 3: 8 * NG * ST}

TILES = {0: 0, 1: 2 * NG * ST, 2: 2 * NG * ST + H * ST, 3: 4 * NG * ST + H * ST}
UNITS = {0: 0, 1: 4 * NG * ST, 2: 4 * NG * ST + H * ST, 3: 8 * NG * ST + H * ST}
SUMS = {0: 0, 1: 2 * NG, 2: 2 * NG + H, 3: 4 * NG + H}
CHUNKED = {0: 0, 1: NC, 2: (1 + NP) * NC}
QSPLIT = {0: 0, 1: 3, 2: 3 + 4 * NP}
QPROJ = {0: 0, 1: 1, 2: 1 + 2 * NP}
assert NVG == NC and ST % RING == 0
NIDENT = 2
NCONST = 20
ADDED = {1: 0, 3: H * ST}
NCOLS = 18
PIECE = 17
PIECES = [(t, min(SF, t + PIECE)) for t in range(0, SF, PIECE)]
WOUT = {0: 0, 1: 1, 2: 1 + NP, 3: 2 + NP}


def build_program(nc, a):
    ctx = ExitStack()
    with ctx:
        def sb(name, shape, dt=F32):
            return ctx.enter_context(nc.sbuf_tensor(name, shape, dt))

        def sem(name):
            return ctx.enter_context(nc.semaphore(name))

        ps = ctx.enter_context(nc.psum_tensor("ps", [P, 8, HT], F32))

        xT = sb("xT", [P, 2, HT])
        work = sb("work", [P, 4, 2, HT])
        z, t1, t2, t3 = (work[:, n] for n in range(4))
        sums = work[:, :, :, :].rearrange("p a h n -> p (a h) n")
        ctxT = sb("ctxT", [P, NC * HT])
        kb = sb("kb", [P, 2, SP], F32R)
        klo = sb("klo", [P, 2, 2 * HT])
        vbuf = sb("vbuf", [P, ST * H * (HD8 + 1)])
        qz = sb("qz", [P, 4 * 2 * HT], F32R)
        qs = sb("qs", [P, 2, 2 * HT])
        probs = sb("probs", [P, RING, 4 * HT])
        kst = sb("kst", [P, RING, P], F32R)
        vst = sb("vst", [P, RING, P])
        cst = sb("cst", [P, RING, P])
        w8 = sb("w8", [P, 2, 3 + NG, P])
        w64 = sb("w64", [P, 6, P])
        wT = sb("wT", [P, 6, P])
        wk3 = sb("wk3", [P, P])
        kernel8 = sb("kernel8", [P, P], BF16)
        cols = sb("cols", [P, 16])
        z8 = sb("z8", [P, 2, HT], BF16)
        kernel8q = sb("kernel8q", [P, P], BF16)
        wr2 = sb("wr2", [P, E8])
        bias8 = sb("bias8", [P, 1], BF16)
        b1c = sb("b1c", [P, 2, E8 * NF])
        rb1 = sb("rb1", [P, 3, E8 * NF])
        b2c = sb("b2c", [P, 2, E8])
        brow = sb("brow", [P, E8])
        ebrow = sb("ebrow", [P, E16])
        ident = sb("ident", [P, P])
        ones = sb("ones", [P, P])
        ones_b = sb("ones_b", [P, P], BF16)
        mean_d = sb("mean_d", [P, P])
        dsel = sb("dsel", [P, P])
        before = sb("before", [P, E16, E16])
        ccol = sb("ccol", [P, 2, NT])
        stat = sb("stat", [P, 32])
        cov = sb("cov", [P, P])
        heads = sb("heads", [P, 32], BF16)
        peak = sb("peak", [P, 2 * NC + 6])
        bnd = sb("bnd", [P, 8])
        given = sb("given", [P, 28])
        warm = sb("warm", [P, 6])
        cpeak = sb("cpeak", [P, 2])
        picks = sb("picks", [P, E16])
        pick = sb("pick", [P, 2], F32R)

        shared = vbuf[:, 6 * P:9 * P].rearrange("p (m n) -> p m n", m=3)
        turned = (cst, vst)
        route = qs[:, :, :].rearrange("p l (m n) -> p (l m) n", m=8)
        flat = probs[:, :, :].rearrange("p a n -> p (a n)")
        wsq = flat[0:E8, 3 * T:3 * T + P]
        cmean = flat[:, 5 * T:5 * T + C]
        xn = probs[:, 0, 0:NT * D].rearrange("p (t d) -> p t d", t=NT)
        wn = probs[:, 1, 0:6 * P].rearrange("p (m n) -> p m n", m=6)
        cn = vbuf[:, 0:ST * C].rearrange("p (t c) -> p t c", t=ST)
        cn2 = vbuf[:, 2 * T:2 * T + ST * C].rearrange("p (t c) -> p t c", t=ST)
        keyrow, queryrow = (place[:, :, :].rearrange("p a n -> p (a n)") for place in (klo, qs))
        pieces = [place[:, 0:(end - t0) * C].rearrange("p (t c) -> p t c", c=C)
                  for place, (t0, end) in zip((keyrow, queryrow, keyrow), PIECES)]
        rest, lens = (keyrow[0:TAIL, PIECE * C:(PIECE + 1) * C], keyrow[:, (PIECE + 1) * C:(PIECE + 1) * C + ST])
        vx = vbuf[:, :].rearrange("p (t h w) -> p t h w", t=ST, h=H)
        vp = vbuf[:, 0:ST * P]
        qh = qz[:, :].rearrange("p (s j n) -> p s j n", s=2, j=G)
        qp = qz[:, :].rearrange("p (e l h n) -> p e l h n", e=2, l=2, h=2)
        shares = qz[0:64, 0:2 * HT].rearrange("p (h n) -> p h n", h=2)
        hid = probs[:, 0:2, :].rearrange("p a (f h n) -> p (a f) h n", f=2, h=2)
        kscr = nc.dram_tensor("k_scratch", [2, 2, P, SP], F32, kind="Internal").ap()
        qscr = nc.dram_tensor("q_scratch", [2, 2, P, T], F32, kind="Internal").ap()
        BQ0, BO0, BQ2, BO2, BO1, GAM, BET, TEMP, SIN, SK, EPS, MODE = range(12)
        top = klo[:, :, :].rearrange("p a (b n) -> p (a b) n", n=HT)
        topcol = ccol[:, :, :].rearrange("p a t -> p (a t)")
        wqk1 = vbuf[:, 0:2 * T].rearrange("p (m n) -> p m n", m=2)
        gram = vbuf[:, 2 * T:2 * T + T // 2].bitcast(BF16).rearrange("p (m n) -> p m n", n=P)
        kch = kb[:, 0, 0:4 * HT].rearrange("p (c e n) -> p c e n", c=2, e=2)
        vch = vbuf[:, 3 * T:4 * T].rearrange("p (c n) -> p c n", c=2)
        cch = vbuf[:, 4 * T:4 * T + HT]
        sum1 = vbuf[:, 5 * T:7 * T].rearrange("p (e h n) -> p e h n", e=2, h=2)
        pr1 = flat[:, 0:4 * T].rearrange("p (u h n) -> p u h n", u=4, h=2)
        t2b, t3b = (work[:, n].bitcast(BF16)[:, :, 0:HT] for n in (2, 3))
        t1r = t1.rearrange("p h n -> p (h n)").bitcast(BF16).rearrange("p (u h n) -> p u h n", u=2, h=2)

        ex_w = [vbuf[:, u * 3 * P:(u + 1) * 3 * P].rearrange("p (m n) -> p m n", m=3) for u in range(2)]
        stores = [[n * ((NC + 1 - c % 2) // 2) + c // 2 for c in range(NC)] for n in range(2)]

        def col(n):
            return cols[:, n:n + 1]

        def tok(ap, t):
            return ap[:, t // 4, (t % 4) * P:(t % 4 + 1) * P]

        names = (
            "consts_set in_x in_ctx0 in_ctx1 in_nat in_cols in_w0 in_w2 turned ctx_turned ctx_even "
            "ctx_odd w_copied sim_root sim_ready cmean_ready ccent_ready cmean_copied in_piece piece_used zeros_set "
            "cov_ready cov_copied dve_step x_ready ln_mean ln_sq ln_var ln_std z_ready "
            "q_proj q_split q_scr k_proj k_high k_split v_proj v_copied v_ones q_zeroed "
            "staged scores_ready exp_done av_done acc_copied added den_ready o_done wo_ready x_added "
            "p_proj p_ready g_proj comb_ready ccol_ready h_ready hid_ready eo_ready eo_used cb_ready "
            "cb_copied moe_acc sum_ready in_wq1 in_wkv1 in_wo1 c_staged q1_high k1_high max_kproj max_khigh max_klow f8_ready f8_done den8 y_ready "
            "q3_proj q3_ready q3_next q3_score s3_ready s3_root v3_copied wt_turned wt_copied hg_ready hg_act "
            "hd_ready ex_w0 ex_w1 moe_w0 moe_w1 k_scr0 k_scr1 k_in0 k_in1 q_in0 q_in1 "
            "out_ready out_stored in_shared rb_ready route_in route_act rec_ready den_copied rec8 hm_ready"
        ).split()
        names += ("norm_sq norm_mm norm_max bound_in bound_out mode_set norm_qsq norm_qmm norm_qmax ln_cent ln_rec ln_spread in_ctx2 in_qk1 "
                  "gram_ready gram_copied b1_q b1_copied b1_r b1_prod b1_sum b1_max ").split()
        names += [f"{n}{l}" for n in ("max_staged", "max_scores", "max_read", "max_spread", "max_known", "shift_sub", "shifted")
                  for l in range(4) if (n, l) != ("max_staged", 1)]
        s = {n: sem(n) for n in names}

        def mode_of(engine, layer):
            engine.wait_ge(s["mode_set"], layer + 1)
            return engine.value_load(cols[0:1, MODE + layer:MODE + layer + 1].bitcast(I32), min_val=0, max_val=2)

        block = ctx.enter_context(nc.Block())

        @block.tensor
        def _(pe):
            def ln_mean(k):
                src = z if k == 6 else xT[:, :, :]
                if k == 6:
                    pe.wait_ge(s["z_ready"], 6)
                else:
                    pe.wait_ge(s["x_ready"], k + 1 if k < 6 else k)
                for h in range(2):
                    pe.matmul(ps[:, h, :], mean_d[:, :], src[:, h, :], start=True, stop=True).then_inc(s["ln_mean"], 1)

            def ln_var(k):
                for h in range(2):
                    pe.wait_ge(s["ln_sq"], 2 * k + h + 1)
                    for t in range(4 * h, 4 * h + 4):
                        mm = pe.matmul(ps[:, 3, t:t + 1], tok(t2, t), mean_d[:, 0:1], start=True, stop=True)
                mm.then_inc(s["ln_var"], 1)

            def ln_spread(k):
                pe.wait_ge(s["ln_rec"], k + 1)
                for h in range(2):
                    for t in range(4 * h, 4 * h + 4):
                        mm = pe.matmul(ps[:, h, (t % 4) * P:(t % 4 + 1) * P], ccol[:, 1, t:t + 1].to_broadcast([P, P]),
                                       ident[:, :], start=True, stop=True)
                    mm.then_inc(s["ln_spread"], 1)

            def layernorm(k):
                ln_mean(k)
                ln_var(k)
                ln_spread(k)

            def stream(first, qk, av, between=lambda: None):
                qk(first, 0)
                for t in range(RING):
                    qk(first + t + 1, (t + 1) % RING)
                    av(first + t, t, t == 0, False)
                between()
                with pe.Fori(0, ST // RING - 2) as i:
                    for u in range(RING):
                        qk(first + i * RING + RING + u + 1, (u + 1) % RING)
                        av(first + i * RING + RING + u, u, False, False)
                for t in range(ST - RING, ST):
                    if t + 1 < ST:
                        qk(first + t + 1, (t + 1) % RING)
                    av(first + t, t % RING, False, t + 1 == ST)

            def maxima(layer, count, banks, units, qk):
                with pe.Fori(0, ST) as t:
                    pe.wait_ge(s["exp_done"], UNITS[layer] + RING + count * units)
                    pe.wait_ge(s[f"max_staged{layer}"], count * ST + t + 1)
                    pe.wait_ge(s[f"max_read{layer}"], count * ST + t + 1)
                    qk().then_inc(s[f"max_scores{layer}"], 1)
                spread_maxima(layer, count, banks)

            def spread_maxima(layer, count, banks):
                pe.wait_ge(s[f"max_read{layer}"], count * ST + ST + 1)
                for b in range(4 * banks):
                    mm = pe.transpose(ps[:, b // 4, (b % 4) * P:(b % 4 + 1) * P],
                                      top[:, b // 4, (b % 4) * P:(b % 4 + 1) * P], ident[:, :])
                mm.then_inc(s[f"max_spread{layer}"], 1)
                pe.wait_ge(s[f"max_known{layer}"], count * 2 + 1)
                for b in range(4 * banks):
                    mm = pe.matmul(ps[:, b // 4, (b % 4) * P:(b % 4 + 1) * P], topcol[:, b:b + 1].to_broadcast([P, P]),
                                   ident[:, :], start=True, stop=True)
                mm.then_inc(s[f"max_spread{layer}"], 1)
                pe.wait_ge(s[f"max_known{layer}"], count * 2 + 2)

            def spread_bound(layer):
                pe.wait_ge(s["bound_in"], layer + 1)
                pe.matmul(ps[:, 2, 0:P], bnd[:, 2 * layer:2 * layer + 1].to_broadcast([P, P]), ident[:, :], start=True, stop=True)
                pe.matmul(ps[:, 2, P:P + 1], ones[:, :], bnd[:, 2 * layer + 1:2 * layer + 2], start=True, stop=True)\
                    .then_inc(s["bound_out"], 1)

            pe.wait_ge(s["consts_set"], NIDENT)
            pe.wait_ge(s["in_x"], 16)
            for t in range(NT):
                mm = pe.transpose(ps[:, t // 4, (t % 4) * P:(t % 4 + 1) * P], xn[:, t, :], ident[:, :])
            mm.then_inc(s["turned"], 1)
            for g, (t0, n) in enumerate(VG):
                if g == 0:
                    pe.wait_ge(s["in_ctx0"], 16)
                if g == NVG // 2:
                    pe.wait_ge(s["in_ctx1"], 32)
                if g >= 4:
                    pe.wait_ge(s["ctx_odd" if g % 2 else "ctx_even"], (g - 4) // 2 + 1)
                for u in range(n):
                    mm = pe.transpose(ps[0:C, 2 + g % 4, u * P:(u + 1) * P], cn[:, t0 + u, :], ident[:, :])
                mm.then_inc(s["ctx_turned"], 1)
            pe.wait_ge(s["consts_set"], NCONST)

            def turn_weights():
                pe.wait_ge(s["in_nat"], 16 * 6)
                for m, w in enumerate((P, P, P, C)):
                    mm = pe.transpose(ps[0:w, 0, m * P:(m + 1) * P], wn[:, m, 0:w], ident[:, :])
                mm.then_inc(s["turned"], 1)
                pe.wait_ge(s["sim_ready"], 2)
                pe.transpose(ps[:, 1, 0:E16], wn[0:E16, 4, :], ident[0:E16, 0:E16])
                pe.transpose(ps[:, 1, E16:E16 + E8], wn[0:E8, 5, :], ident[0:E8, 0:E8]).then_inc(s["turned"], 1)

            def queries8(n, layer, ln):
                pe.wait_ge(s["z_ready"], ln + 1)
                for h in range(2):
                    mm = pe.matmul(ps[:, h, :], w8[:, n, 0, :], z[:, h, :], start=True, stop=True)
                mm.then_inc(s["q_proj"], 1)

            def query_norms8(n):
                pe.wait_ge(s["norm_qsq"], n + 1)
                for h in range(2):
                    mm = pe.matmul(ps[0:32, h, :], heads[:, :], t2b[:, h, :], start=True, stop=True)
                mm.then_inc(s["norm_qmm"], 1)

            def keys8(n, layer, between):
                w = w8[:, n]
                base = n * NC

                def norms(c):
                    wd = CHUNKS[c][1]
                    pe.wait_ge(s["norm_sq"], base + c + 1)
                    if c:
                        pe.wait_ge(s["norm_max"], base + c)
                    pe.matmul(ps[0:32, 2, 0:wd], heads[:, :], t3b[:, c % 2, 0:wd], start=True, stop=True)\
                        .then_inc(s["norm_mm"], 1)

                pe.wait_ge(s["in_w2" if n else "in_w0"], 16 * 10)
                if n == 0:
                    pe.wait_ge(s["zeros_set"], 5)
                    pe.wait_ge(s["ctx_even"], (NVG + 1) // 2)
                    pe.wait_ge(s["ctx_odd"], NVG // 2)
                for c, (c0, wd) in enumerate(CHUNKS):
                    if c >= 2:
                        pe.wait_ge(s["k_split"], CHUNKED[layer] + c - 1)
                    pe.matmul(ps[:, 6 + c % 2, 0:wd], w[:, 1, :], ctxT[:, c0:c0 + wd], start=True, stop=True)\
                        .then_inc(s["k_proj"], 1)
                    t0, m = VG[c]
                    if c >= 2:
                        pe.wait_ge(s["v_copied"], CHUNKED[layer] + c - 1)
                    for u in range(m):
                        mm = pe.matmul(ps[:, 4 + c % 2, u * P:(u + 1) * P], ctxT[:, (t0 + u) * P:(t0 + u + 1) * P],
                                       w[:, 2, :], start=True, stop=True)
                    mm.then_inc(s["v_proj"], 1)
                    if c:
                        norms(c - 1)
                    if c in between:
                        between[c]()
                norms(NC - 1)

            def attention8(n, layer):
                w = w8[:, n]
                pe.wait_ge(s["norm_max"], NC * (n + 1))
                spread_bound(layer)
                mode = mode_of(pe, layer)

                def denominators(gh, half):
                    pe.wait_ge(s["acc_copied"], gh + SUMS[layer] + 3)
                    pe.matmul(ps[:, 6 + half, :], dsel[:, :], sums[:, bass.ds(gh, 1), :].rearrange("p o n -> p (o n)"),
                              start=True, stop=True).then_inc(s["den8"], 1)

                def group(gi, par):
                    g = gi * 2 + par
                    for half in range(2):
                        def qk_maxima():
                            for j in range(G):
                                mm = pe.matmul(ps[:, j, :], kst[:, 0, :], qh[:, half, j, :], start=True, stop=True)
                            return mm

                        local = (g * 2 + half) * ST
                        pe.wait_ge(s[f"q_in{half}"], g * (32 * G) + 32 * G * (NG * n + 1))

                        def qk(t, r):
                            pe.wait_ge(s["staged"], (t - TILES[layer]) * 2 + STAGED[layer] + 2)
                            for b in range(2):
                                buf = (2 * r + b) % RING
                                pe.wait_ge(s["exp_done"], (t - TILES[layer]) * 2 + UNITS[layer] + b + 1)
                                for j in range(2):
                                    mm = pe.matmul(ps[:, 2 * buf + j, :], kst[:, r, :], qh[:, half, 2 * b + j, :],
                                                   start=True, stop=True)
                                mm.then_inc(s["scores_ready"], 1)

                        def av(t, r, start, stop):
                            if start:
                                pe.wait_ge(s["o_done"], g * 2 + half + SUMS[layer] + 1)
                            pe.wait_ge(s["exp_done"], (t - TILES[layer]) * 2 + UNITS[layer] + 2 + RING)
                            for j in range(G):
                                mm = pe.matmul(ps[32 * j:32 * j + 32, 6 + half, :], vst[:, r, 32 * j:32 * j + 32],
                                               probs[:, r, j * HT:(j + 1) * HT], start=start, stop=stop)
                            mm.then_inc(s["av_done"], 1)

                        with pe.If(mode >= 1):
                            maxima(layer, g * 2 + half, G, 2 * ST, qk_maxima)
                        def last_sums():
                            if half:
                                denominators(g * 2, 0)
                            elif par:
                                denominators(gi * 4 + 1, 1)
                            else:
                                with pe.If(gi >= 1):
                                    denominators(3, 1)

                        stream(local + TILES[layer], qk, av, last_sums)

                pe.wait_ge(s["v_copied"], CHUNKED[layer] + NVG)
                pe.wait_ge(s["k_split"], CHUNKED[layer] + NC)
                pe.wait_ge(s["q_split"], QSPLIT[layer] + 3)
                with pe.Fori(0, NG // 2) as gi:
                    for par in range(2):
                        group(gi, par)
                denominators(2 * NG - 1, 1)
                for half in range(2):
                    for g in range(NG):
                        if g == NG - 1:
                            pe.wait_ge(s["o_done"], SUMS[layer] + 2 * g + half + 3)
                        mm = pe.matmul(ps[:, 4 + half, :], w[:, 3 + g, :], sums[:, 2 * g + half, :],
                                       start=(g == 0), stop=(g == NG - 1))
                mm.then_inc(s["wo_ready"], 1)

            def experts8(m):
                def expert(i, u):
                    e = i * 2 + u
                    n = e + E8 * m
                    wts = vbuf[:, u * 2 * F:(u + 1) * 2 * F]
                    pe.wait_ge(s[f"moe_w{u}"], i * 32 + 32 * (E8 // 2 * m + 1))
                    for f in range(NF):
                        pe.wait_ge(s["hid_ready"], n * NF + f + 1)
                        for h in range(2):
                            mm = pe.matmul(ps[:, 2 * (f % 2) + h, :], wts[:, f * P:(f + 1) * P], z[:, h, :],
                                           start=True, stop=True)
                        mm.then_inc(s["h_ready"], 1)
                    pe.wait_ge(s["ccol_ready"], n + 1)
                    for h in range(2):
                        pe.wait_ge(s["cb_copied"], n * 2 + h + 1)
                        for t in range(4):
                            mm = pe.matmul(ps[:, 6, t * P:(t + 1) * P],
                                           ccol[:, u, 4 * h + t:4 * h + t + 1].to_broadcast([P, P]), ident[:, :],
                                           start=True, stop=True)
                        mm.then_inc(s["cb_ready"], 1)
                        if h == 0:
                            pe.wait_ge(s["eo_used"], n + 1)
                            if m == 1:
                                pe.wait_ge(s["rb_ready"], 1)
                                for f in range(NF):
                                    pe.matmul(ps[:, 7, bass.ds(e, 1)], wts[:, F + f * D:F + (f + 1) * D],
                                              rb1[:, 0, bass.ds(e * NF + f, 1)], start=(f == 0), stop=(f == NF - 1))
                        for f in range(NF):
                            pe.wait_ge(s["hid_ready"], n * NF + f + 3)
                            mm = pe.matmul(ps[:, 4 + h, :], wts[:, F + f * D:F + (f + 1) * D], hid[:, f, h, :],
                                           start=(f == 0), stop=(f == NF - 1))
                    mm.then_inc(s["eo_ready"], 1)

                with pe.Fori(0, E8 // 2) as i:
                    for u in range(2):
                        expert(i, u)

            pe.wait_ge(s["x_ready"], 1)
            keys8(0, 0, {1: lambda: ln_mean(0), 2: lambda: ln_var(0), 3: lambda: ln_spread(0),
                         5: lambda: queries8(0, 0, 0), 7: lambda: query_norms8(0)})
            pe.wait_ge(s["norm_qmax"], 1)
            turn_weights()
            pe.wait_ge(s["w_copied"], 1)
            attention8(0, 0)

            layernorm(1)
            pe.wait_ge(s["z_ready"], 2)
            for h in range(2):
                mm = pe.matmul(ps[:, h, :], wT[:, 0, :], z[:, h, :], start=True, stop=True)
            mm.then_inc(s["p_proj"], 1)
            pe.wait_ge(s["p_ready"], 1)
            for t in range(NT):
                pe.matmul(ps[:, 6, t * E16:t * E16 + E8], tok(t1, t), wT[:, 5, 0:E8], start=True, stop=True)
                mm = pe.matmul(ps[:, 6, t * E16 + E8:t * E16 + E8 + 1], tok(t2, t), ones[:, 0:1], start=True, stop=True)
            mm.then_inc(s["g_proj"], 1)
            experts8(0)

            layernorm(2)
            pe.wait_ge(s["z_ready"], 3)
            pe.wait_ge(s["in_qk1"], 32)
            for p in range(NP):
                cut = slice(p * P, (p + 1) * P)
                mm = pe.matmul(ps[:, 6 + p // 4, (p % 4) * P:(p % 4 + 1) * P], wqk1[0:C, 0, cut], wqk1[0:C, 0, cut],
                               start=True, stop=True)
            mm.then_inc(s["gram_ready"], 1)

            def pair_squares(p):
                pe.wait_ge(s["gram_copied"], 2)
                pe.wait_ge(s["b1_copied"], p + 1)
                pe.wait_ge(s["b1_prod"], p + 1)
                for h in range(2):
                    mm = pe.matmul(ps[:, 4 + h, :], gram[:, p, :],
                                   (t2b, t3b)[p % 2][:, h, :], start=True, stop=True)
                mm.then_inc(s["b1_r"], 1)

            def pair_sums(p):
                pe.wait_ge(s["b1_prod"], p + 2)
                if p:
                    pe.wait_ge(s["b1_max"], p)
                for h in range(2):
                    mm = pe.matmul(ps[:, 6 + h, :], ones_b[:, :], t1r[:, p % 2, h, :], start=True, stop=True)
                mm.then_inc(s["b1_sum"], 1)

            for p in range(NP):
                if p >= 2:
                    pe.wait_ge(s["b1_copied"], p - 1)
                for h in range(2):
                    mm = pe.matmul(ps[:, 2 * (p % 2) + h, :], wqk1[:, 1, p * P:(p + 1) * P], z[:, h, :], start=True, stop=True)
                mm.then_inc(s["b1_q"], 1)
                if p:
                    pair_squares(p - 1)
                if p >= 2:
                    pair_sums(p - 2)
            pair_squares(NP - 1)
            pair_sums(NP - 2)
            pair_sums(NP - 1)
            pe.wait_ge(s["b1_copied"], NP)
            pe.wait_ge(s["bound_in"], 2)
            pe.matmul(ps[:, 2, 2 * P:3 * P], cpeak[:, 0:1].to_broadcast([P, P]), ident[:, :], start=True, stop=True)
            spread_bound(1)
            mode1 = mode_of(pe, 1)
            K0 = CHUNKED[1]

            def keys1(p, c, c0, wd):
                pe.wait_ge(s["k_split"], p * NC + K0 + c)
                pe.matmul(ps[:, 6, 0:wd], w64[:, 2, :], ctxT[:, bass.ds(c0, wd)], start=True, stop=True)\
                    .then_inc(s["k_proj"], 1)

            def values1(p, c, m):
                pe.wait_ge(s["v_copied"], p * NC + K0 + c)
                pe.wait_ge(s["c_staged"], p * NC + c + 1)
                for u in range(m):
                    mm = pe.matmul(ps[:, 7, u * P:(u + 1) * P], cch[:, u * P:(u + 1) * P], w64[:, 3, :],
                                   start=True, stop=True)
                mm.then_inc(s["v_proj"], 1)

            def scores1(e, slot, u):
                for h in range(2):
                    for l in range(2):
                        mm = pe.matmul(ps[:, 2 * e + h, :], kch[:, slot, e, u * P:(u + 1) * P], qp[:, e, l, h, :],
                                       start=(l == 0), stop=(l == 1))
                return mm

            def qk1(p, c, slot, i):
                unit = p * PU + c * 8 + i
                if i == 0:
                    pe.wait_ge(s["k_split"], p * NC + K0 + c + 1)
                pe.wait_ge(s["exp_done"], unit + UNITS[1] + RING - 1)
                scores1(i % 2, slot, i // 2).then_inc(s["scores_ready"], 1)

            def av1(p, c, slot, i, start, stop):
                unit = p * PU + c * 8 + i
                e = i % 2
                if i == 0:
                    pe.wait_ge(s["v_copied"], p * NC + K0 + c + 1)
                if start and p is not first_pair:
                    pe.wait_ge(s["den_copied"], p)
                pe.wait_ge(s["exp_done"], unit + UNITS[1] + RING + 1)
                for h in range(2):
                    mm = pe.matmul(ps[64 * h:64 * h + 64, 4 + e, :], vch[:, slot, (i // 2) * P + e * HD64:(i // 2) * P + (e + 1) * HD64],
                                   pr1[:, i % 4, h, :], start=start, stop=stop)
                mm.then_inc(s["av_done"], 1)

            def chunk1(p, c, at, slot, last):
                m = VG[at][1]
                for u in range(m):
                    for e in range(2):
                        if u + 1 < m:
                            qk1(p, c, slot, 2 * u + 2 + e)
                        elif not last:
                            qk1(p, c + 1, 1 - slot, e)
                    for e in range(2):
                        av1(p, c, slot, 2 * u + e, at == 0 and u == 0, last and u == m - 1)
                    if at == 1 and u == 0 and p is not first_pair:
                        output1(p - 1)
                    if at == 1 and u == 1 and p is not first_pair:
                        pe.wait_ge(s["x_added"], p + 1)
                    if not last and u == (1 if at == 1 else 0):
                        keys1(p, c + 1, c * HT + HT, CHUNKS[at + 1][1])
                        values1(p, c + 1, VG[at + 1][1])

            def sums1(p):
                pe.wait_ge(s["added"], p * PU + ADDED[1] + RING + PU)
                pe.wait_ge(s["acc_copied"], p * 2 + SUMS[1] + 4)
                for e in range(2):
                    for h in range(2):
                        mm = pe.matmul(ps[64 * h:64 * h + 64, 4 + e, :], ones[:, 0:HD64], sum1[:, e, h, :], start=True, stop=True)
                    mm.then_inc(s["den_ready"], 1)

            def output1(p):
                pe.wait_ge(s["in_wo1"], p * 32 + 32)
                if p is not NP - 1:
                    pe.wait_ge(s["k_split"], p * NC + K0 + NC + 2)
                    pe.wait_ge(s["v_copied"], p * NC + K0 + NC + 2)
                for e in range(2):
                    pe.wait_ge(s["o_done"], p * 2 + SUMS[1] + 3 + e)
                    for h in range(2):
                        mm = pe.matmul(ps[:, 6 + h, :], w64[64 * h:64 * h + 64, 4 + e, :], t1[64 * h:64 * h + 64, e, :],
                                       start=(e == 0), stop=(e == 1))
                mm.then_inc(s["wo_ready"], 1)

            def maxima1(p):
                def chunk(c, at):
                    pe.wait_ge(s["max_klow"], p * NC + c + 1)
                    pe.wait_ge(s["k_split"], p * NC + K0 + 1)
                    wd = CHUNKS[at][1]
                    pe.matmul(ps[:, 6, 0:wd], w64[:, 2, :], ctxT[:, bass.ds(c * HT, wd)], start=True, stop=True)\
                        .then_inc(s["max_kproj"], 1)
                    pe.wait_ge(s["max_klow"], p * NC + c + 2)
                    for u in range(VG[at][1]):
                        pe.wait_ge(s["max_read1"], p * ST + c * 4 + u + 1)
                        scores1(0, 1, u)
                        scores1(1, 1, u).then_inc(s["max_scores1"], 1)

                with pe.Fori(0, NC - 1) as c:
                    chunk(c, 0)
                chunk(NC - 1, NC - 1)
                spread_maxima(1, p, 4)

            first_pair = 0

            def pair1(p):
                pe.wait_ge(s["in_wq1"], p * 32 + 32)
                for e in range(2):
                    pe.wait_ge(s["exp_done"], p * PU + UNITS[1] + RING - 1 + e)
                    for h in range(2):
                        mm = pe.matmul(ps[:, 2 * e + h, :], w64[:, e, :], z[:, h, :], start=True, stop=True)
                    mm.then_inc(s["q_proj"], 1)
                pe.wait_ge(s["in_wkv1"], p * 32 + 32)
                keys1(p, 0, 0, CHUNKS[0][1])
                values1(p, 0, VG[0][1])
                if p is not first_pair:
                    sums1(p - 1)
                pe.wait_ge(s["q_split"], p * 4 + QSPLIT[1] + 4)
                with pe.If(mode1 >= 1):
                    maxima1(p)
                for e in range(2):
                    qk1(p, 0, 0, e)
                chunk1(p, 0, 0, 0, False)
                chunk1(p, 1, 1, 1, False)
                with pe.Fori(0, (NC - 3) // 2 - 1) as i:
                    chunk1(p, i * 2 + 2, 2, 0, False)
                    chunk1(p, i * 2 + 3, 3, 1, False)
                chunk1(p, NC - 3, NC - 3, 0, False)
                chunk1(p, NC - 2, NC - 2, 1, False)
                chunk1(p, NC - 1, NC - 1, 0, True)

            pair1(first_pair)
            with pe.Fori(1, NP) as p:
                pair1(p)
            sums1(NP - 1)
            output1(NP - 1)

            def float8():
                pe.wait_ge(s["f8_ready"], 1)
                for h in range(2):
                    mm = pe.matmul(ps[:, h, :], kernel8q[:, :], z8[:, h, :], start=True, stop=True)
                mm.then_inc(s["f8_done"], 1)

            pe.wait_ge(s["x_ready"], 4)
            keys8(1, 2, {0: lambda: ln_mean(3), 1: lambda: ln_var(3), 2: lambda: ln_spread(3), 4: float8,
                         5: lambda: ln_mean(4), 6: lambda: ln_var(4), 7: lambda: ln_spread(4),
                         9: lambda: queries8(1, 2, 4), 11: lambda: query_norms8(1)})
            pe.wait_ge(s["norm_qmax"], 2)
            attention8(1, 2)
            pe.wait_ge(s["x_ready"], 6)
            pe.matmul(ps[:, 5, 0:P], stat[:, 0:1].to_broadcast([P, P]), ident[:, :], start=True, stop=True)\
                .then_inc(s["cmean_ready"], 1)
            layernorm(5)
            layernorm(6)
            pe.wait_ge(s["z_ready"], 7)
            for t in range(NT):
                mm = pe.matmul(ps[:, 6, t * E16:t * E16 + E8], tok(z, t), wr2[:, :], start=True, stop=True)
            mm.then_inc(s["g_proj"], 1)
            experts8(1)
            pe.wait_ge(s["hid_ready"], 2 + 2 * E8 * NF)
            for t in range(NT):
                mm = pe.matmul(ps[:, t // 4, (t % 4) * P:(t % 4 + 1) * P],
                               stat[:, 16 + t:17 + t].to_broadcast([P, P]), ident[:, :], start=True, stop=True)
            mm.then_inc(s["sum_ready"], 1)

            pe.wait_ge(s["ccent_ready"], 2)
            for t in range(ST):
                k = P if t < SF else TAIL
                mm = pe.matmul(ps[0:C, 2, 0:C], cn2[0:k, t, :], cn2[0:k, t, :], start=(t == 0), stop=(t == ST - 1))
            mm.then_inc(s["cov_ready"], 1)

            layernorm(7)
            pe.wait_ge(s["cov_copied"], 1)
            pe.wait_ge(s["z_ready"], 8)
            for h in range(2):
                mm = pe.matmul(ps[:, h, :], wT[:, 1, :], z[:, h, :], start=True, stop=True)
            mm.then_inc(s["q3_proj"], 1)
            pe.wait_ge(s["q3_ready"], 1)
            pe.wait_ge(s["in_cols"], 16 * NCOLS)
            for h in range(2):
                mm = pe.matmul(ps[:, 2 + h, :], wk3[:, :], t1[:, h, :], start=True, stop=True)
            mm.then_inc(s["q3_proj"], 1)
            pe.wait_ge(s["q3_ready"], 2)
            for h in range(2):
                pe.matmul(ps[:, h, :], cov[:, :], z[:, h, :], start=True, stop=True)
            for h in range(2):
                mm = pe.matmul(ps[:, 4 + h, :], stat[:, 0:1].to_broadcast([P, P]), z[:, h, :], start=True, stop=True)
            mm.then_inc(s["q3_proj"], 1)
            pe.wait_ge(s["q3_next"], 1)
            pe.matmul(ps[:, 2, 0:1], mean_d[:, :], stat[:, 1:2], start=True, stop=True).then_inc(s["q3_score"], 1)
            for g, (t0, m) in enumerate(VG):
                if g >= 2:
                    pe.wait_ge(s["v3_copied"], g - 1)
                for u in range(m):
                    mm = pe.matmul(ps[:, 6 + g % 2, u * P:(u + 1) * P], ctxT[0:C, (t0 + u) * P:(t0 + u + 1) * P],
                                   wT[0:C, 3, :], start=True, stop=True)
                mm.then_inc(s["v_proj"], 1)
            pe.wait_ge(s["v3_copied"], NVG)
            pe.wait_ge(s["s3_ready"], 1)

            def scores3(bank, r):
                for h in range(2):
                    mm = pe.matmul(ps[:, bank + h, :], cst[:, r, :], z[:, h, :], start=True, stop=True)
                return mm

            def qk3(t, r):
                pe.wait_ge(s["staged"], (t - TILES[3]) * 2 + STAGED[3] + 2)
                pe.wait_ge(s["exp_done"], t - TILES[3] + UNITS[3] + 1)
                scores3(2 * r, r).then_inc(s["scores_ready"], 1)

            def av3(t, r, start, stop):
                pe.wait_ge(s["exp_done"], t - TILES[3] + UNITS[3] + 1 + RING)
                for h in range(2):
                    mm = pe.matmul(ps[:, 6 + h, :], vst[:, r, :], probs[:, r, h * HT:(h + 1) * HT], start=start, stop=stop)
                mm.then_inc(s["av_done"], 1)

            pe.wait_ge(s["b1_prod"], NP + 2)
            for h in range(2):
                mm = pe.matmul(ps[:, h, :], ones_b[:, :], t2b[:, h, :], start=True, stop=True)
            mm.then_inc(s["b1_sum"], 1)
            spread_bound(3)
            mode3 = mode_of(pe, 3)
            with pe.If(mode3 >= 1):
                maxima(3, 0, 2, ST, lambda: scores3(0, 0))
            stream(TILES[3], qk3, av3)
            pe.wait_ge(s["added"], (H + 1) * ST + RING)
            for t in range(NT):
                mm = pe.matmul(ps[:, 0, t:t + 1], tok(t3, t), ones[:, 0:1], start=True, stop=True)
            mm.then_inc(s["den_ready"], 1)
            pe.wait_ge(s["rec_ready"], 2 * NP + 1)
            for t in range(NT):
                mm = pe.matmul(tok(ps[:, 2:4, :], t), ccol[:, 1, t:t + 1].to_broadcast([P, P]), ident[:, :], start=True, stop=True)
            mm.then_inc(s["den8"], 1)
            pe.wait_ge(s["o_done"], SUMS[3] + 3)
            for h in range(2):
                mm = pe.matmul(ps[:, 2 + h, :], wT[:, 2, :], t1[:, h, :], start=True, stop=True)
            mm.then_inc(s["wo_ready"], 1)

            layernorm(8)
            pe.wait_ge(s["z_ready"], 9)
            for t in range(NT):
                mm = pe.matmul(ps[:, 6, t * E16:(t + 1) * E16], tok(z, t), wT[:, 4, 0:E16], start=True, stop=True)
            mm.then_inc(s["g_proj"], 1)
            pe.wait_ge(s["in_shared"], 48)

            def turn16(n, wts, first):
                if not first:
                    pe.wait_ge(s["hg_act"], n)
                for m in range(3):
                    mm = pe.transpose(ps[:, 0, m * P:(m + 1) * P], wts[:, m, :], ident[:, :])
                mm.then_inc(s["wt_turned"], 1)

            def hidden16(n, b, m):
                if m == 0:
                    pe.wait_ge(s["wt_copied"], n + 1)
                for h in range(2):
                    mm = pe.matmul(ps[:, 2 * m + h, :], turned[b][:, m, :], z[:, h, :], start=True, stop=True)
                mm.then_inc(s["hg_ready"], 1)

            def weights16(n, u):
                pe.wait_ge(s["ccol_ready"], n + 2 * E8)
                for h in range(2):
                    mm = pe.matmul(ps[:, 6 + h, :], pick[0:64, u:u + 1].to_broadcast([64, P]), shares[:, h, :],
                                   start=True, stop=True)
                mm.then_inc(s["cb_ready"], 1)

            def output16(n, b, start, stop):
                pe.wait_ge(s["hd_ready"], n + 1)
                for h in range(2):
                    mm = pe.matmul(ps[:, 4 + h, :], turned[b][:, 2, :], t1[:, h, :], start=start, stop=stop)
                mm.then_inc(s["y_ready"], 1)

            def expert16(n, u):
                weights16(n, u)
                hidden16(n + 1, u, 0)
                pe.wait_ge(s["hm_ready"], n)
                hidden16(n + 1, u, 1)
                output16(n, 1 - u, False, False)

            turn16(0, shared, True)
            for m in range(2):
                hidden16(0, 0, m)
            pe.wait_ge(s["ex_w0"], 48)
            turn16(1, ex_w[0], False)
            hidden16(1, 1, 0)
            pe.wait_ge(s["hd_ready"], 1)
            hidden16(1, 1, 1)
            output16(0, 0, True, False)
            pe.wait_ge(s["ex_w1"], 48)
            turn16(2, ex_w[1], False)
            pe.wait_ge(s["comb_ready"], 3)
            for t in range(NT):
                mm = pe.transpose(ps[0:E16, 6 + t // 4, (t % 4) * P:(t % 4 + 1) * P], route[:, 7, t * E16:(t + 1) * E16], ident[:, :])
            mm.then_inc(s["turned"], 1)
            pe.wait_ge(s["w_copied"], 3)
            with pe.Fori(0, E16 // 2 - 1) as i:
                for u in range(2):
                    expert16(i * 2 + u + 1, u)
                    pe.wait_ge(s[f"ex_w{u}"], i * 48 + 96)
                    turn16(i * 2 + u + 3, ex_w[u], False)
            expert16(E16 - 1, 0)
            weights16(E16, 1)
            output16(E16, 0, False, True)

            pe.wait_ge(s["x_ready"], 9)
            for t in range(NT):
                mm = pe.transpose(ps[:, t // 4, (t % 4) * P:(t % 4 + 1) * P], tok(xT, t), ident[:, :])
            mm.then_inc(s["turned"], 1)

        @block.scalar
        def _(act):
            def load_table(k, func):
                act.activation(warm[:, k:k + 1], ones[:, 0:1], func)

            def ln_sq(k):
                for h in range(2):
                    act.wait_ge(s["ln_cent"], 2 * k + h + 1)
                    act.activation(t2[:, h, :], t1[:, h, :], ACT.Square).then_inc(s["ln_sq"], 1)

            def ln_std(k):
                act.wait_ge(s["ln_var"], k + 1)
                act.activation(ccol[:, 0, :], ps[:, 3, 0:NT], ACT.Sqrt, bias=col(EPS)).then_inc(s["ln_std"], 1)

            def layernorm(k):
                ln_sq(k)
                ln_std(k)

            def queries8(n, layer, bias):
                act.wait_ge(s["q_proj"], QPROJ[layer] + 1)
                act.activation(t1, ps[:, 0:2, :], ACT.Identity, bias=col(bias)).then_inc(s["q_split"], 1)
                act.activation(qs[:, 0, :].rearrange("p (h n) -> p h n", h=2).bitcast(F32R), ps[:, 0:2, :], ACT.Identity,
                               bias=col(bias)).then_inc(s["q_split"], 1)
                act.wait_ge(s["q_split"], QSPLIT[layer] + 1)
                act.activation(t2b, t1, ACT.Square, scale=SHRINK).then_inc(s["norm_qsq"], 1)

            def keys8(n, layer, between):
                base = n * NC
                for c, (t0, m) in enumerate(VG):
                    wd = CHUNKS[c][1]
                    act.wait_ge(s["k_proj"], CHUNKED[layer] + c + 1)
                    if stores[n][c]:
                        act.wait_ge(s[f"k_scr{c % 2}"], 16 * stores[n][c])
                    if c >= 2:
                        act.wait_ge(s["k_split"], CHUNKED[layer] + c - 1)
                        act.wait_ge(s["norm_sq"], base + c - 1)
                    act.activation(klo[:, c % 2, 0:wd].bitcast(F32R), ps[:, 6 + c % 2, 0:wd], ACT.Copy).then_inc(s["k_high"], 1)
                    act.wait_ge(s["v_proj"], CHUNKED[layer] + c + 1)
                    act.activation(vx[:, t0:t0 + m, :, 0:HD8],
                                   ps[:, 4 + c % 2, 0:m * P].rearrange("p (t h w) -> p t h w", t=m, h=H),
                                   ACT.Copy).then_inc(s["v_copied"], 1)
                    act.wait_ge(s["k_high"], NC * n + c + 1)
                    if c >= 2:
                        act.wait_ge(s["norm_mm"], base + c - 1)
                    act.activation(t3b[:, c % 2, 0:wd], klo[:, c % 2, 0:wd], ACT.Square, scale=SHRINK)\
                        .then_inc(s["norm_sq"], 1)
                    if c in between:
                        between[c]()

            def exps8(layer):
                mode = mode_of(act, layer)
                with act.If(mode >= 1):
                    exps8_loop(layer, f"shifted{layer}", 0)
                with act.Else():
                    exps8_loop(layer, "scores_ready", UNITS[layer])

            def exps8_loop(layer, ready, base):
                with act.Fori(0, 2 * NG * ST // RING) as i:
                    for r in range(RING):
                        act.wait_ge(s["av_done"], i * RING + r + TILES[layer] + 1)
                        for b in range(2):
                            buf = (2 * r + b) % RING
                            act.wait_ge(s[ready], i * (2 * RING) + 2 * r + b + base + 1)
                            act.activation(probs[:, r, b * T:(b + 1) * T].rearrange("p (h n) -> p h n", h=2),
                                           ps[:, 2 * buf:2 * buf + 2, :], ACT.Exp,
                                           scale=HD8 ** -0.5).then_inc(s["exp_done"], 1)

            def exps1(layer, mode, first, scale):
                with act.If(mode >= 1):
                    exps1_loop(layer, first, scale, f"shifted{layer}", 0)
                with act.Else():
                    exps1_loop(layer, first, scale, "scores_ready", UNITS[layer])

            def exps1_loop(layer, first, scale, ready, base):
                with act.Fori(0, ST // RING) as i:
                    for r in range(RING):
                        local = first + i * RING + r
                        act.wait_ge(s["av_done"], local + TILES[layer] + 1)
                        act.wait_ge(s["added"], local + ADDED[layer] + 1)
                        act.wait_ge(s[ready], local + base + 1)
                        act.activation(probs[:, r, 0:T].rearrange("p (h n) -> p h n", h=2), ps[:, 2 * r:2 * r + 2, :],
                                       ACT.Exp, scale=scale).then_inc(s["exp_done"], 1)

            def experts8(m):
                with act.Fori(0, E8 // 2) as i:
                    for u in range(2):
                        e = i * 2 + u
                        n = e + E8 * m
                        for f in range(NF):
                            if m == 0:
                                act.wait_ge(s["h_ready"], n * NF + f + 1)
                                if f == 0:
                                    act.wait_ge(s["eo_ready"], n + 2)
                                act.activation(hid[:, f, :, :], ps[:, 2 * (f % 2):2 * (f % 2) + 2, :], ACT.Gelu,
                                               bias=b1c[:, 0, bass.ds(e * NF + f, 1)]).then_inc(s["hid_ready"], 1)
                        for h in range(2):
                            act.wait_ge(s["cb_ready"], n * 2 + h + 1)
                            if h == 0:
                                act.wait_ge(s["eo_used"], n + 1)
                            act.activation(t3[:, h, :], ps[:, 6, :], ACT.Copy).then_inc(s["cb_copied"], 1)

            for g in range(1, NVG, 2):
                t0, m = VG[g]
                act.wait_ge(s["ctx_turned"], g + 1)
                act.activation(ctxT[0:C, t0 * P:(t0 + m) * P], ps[0:C, 2 + g % 4, 0:m * P], ACT.Copy)\
                    .then_inc(s["ctx_odd"], 1)

            act.wait_ge(s["in_w0"], 16 * 10)
            keys8(0, 0, {1: lambda: ln_sq(0), 2: lambda: ln_std(0), 5: lambda: queries8(0, 0, BQ0)})
            act.wait_ge(s["sim_ready"], 1)
            act.activation(stat[0:E8, 3:4], stat[0:E8, 2:3], ACT.Sqrt).then_inc(s["sim_root"], 1)
            load_table(0, ACT.Exp)
            exps8(0)
            layernorm(1)
            act.wait_ge(s["g_proj"], 1)
            act.activation(route[:, 0, 0:NT], ps[:, 6, 0:NT * E16].rearrange("p (t e) -> p t e", t=NT)[:, :, E8],
                           ACT.Sqrt).then_inc(s["route_act"], 1)
            act.wait_ge(s["route_in"], 1)
            act.activation(route[:, 2, 0:NT * E8], route[:, 1, 0:NT * E8], ACT.Exp).then_inc(s["route_act"], 1)
            act.wait_ge(s["in_cols"], 16 * NCOLS)
            load_table(1, ACT.Gelu)
            act.wait_ge(s["comb_ready"], 1)
            experts8(0)

            layernorm(2)
            act.wait_ge(s["gram_ready"], 1)
            for e in range(2):
                rows = slice(HD64 * e, HD64 * (e + 1))
                act.activation(gram[rows, :, rows],
                               ps[rows, 6:8, :].rearrange("p a (m n) -> p (a m) n", n=P)[:, :, rows], ACT.Copy)\
                    .then_inc(s["gram_copied"], 1)
            for p in range(NP):
                act.wait_ge(s["b1_q"], p + 1)
                if p >= 2:
                    act.wait_ge(s["b1_prod"], p)
                act.activation((t2b, t3b)[p % 2], ps[:, 2 * (p % 2):2 * (p % 2) + 2, :], ACT.Copy)\
                    .then_inc(s["b1_copied"], 1)
            load_table(2, ACT.Exp)
            mode1 = mode_of(act, 1)

            def keys1(kproj, khigh, count, slot, wd):
                act.wait_ge(s[kproj], count + 1)
                for e in range(2):
                    rows = slice(HD64 * e, HD64 * (e + 1))
                    act.activation(kch[rows, slot, e, 0:wd], ps[rows, 6, 0:wd], ACT.Copy).then_inc(s[khigh], 1)

            def values1(count, slot, m):
                act.wait_ge(s["v_proj"], count + CHUNKED[1] + 1)
                act.activation(vch[:, slot, 0:m * P], ps[:, 7, 0:m * P], ACT.Copy).then_inc(s["v_copied"], 1)

            def exp1(p, c, i, at, ready, base):
                unit = p * PU + c * 8 + i
                back = 1 if at == 0 and i < 2 else 3
                act.wait_ge(s["av_done"], unit + TILES[1] + RING - back)
                act.wait_ge(s["added"], unit + ADDED[1] + RING - back)
                act.wait_ge(s[ready], unit + base + 1)
                act.activation(pr1[:, i % 4], ps[:, 2 * (i % 2):2 * (i % 2) + 2, :], ACT.Exp, scale=HD64 ** -0.5)\
                    .then_inc(s["exp_done"], 1)

            def chunk1(p, c, at, slot, last, ready, base):
                for i in range(2 * VG[at][1]):
                    exp1(p, c, i, at, ready, base)
                    if not last and i == (5 if at == 1 else 3):
                        keys1("k_proj", "k1_high", p * NC + c + 1 + CHUNKED[1], 1 - slot, CHUNKS[at + 1][1])
                    if not last and i == (5 if at == 1 else 3):
                        values1(p * NC + c + 1, 1 - slot, VG[at + 1][1])

            def stream1(p, ready, base):
                chunk1(p, 0, 0, 0, False, ready, base)
                chunk1(p, 1, 1, 1, False, ready, base)
                with act.Fori(0, (NC - 3) // 2 - 1) as i:
                    chunk1(p, i * 2 + 2, 2, 0, False, ready, base)
                    chunk1(p, i * 2 + 3, 3, 1, False, ready, base)
                chunk1(p, NC - 3, NC - 3, 0, False, ready, base)
                chunk1(p, NC - 2, NC - 2, 1, False, ready, base)
                chunk1(p, NC - 1, NC - 1, 0, True, ready, base)

            def sums1(p):
                act.wait_ge(s["av_done"], p * PU + TILES[1] + RING + PU)
                act.wait_ge(s["wo_ready"], p + WOUT[1])
                for e in range(2):
                    act.activation(t1[:, e, :], ps[:, 4 + e, :], ACT.Copy).then_inc(s["acc_copied"], 1)

            def pair1(p, first):
                if not first:
                    sums1(p - 1)
                for e in range(2):
                    act.wait_ge(s["q_proj"], p * 2 + QPROJ[1] + e + 1)
                    act.activation(qp[:, e, 0], ps[:, 2 * e:2 * e + 2, :], ACT.Copy).then_inc(s["q1_high"], 1)
                keys1("k_proj", "k1_high", p * NC + CHUNKED[1], 0, CHUNKS[0][1])
                values1(p * NC, 0, VG[0][1])
                with act.If(mode1 >= 1):
                    with act.Fori(0, NC - 1) as c:
                        keys1("max_kproj", "max_khigh", p * NC + c, 1, HT)
                    keys1("max_kproj", "max_khigh", p * NC + NC - 1, 1, CHUNKS[-1][1])
                    stream1(p, "shifted1", 0)
                with act.Else():
                    stream1(p, "scores_ready", UNITS[1])

            pair1(0, True)
            with act.Fori(1, NP) as p:
                pair1(p, False)
            sums1(NP - 1)

            keys8(1, 2, {0: lambda: ln_sq(3), 1: lambda: ln_std(3), 5: lambda: ln_sq(4), 6: lambda: ln_std(4),
                         9: lambda: queries8(1, 2, BQ2)})
            load_table(3, ACT.Exp)
            exps8(2)
            layernorm(5)
            layernorm(6)
            act.wait_ge(s["route_in"], 2)
            act.activation(route[:, 2, 0:NT * E8], route[:, 1, 0:NT * E8], ACT.Exp).then_inc(s["route_act"], 1)
            experts8(1)

            layernorm(7)
            act.wait_ge(s["s3_ready"], 1)
            act.activation(stat[:, 11:12], stat[:, 10:11], ACT.Sqrt, bias=col(EPS)).then_inc(s["s3_root"], 1)
            for g, (t0, m) in enumerate(VG):
                act.wait_ge(s["v_proj"], (2 + NP) * NVG + g + 1)
                act.activation(vp[:, t0 * P:(t0 + m) * P], ps[:, 6 + g % 2, 0:m * P], ACT.Copy)\
                    .then_inc(s["v3_copied"], 1)
            act.wait_ge(s["s3_ready"], 2)
            load_table(4, ACT.Exp)
            mode3 = mode_of(act, 3)
            exps1(3, mode3, 0, stat[:, 12:13])
            layernorm(8)
            act.wait_ge(s["g_proj"], 3)
            act.activation(route[:, 1, :], ps[:, 6, 0:NT * E16], ACT.Sigmoid).then_inc(s["route_act"], 1)

            def gate(n):
                act.wait_ge(s["hg_ready"], n * 2 + 1)
                act.wait_ge(s["hd_ready"], n)
                act.activation(t2, ps[:, 0:2, :], ACT.Silu).then_inc(s["hg_act"], 1)

            gate(0)
            with act.Fori(1, E16 + 1) as n:
                gate(n)

        @block.gpsimd
        def _(pool):
            done = [0]

            def const(ins):
                done[0] += 1
                ins.then_inc(s["consts_set"], 1)
                pool.wait_ge(s["consts_set"], done[0])

            def diagonal(ap, pattern, base):
                const(pool.affine_select(out=ap, in_=ap, compare_op=ALU.not_equal, fill=1.0, base=base,
                                         pattern=pattern, channel_multiplier=1))

            const(pool.memset(ident[:, :], 0.0))
            diagonal(ident[:, :], [[-1, P]], 0)
            assert done[0] == NIDENT
            const(pool.memset(heads[:, :], 0.0))
            in_head = heads[:, 0:H]
            const(pool.affine_select(out=in_head, in_=in_head, compare_op=ALU.is_gt, fill=1.0, base=0,
                                     pattern=[[HD8, H]], channel_multiplier=-1))
            const(pool.affine_select(out=in_head, in_=in_head, compare_op=ALU.is_gt, fill=0.0, base=HD8,
                                     pattern=[[HD8, H]], channel_multiplier=-1))
            const(pool.memset(mean_d[:, :], 1.0 / D))
            const(pool.memset(cols[:, EPS:EPS + 1], LN_EPS))
            const(pool.memset(ones[:, :], 1.0))
            const(pool.memset(ones_b[:, :], 1.0))
            const(pool.memset(stat[:, :], 0.0))
            const(pool.memset(peak[:, :], 0.0))
            const(pool.memset(bnd[:, :], 0.0))
            const(pool.memset(dsel[:, :], 0.0))
            diagonal(dsel[:, :].rearrange("p (j w) -> p j w", j=G), [[-32, G], [0, 32]], -HD8)
            const(pool.memset(before[:, :, :], 1.0))
            const(pool.affine_select(out=before[:, :, :], in_=before[:, :, :], compare_op=ALU.is_gt, fill=0.0, base=0,
                                     pattern=[[1, E16], [-1, E16]], channel_multiplier=0))
            const(pool.memset(cpeak[:, :], 0.0))
            const(pool.memset(picks[:, :], 0.0))
            diagonal(picks[:, :], [[-1, E16]], 0)
            diagonal(picks[:, :], [[-1, E16]], -32)
            assert done[0] == NCONST
            credits = [("exp_done", RING), ("av_done", RING), ("added", RING), ("acc_copied", 2), ("hid_ready", 2),
                       ("eo_ready", 2), ("x_added", 1), ("cb_copied", 1), ("eo_used", 1), ("moe_acc", 1),
                       ("den_ready", 1), ("max_klow", 1), ("y_ready", 1), ("wt_turned", 1), ("o_done", 2)]
            credits += [(f"{n}{l}", 1) for n in ("max_scores", "max_read", "shift_sub") for l in range(4)]
            for k, (name, count) in enumerate(credits):
                pool.memset(given[:, k:k + 1], 0.0).then_inc(s[name], count)

            def stage_maxima(layer, count, first, out, tile, loads):
                with pool.Fori(0, ST) as t:
                    loads()
                    pool.wait_ge(s["av_done"], first + RING)
                    pool.tensor_copy(out, tile(t)).then_inc(s[f"max_staged{layer}"], 1)
                    pool.wait_ge(s[f"max_scores{layer}"], count * ST + t + 2)

            def stage8(n, layer):
                pool.wait_ge(s["zeros_set"], 6)
                pool.wait_ge(s["v_proj"], CHUNKED[layer] + 1)
                pool.memset(vx[:, 0:SF, :, HD8:HD8 + 1], 1.0).then_inc(s["v_ones"], 1)
                pool.memset(vx[:, SF, :, HD8:HD8 + 1], 0.0).then_inc(s["v_ones"], 1)
                pool.wait_ge(s["v_ones"], 3 * n + 2)
                pool.memset(vx[0:TAIL, SF, :, HD8:HD8 + 1], 1.0).then_inc(s["v_ones"], 1)
                pool.wait_ge(s["v_ones"], 3 * n + 3)
                mode = mode_of(pool, layer)
                with pool.Fori(0, NG // 2) as gi:
                    for par in range(2):
                        g = gi * 2 + par

                        def loads():
                            pool.wait_ge(s["v_copied"], CHUNKED[layer] + NVG)
                            pool.wait_ge(s[f"k_in{par}"], gi * (16 * 2 * G) + 16 * 2 * G * (NG // 2 * n + 1))

                        for half in range(2):
                            with pool.If(mode >= 1):
                                stage_maxima(layer, g * 2 + half, (g * 2 + half) * ST + TILES[layer], kst[:, 0, :],
                                             lambda t: kb[:, par, bass.ds(t * P, P)], loads)
                            with pool.Fori(0, ST // RING) as i:
                                loads()
                                for r in range(RING):
                                    t = i * RING + r
                                    pool.wait_ge(s["av_done"], (g * 2 + half) * ST + t + TILES[layer] + 1)
                                    pool.tensor_copy(kst[:, r, :], kb[:, par, bass.ds(t * P, P)]).then_inc(s["staged"], 1)
                                    pool.tensor_copy(
                                        vst[:, r, :].rearrange("p (j w) -> p j w", j=G)[:, :, 0:HD8 + 1],
                                        vbuf[:, bass.ds(t * (H * (HD8 + 1)) + g * (G * (HD8 + 1)), G * (HD8 + 1))]
                                        .rearrange("p (j w) -> p j w", j=G)).then_inc(s["staged"], 1)

            def weights8(m):
                pool.wait_ge(s["comb_ready"], m + 1)
                with pool.Fori(0, E8 // 2) as i:
                    for u in range(2):
                        n = i * 2 + u + E8 * m
                        pool.wait_ge(s["eo_ready"], n + 1)
                        pool.tensor_copy(ccol[:, u, :],
                                         route[:, 7, 0:NT * E8].rearrange("p (t e) -> p e t", t=NT)[:, bass.ds(i * 2 + u, 1), :]
                                         .rearrange("p o t -> p (o t)")).then_inc(s["ccol_ready"], 1)

            pool.memset(qz[:, :].bitcast(F32), 0.0).then_inc(s["q_zeroed"], 1)
            stage8(0, 0)
            weights8(0)
            pool.wait_ge(s["mode_set"], 2)
            with pool.Fori(0, NP) as p:
                with pool.Fori(0, NC) as c:
                    pool.wait_ge(s["v_proj"], p * NC + CHUNKED[1] + c)
                    pool.tensor_copy(cch[:, :], ctxT[:, bass.ds(c * HT, HT)]).then_inc(s["c_staged"], 1)
            pool.wait_ge(s["av_done"], TILES[2] + RING)
            pool.memset(qz[:, :].bitcast(F32), 0.0).then_inc(s["q_zeroed"], 1)
            stage8(1, 2)
            pool.wait_ge(s["in_ctx2"], 32)
            pool.wait_ge(s["cmean_copied"], 1)
            pool.tensor_tensor(cn2[:, 0:SF, :], cn2[:, 0:SF, :], cmean.unsqueeze(1).to_broadcast([P, SF, C]), ALU.subtract)\
                .then_inc(s["ccent_ready"], 1)
            pool.tensor_tensor(cn2[0:TAIL, SF, :], cn2[0:TAIL, SF, :], cmean[0:TAIL], ALU.subtract).then_inc(s["ccent_ready"], 1)
            weights8(1)
            mode3 = mode_of(pool, 3)
            with pool.If(mode3 >= 1):
                stage_maxima(3, 0, TILES[3], cst[:, 0, :], lambda t: ctxT[:, bass.ds(t * P, P)], lambda: None)
            pool.wait_ge(s["v3_copied"], NVG)
            with pool.Fori(0, ST // RING) as i:
                for r in range(RING):
                    t = i * RING + r
                    pool.wait_ge(s["av_done"], t + TILES[3] + 1)
                    pool.tensor_copy(cst[:, r, :], ctxT[:, bass.ds(t * P, P)]).then_inc(s["staged"], 1)
                    pool.tensor_copy(vst[:, r, :], vp[:, bass.ds(t * P, P)]).then_inc(s["staged"], 1)
            with pool.Fori(0, E16 // 2) as i:
                for u in range(2):
                    n = i * 2 + u + 1
                    pool.wait_ge(s["y_ready"], i * 2 + u + 1)
                    pool.tensor_copy(pick[:, u:u + 1], picks[:, bass.ds(i * 2 + u, 1)]).then_inc(s["ccol_ready"], 1)

        @block.vector
        def _(dve):
            steps = [0]

            def then(ins):
                steps[0] += 1
                ins.then_inc(s["dve_step"], 1)
                dve.wait_ge(s["dve_step"], steps[0])

            def ln_center(k):
                src = z if k == 6 else xT[:, :, :]
                for h in range(2):
                    dve.wait_ge(s["ln_mean"], 2 * k + h + 1)
                    dve.tensor_tensor(t1[:, h, :], src[:, h, :], ps[:, h, :], ALU.subtract).then_inc(s["ln_cent"], 1)

            def ln_rec(k):
                dve.wait_ge(s["ln_std"], k + 1)
                dve.reciprocal(ccol[:, 1, :], ccol[:, 0, :]).then_inc(s["ln_rec"], 1)

            def ln_out(k):
                dve.wait_ge(s["ln_cent"], 2 * k + 2)
                for h in range(2):
                    dve.wait_ge(s["ln_spread"], 2 * k + h + 1)
                    ins = dve.tensor_tensor(z[:, h, :], t1[:, h, :], ps[:, h, :], ALU.mult)
                if k == 6:
                    then(ins)
                    dve.wait_ge(s["in_cols"], 16 * NCOLS)
                    ins = dve.tensor_scalar(z, z, col(GAM), col(BET), ALU.mult, ALU.add)
                ins.then_inc(s["z_ready"], 1)

            def layernorm(k):
                ln_center(k)
                ln_rec(k)
                ln_out(k)

            def best(sc, E, K):
                shape = [P, NT, E, E]
                cmp = flat[:, 0:NT * E * E].rearrange("p (t e f) -> p t e f", t=NT, e=E)
                eq = flat[:, 2048:2048 + NT * E * E].rearrange("p (t e f) -> p t e f", t=NT, e=E)
                other = sc.unsqueeze(2).to_broadcast(shape)
                own = sc.unsqueeze(3).to_broadcast(shape)
                earlier = before[:, 0:E, 0:E].unsqueeze(1).to_broadcast(shape)
                dve.tensor_tensor(cmp, other, own, ALU.is_gt)
                then(dve.tensor_tensor(eq, other, own, ALU.is_equal))
                then(dve.tensor_tensor(eq, eq, earlier, ALU.mult))
                then(dve.tensor_tensor(cmp, cmp, eq, ALU.add))
                rank = route[:, 3, 0:NT * E].rearrange("p (t e) -> p t e", t=NT)
                then(dve.reduce_sum(rank, cmp, AX.X))
                sel = route[:, 4, 0:NT * E].rearrange("p (t e) -> p t e", t=NT)
                then(dve.tensor_scalar(sel, rank, K - 0.5, None, ALU.is_lt))
                return sel

            def r8(n):
                return route[:, n, 0:NT * E8].rearrange("p (t e) -> p t e", t=NT)

            def r16(n):
                return route[:, n, :].rearrange("p (t e) -> p t e", t=NT)

            def per_token(n, e):
                return route[:, 5, n * NT:(n + 1) * NT].unsqueeze(2).to_broadcast([P, NT, e])

            def tokens(n):
                return route[:, 5, n * NT:(n + 1) * NT]

            def set_mode(layer, most):
                dve.wait_ge(s["bound_out"], layer + 1)
                low, odd = stat[:, 20:21], stat[:, 21:22]
                then(dve.reduce_max(stat[:, 22:23], ps[:, 2, 0:P], AX.X))
                if layer == 1:
                    then(dve.reduce_max(cpeak[:, 1:2], ps[:, 2, 2 * P:3 * P], AX.X))
                    then(dve.tensor_tensor(stat[:, 22:23], stat[:, 22:23], cpeak[:, 1:2], ALU.mult))
                then(dve.tensor_scalar(low, stat[:, 22:23], most, -1.0, ALU.is_lt, ALU.mult))
                then(dve.tensor_scalar(odd, ps[:, 2, P:P + 1], 0.0, -2.0, ALU.is_equal, ALU.mult))
                then(dve.tensor_scalar(odd, odd, 2.0, None, ALU.add))
                then(dve.scalar_tensor_tensor(out=low, in0=low, scalar=1.0, in1=odd, op0=ALU.add, op1=ALU.max))
                dve.tensor_copy(cols[:, MODE + layer:MODE + layer + 1].bitcast(I32), low).then_inc(s["mode_set"], 1)

            def tile_max(layer, n, banks, rows, first):
                read = s[f"max_read{layer}"]
                into, scores = top[0:rows, 0:banks, :], ps[0:rows, 0:banks, :]
                dve.wait_ge(s[f"max_scores{layer}"], n + 2)
                if first:
                    dve.tensor_copy(into, scores).then_inc(read, 1)
                else:
                    dve.wait_ge(read, n + 1)
                    dve.tensor_tensor(into, into, scores, ALU.max).then_inc(read, 1)

            def largest(layer, count, banks, most):
                known = s[f"max_known{layer}"]
                into, scores = top[:, 0:banks, :], ps[:, 0:banks, :]
                dve.wait_ge(s[f"max_spread{layer}"], count * 2 + 1)
                dve.reduce_max(topcol[:, 0:4 * banks], scores.rearrange("p b (m n) -> p (b m) n", n=P), AX.X).then_inc(known, 1)
                dve.wait_ge(s[f"max_spread{layer}"], count * 2 + 2)
                dve.tensor_scalar(into, scores, most, None, ALU.min).then_inc(known, 1)

            def maxima(layer, count, banks, units, most):
                dve.wait_ge(s[f"shift_sub{layer}"], count * units + 1)
                tile_max(layer, count * ST, banks, P, True)
                with dve.Fori(1, ST - 1) as t:
                    tile_max(layer, count * ST + t, banks, P, False)
                tile_max(layer, count * ST + ST - 1, banks, TAIL, False)
                largest(layer, count, banks, most)

            def shift(layer, count, unit, scores, largest, least, mode):
                sub = s[f"shift_sub{layer}"]

                def subtract():
                    dve.wait_ge(s[f"max_known{layer}"], count * 2 + 2)
                    dve.wait_ge(s["scores_ready"], unit + UNITS[layer] + 1)
                    dve.scalar_tensor_tensor(out=scores, in0=scores, scalar=least, in1=largest, op0=ALU.max,
                                             op1=ALU.subtract).then_inc(sub, 1)

                if layer == 0:
                    with dve.If(mode == 2):
                        dve.wait_ge(s["scores_ready"], unit + UNITS[layer] + 1)
                        dve.memset(scores, 0.0).then_inc(sub, 1)
                    with dve.Else():
                        subtract()
                else:
                    subtract()
                dve.wait_ge(sub, unit + 2)
                dve.tensor_scalar(scores, scores, 0.0, None, ALU.min).then_inc(s[f"shifted{layer}"], 1)

            for place in (cn[:, SF, :], w8[:, :, :, :], ctxT[C:P, S:], ctxT[0:C, SP:]):
                dve.memset(place, 0.0).then_inc(s["zeros_set"], 1)
            dve.memset(ctxT[C:P, 0:S], 1.0).then_inc(s["zeros_set"], 1)
            dve.wait_ge(s["turned"], 1)
            dve.tensor_copy(xT[:, :, :], ps[:, 0:2, :]).then_inc(s["x_ready"], 1)
            for g in range(0, NVG, 2):
                t0, m = VG[g]
                dve.wait_ge(s["ctx_turned"], g + 1)
                dve.tensor_copy(ctxT[0:C, t0 * P:(t0 + m) * P], ps[0:C, 2 + g % 4, 0:m * P]).then_inc(s["ctx_even"], 1)
            for place in (vst[:, :, :], w64[:, :, :], wk3[:, :], cov[:, :]):
                dve.memset(place, 0.0).then_inc(s["zeros_set"], 1)

            def turn_weights():
                dve.wait_ge(s["in_nat"], 16 * 6)
                dve.wait_ge(s["consts_set"], NCONST)
                then(dve.tensor_tensor(wsq, wn[0:E8, 5, :], wn[0:E8, 5, :], ALU.mult))
                dve.reduce_sum(stat[0:E8, 2:3], wsq, AX.X).then_inc(s["sim_ready"], 1)
                dve.wait_ge(s["sim_root"], 1)
                then(dve.tensor_scalar(stat[0:E8, 3:4], stat[0:E8, 3:4], TINY, None, ALU.max))
                then(dve.reciprocal(stat[0:E8, 3:4], stat[0:E8, 3:4]))
                dve.tensor_scalar(wn[0:E8, 5, :], wn[0:E8, 5, :], stat[0:E8, 3:4], None, ALU.mult).then_inc(s["sim_ready"], 1)
                dve.wait_ge(s["turned"], 2)
                dve.tensor_copy(wT[:, 0:3, :], ps[:, 0, 0:3 * P].rearrange("p (m n) -> p m n", m=3))
                dve.tensor_copy(wT[0:C, 3, :], ps[0:C, 0, 3 * P:4 * P])
                dve.wait_ge(s["turned"], 3)
                dve.tensor_copy(wT[:, 4, 0:E16], ps[:, 1, 0:E16])
                dve.tensor_copy(wT[:, 5, 0:E8], ps[:, 1, E16:E16 + E8]).then_inc(s["w_copied"], 1)

            def context_lengths():
                dve.wait_ge(s["in_piece"], 16 * 3)
                then(dve.memset(lens, 0.0))
                then(dve.tensor_tensor(rest, rest, rest, ALU.mult))
                then(dve.reduce_sum(lens[0:TAIL, SF:ST], rest, AX.X))
                for n, (t0, end) in enumerate(PIECES):
                    if n == 2:
                        dve.wait_ge(s["in_piece"], 16 * 4)
                    then(dve.tensor_tensor(pieces[n], pieces[n], pieces[n], ALU.mult))
                    ins = dve.reduce_sum(lens[:, t0:end], pieces[n], AX.X)
                    ins.then_inc(s["piece_used"], 1)
                dve.wait_ge(s["piece_used"], len(PIECES))
                then(dve.reduce_max(cpeak[:, 0:1], lens, AX.X))
                then(dve.reduce_sum(stat[0:C, 1:2], ctxT[0:C, 0:SP], AX.X))
                then(dve.tensor_scalar(stat[0:C, 0:1], stat[0:C, 1:2], 1.0 / S, None, ALU.mult))

            def queries8(n, layer):
                dve.wait_ge(s["q_split"], QSPLIT[layer] + 2)
                dve.tensor_tensor(qs[:, 1, :].rearrange("p (h n) -> p h n", h=2).bitcast(F32R), t1,
                                  qs[:, 0, :].rearrange("p (h n) -> p h n", h=2), ALU.subtract).then_inc(s["q_split"], 1)

            def query_norms8(n):
                dve.wait_ge(s["norm_qmm"], n + 1)
                dve.reduce_max(peak[0:32, 2 * NC:2 * NC + 1], ps[0:32, 0:2, :], AX.XY)
                dve.reduce_sum(peak[0:32, 2 * NC + 1:2 * NC + 2], ps[0:32, 0:2, :], AX.XY).then_inc(s["norm_qmax"], 1)

            def keys8(n, layer, between):
                base = n * NC

                def norms(c):
                    dve.wait_ge(s["norm_mm"], base + c + 1)
                    dve.reduce_max(peak[0:32, c:c + 1], ps[0:32, 2, 0:CHUNKS[c][1]], AX.X)
                    dve.reduce_sum(peak[0:32, NC + c:NC + c + 1], ps[0:32, 2, 0:CHUNKS[c][1]], AX.X).then_inc(s["norm_max"], 1)

                for c, (c0, wd) in enumerate(CHUNKS):
                    r = c % 2
                    dve.wait_ge(s["k_high"], base + c + 1)
                    if stores[n][c]:
                        dve.wait_ge(s[f"k_scr{r}"], 16 * stores[n][c])
                    dve.tensor_tensor(klo[:, r, HT:HT + wd].bitcast(F32R), ps[:, 6 + r, 0:wd], klo[:, r, 0:wd], ALU.subtract)\
                        .then_inc(s["k_split"], 1)
                    if c:
                        norms(c - 1)
                    if c in between:
                        between[c]()
                norms(NC - 1)
                dve.wait_ge(s["norm_max"], NC * (n + 1))

            def attention8(n, layer, bo):
                far = 2 * NC + 2
                then(dve.reduce_max(peak[0:32, far:far + 1], peak[0:32, 0:NC], AX.X))
                then(dve.tensor_tensor(bnd[0:32, 2 * layer:2 * layer + 1], peak[0:32, far:far + 1], peak[0:32, 2 * NC:2 * NC + 1], ALU.mult))
                then(dve.reduce_sum(peak[0:32, far + 1:far + 2], peak[0:32, NC:2 * NC], AX.X))
                then(dve.tensor_tensor(peak[0:32, far + 1:far + 2], peak[0:32, far + 1:far + 2], peak[0:32, 2 * NC + 1:2 * NC + 2], ALU.add))
                dve.tensor_scalar(bnd[0:32, 2 * layer + 1:2 * layer + 2], peak[0:32, far + 1:far + 2], 0.0, None, ALU.mult)\
                    .then_inc(s["bound_in"], 1)
                set_mode(layer, LIMIT ** 2 * HD8 * SHRINK ** 4)
                if n == 0:
                    context_lengths()
                mode = mode_of(dve, layer)
                rec = qs[:, 0, 0:HT]

                def normalise8(gh, half):
                    dve.wait_ge(s["den8"], gh + 2 * NG * n + 1)
                    dve.reciprocal(rec, ps[:, 6 + half, :]).then_inc(s["rec8"], 1)
                    dve.wait_ge(s["rec8"], gh + 2 * NG * n + 1)
                    values = sums[:, bass.ds(gh, 1), :].rearrange("p o n -> p (o n)")
                    dve.tensor_tensor(values, values, rec, ALU.mult).then_inc(s["o_done"], 1)

                assert NG // 2 == 2
                with dve.Fori(0, NG // 2) as gi:
                    for par, half in ((0, 0), (0, 1), (1, 0), (1, 1)):
                        g = gi * 2 + par
                        with dve.If(mode >= 1):
                            maxima(layer, g * 2 + half, G, 2 * ST, CLIP if layer == 0 else HUGE)
                            with dve.Fori(0, 2 * ST // (2 * RING)) as i:
                                for k in range(2 * RING):
                                    buf = k % RING
                                    shift(layer, g * 2 + half, (g * 2 + half) * (2 * ST) + i * (2 * RING) + k,
                                          ps[:, 2 * buf:2 * buf + 2, :], top[:, 2 * (k % 2):2 * (k % 2) + 2, :],
                                          -CLIP if layer == 0 else -HUGE, mode)
                        if half:
                            normalise8(g * 2, 0)
                        elif par:
                            normalise8(gi * 4 + 1, 1)
                        else:
                            with dve.If(gi >= 1):
                                normalise8(3, 1)
                        dve.wait_ge(s["av_done"], (g * 2 + half) * ST + TILES[layer] + RING + ST)
                        dve.tensor_copy(sums[:, bass.ds(g * 2 + half, 1), :], ps[:, 6 + half:7 + half, :])\
                            .then_inc(s["acc_copied"], 1)
                normalise8(2 * NG - 1, 1)
                dve.wait_ge(s["wo_ready"], WOUT[layer] + 1)
                dve.wait_ge(s["in_cols"], 16 * NCOLS)
                dve.scalar_tensor_tensor(out=xT[:, :, :], in0=ps[:, 4:6, :], scalar=col(bo), in1=xT[:, :, :],
                                         op0=ALU.add, op1=ALU.add).then_inc(s["x_ready"], 1)

            def experts8(m):
                then(dve.memset(t2, 0.0))
                with dve.Fori(0, E8 // 2) as i:
                    for u in range(2):
                        e = i * 2 + u
                        n = e + E8 * m
                        if m == 1:
                            for f in range(NF):
                                dve.wait_ge(s["h_ready"], n * NF + f + 1)
                                if f == 0:
                                    dve.wait_ge(s["eo_ready"], n + 2)
                                dve.tensor_scalar(hid[:, f, :, :], ps[:, 2 * (f % 2):2 * (f % 2) + 2, :],
                                                  rb1[:, 1, bass.ds(e * NF + f, 1)], rb1[:, 2, bass.ds(e * NF + f, 1)],
                                                  ALU.add, ALU.max).then_inc(s["hid_ready"], 1)
                        dve.wait_ge(s["moe_acc"], n + 1)
                        dve.wait_ge(s["eo_ready"], n + 3)
                        dve.wait_ge(s["cb_copied"], n * 2 + 3)
                        if m == 0:
                            dve.scalar_tensor_tensor(out=t1, in0=ps[:, 4:6, :], scalar=b2c[:, 0, bass.ds(e, 1)], in1=t3,
                                                     op0=ALU.add, op1=ALU.mult).then_inc(s["eo_used"], 1)
                        else:
                            dve.tensor_tensor(t1, ps[:, 4:6, :], t3, ALU.mult).then_inc(s["eo_used"], 1)
                        dve.wait_ge(s["eo_used"], n + 2)
                        dve.tensor_tensor(t2, t2, t1, ALU.add).then_inc(s["moe_acc"], 1)
                dve.wait_ge(s["moe_acc"], E8 * (m + 1) + 1)

            def sums_of(layer, first, count, mode):
                with dve.If(mode >= 1):
                    maxima(layer, count, 2, ST, HUGE)
                    sums_loop(layer, first, count, mode, True)
                with dve.Else():
                    sums_loop(layer, first, count, mode, False)

            def sums_loop(layer, first, count, mode, general):
                def add(local, r, t):
                    if general:
                        shift(layer, count, local, ps[:, 2 * r:2 * r + 2, :], top[:, 0:2, :], -HUGE, mode)
                    dve.wait_ge(s["exp_done"], local + UNITS[layer] + RING + 1)
                    k = TAIL if t == ST - 1 else P
                    e = probs[0:k, r, 0:T].rearrange("p (h n) -> p h n", h=2)
                    if t == 0:
                        dve.wait_ge(s["den_ready"], count + 1)
                        dve.tensor_copy(t3, e).then_inc(s["added"], 1)
                    else:
                        dve.wait_ge(s["added"], local + ADDED[layer] + RING)
                        dve.tensor_tensor(t3[0:k], t3[0:k], e, ALU.add).then_inc(s["added"], 1)

                for t in range(RING):
                    add(first + t, t, t)
                with dve.Fori(0, ST // RING - 2) as i:
                    for r in range(RING):
                        add(first + i * RING + RING + r, r, RING)
                for t in range(ST - RING, ST):
                    add(first + t, t % RING, t)

            keys8(0, 0, {1: lambda: ln_center(0), 2: lambda: ln_rec(0), 3: lambda: ln_out(0), 5: lambda: queries8(0, 0),
                         7: lambda: query_norms8(0)})
            dve.wait_ge(s["norm_qmax"], 1)
            turn_weights()
            attention8(0, 0, BO0)
            layernorm(1)
            dve.wait_ge(s["p_proj"], 1)
            then(dve.tensor_copy(t1, ps[:, 0:2, :]))
            dve.tensor_tensor(t2, t1, t1, ALU.mult).then_inc(s["p_ready"], 1)
            then(dve.reciprocal(stat[:, 4:5], col(TEMP)))
            dve.wait_ge(s["route_act"], 1)
            then(dve.tensor_scalar(tokens(0), route[:, 0, 0:NT], TINY, None, ALU.max))
            then(dve.reciprocal(tokens(0), tokens(0)))
            dots = ps[:, 6, 0:NT * E16].rearrange("p (t e) -> p t e", t=NT)[:, :, 0:E8]
            then(dve.tensor_tensor(r8(0), dots, per_token(0, E8), ALU.mult))
            then(dve.tensor_scalar(r8(0), r8(0), stat[:, 4:5], None, ALU.mult))
            then(dve.reduce_max(tokens(1), r8(0), AX.X))
            dve.tensor_tensor(r8(1), r8(0), per_token(1, E8), ALU.subtract).then_inc(s["route_in"], 1)
            sel = best(r8(0), E8, 2)
            dve.wait_ge(s["route_act"], 2)
            then(dve.tensor_tensor(r8(2), r8(2), sel, ALU.mult))
            then(dve.reduce_sum(tokens(2), r8(2), AX.X))
            then(dve.reciprocal(tokens(2), tokens(2)))
            dve.tensor_tensor(r8(7), r8(2), per_token(2, E8), ALU.mult).then_inc(s["comb_ready"], 1)
            experts8(0)
            dve.tensor_tensor(xT[:, :, :], xT[:, :, :], t2, ALU.add).then_inc(s["x_ready"], 1)

            layernorm(2)
            dve.wait_ge(s["in_qk1"], 32)
            dve.memset(gram[0:HD64, :, HD64:P], 0.0)
            dve.memset(gram[HD64:P, :, 0:HD64], 0.0).then_inc(s["b1_prod"], 1)
            for p in range(NP + 1):
                if p < NP:
                    dve.wait_ge(s["b1_r"], p + 1)
                    if p >= 2:
                        dve.wait_ge(s["b1_sum"], p - 1)
                    dve.tensor_tensor(t1r[:, p % 2], ps[:, 4:6, :], (t2b, t3b)[p % 2], ALU.mult).then_inc(s["b1_prod"], 1)
                if p:
                    dve.wait_ge(s["b1_sum"], p)
                    dve.reduce_max(peak[:, p - 1:p], ps[:, 6:8, :], AX.XY).then_inc(s["b1_max"], 1)
            dve.wait_ge(s["b1_max"], NP)
            then(dve.reduce_max(stat[:, 19:20], peak[:, 0:NP], AX.X))
            dve.tensor_copy(bnd[:, 2:3], stat[:, 19:20]).then_inc(s["bound_in"], 1)
            set_mode(1, LIMIT ** 2 * HD64)
            mode1 = mode_of(dve, 1)

            def low_keys1(khigh, high_count, klow, slot, wd):
                dve.wait_ge(s[khigh], high_count + 2)
                for e in range(2):
                    rows, other = slice(HD64 * e, HD64 * (e + 1)), slice(HD64 * (1 - e), HD64 * (2 - e))
                    ins = dve.tensor_tensor(kch[other, slot, e, 0:wd], ps[rows, 6, 0:wd], kch[rows, slot, e, 0:wd].bitcast(F32),
                                            ALU.subtract)
                ins.then_inc(s[klow], 1)

            def add1(p, c, i, at, last, general):
                unit = p * PU + c * 8 + i
                e = i % 2
                if general:
                    shift(1, p, unit, ps[:, 2 * e:2 * e + 2, :], top[:, 2 * e:2 * e + 2, :], -HUGE, mode1)
                dve.wait_ge(s["exp_done"], unit + UNITS[1] + RING + 1)
                k = TAIL if last and i >= 2 * VG[at][1] - 2 else P
                if at == 0 and i < 2:
                    dve.wait_ge(s["den_ready"], p * 2 + 1)
                    dve.tensor_copy(sum1[:, e], pr1[:, i % 4]).then_inc(s["added"], 1)
                else:
                    dve.wait_ge(s["added"], unit + ADDED[1] + RING - 1)
                    dve.tensor_tensor(sum1[0:k, e], sum1[0:k, e], pr1[0:k, i % 4], ALU.add).then_inc(s["added"], 1)

            def chunk1(p, c, at, slot, last, general, first):
                for i in range(2 * VG[at][1]):
                    add1(p, c, i, at, last, general)
                    if at == 0 and i in (1, 4) and not first:
                        normalise1(p - 1, i // 4)
                    if at == 1 and i == 1 and not first:
                        output1(p - 1)
                    if not last and i == (5 if at == 1 else 3):
                        low_keys1("k1_high", (p * NC + c + 1) * 2, "k_split", 1 - slot, CHUNKS[at + 1][1])

            def stream1(p, general, first):
                chunk1(p, 0, 0, 0, False, general, first)
                chunk1(p, 1, 1, 1, False, general, first)
                with dve.Fori(0, (NC - 3) // 2 - 1) as i:
                    chunk1(p, i * 2 + 2, 2, 0, False, general, first)
                    chunk1(p, i * 2 + 3, 3, 1, False, general, first)
                chunk1(p, NC - 3, NC - 3, 0, False, general, first)
                chunk1(p, NC - 2, NC - 2, 1, False, general, first)
                chunk1(p, NC - 1, NC - 1, 0, True, general, first)

            def denominators1(p):
                dve.wait_ge(s["den_ready"], p * 2 + 3)
                dve.tensor_copy(t2, ps[:, 4:6, :]).then_inc(s["den_copied"], 1)

            def normalise1(p, e):
                dve.wait_ge(s["den_copied"], p + 1)
                dve.reciprocal(t2[:, e, :], t2[:, e, :]).then_inc(s["rec_ready"], 1)
                dve.wait_ge(s["rec_ready"], p * 2 + e + 1)
                dve.wait_ge(s["acc_copied"], p * 2 + SUMS[1] + 2 + e + 1)
                dve.tensor_tensor(t1[:, e, :], t1[:, e, :], t2[:, e, :], ALU.mult).then_inc(s["o_done"], 1)

            def output1(p):
                dve.wait_ge(s["wo_ready"], p + WOUT[1] + 1)
                dve.wait_ge(s["x_added"], p + 1)
                dve.tensor_tensor(xT[:, :, :], xT[:, :, :], ps[:, 6:8, :], ALU.add).then_inc(s["x_added"], 1)

            def maxima1(p):
                def chunk(c, at, first):
                    low_keys1("max_khigh", (p * NC + c) * 2, "max_klow", 1, CHUNKS[at][1])
                    for u in range(VG[at][1]):
                        rows = TAIL if at == NC - 1 and u == VG[at][1] - 1 else P
                        tile_max(1, p * ST + c * 4 + u, 4, rows, first and u == 0)

                dve.wait_ge(s["shift_sub1"], p * PU + 1)
                chunk(0, 0, True)
                with dve.Fori(1, NC - 1) as c:
                    chunk(c, 1, False)
                chunk(NC - 1, NC - 1, False)
                largest(1, p, 4, HUGE)

            def pair1(p, first):
                for e in range(2):
                    dve.wait_ge(s["q1_high"], p * 2 + e + 1)
                    dve.tensor_tensor(qp[:, e, 1], ps[:, 2 * e:2 * e + 2, :], qp[:, e, 0].bitcast(F32), ALU.subtract)\
                        .then_inc(s["q_split"], 2)
                if first:
                    kernel_to_float8()
                low_keys1("k1_high", p * (2 * NC), "k_split", 0, CHUNKS[0][1])
                if not first:
                    denominators1(p - 1)
                with dve.If(mode1 >= 1):
                    maxima1(p)
                    stream1(p, True, first)
                with dve.Else():
                    stream1(p, False, first)

            def to_float8(out, v, scale, a, b):
                then(dve.tensor_scalar(a, v, scale, None, ALU.mult))
                then(dve.tensor_scalar(b.bitcast(I32), a.bitcast(I32), 0x7F800000, None, ALU.bitwise_and))
                then(dve.tensor_scalar(b, b, 2.0 ** -6, 1.5 * 2.0 ** 20, ALU.max, ALU.mult))
                then(dve.tensor_tensor(a, a, b, ALU.add))
                then(dve.tensor_tensor(a, a, b, ALU.subtract))
                then(dve.tensor_tensor(b, a, a, ALU.mult))
                then(dve.tensor_scalar(b, b, FP8_MAX ** 2, 3e38, ALU.is_gt, ALU.mult))
                then(dve.tensor_scalar(b, b, 3e38, None, ALU.mult))
                then(dve.tensor_tensor(b, b, b, ALU.subtract))
                return dve.tensor_tensor(out, a, b, ALU.add)

            def kernel_to_float8():
                then(dve.reciprocal(stat[:, 5:6], col(SIN)))
                then(dve.reciprocal(stat[:, 6:7], col(SK)))
                then(dve.tensor_tensor(stat[:, 7:8], col(SIN), col(SK), ALU.mult))
                then(to_float8(kernel8q[:, :], kernel8[:, :], stat[:, 6:7], t1[:, 0, 0:P], t2[:, 0, 0:P]))

            pair1(0, True)
            with dve.Fori(1, NP) as p:
                pair1(p, False)
            denominators1(NP - 1)
            for e in range(2):
                normalise1(NP - 1, e)
            output1(NP - 1)
            dve.wait_ge(s["x_added"], NP + 1)
            dve.tensor_scalar(xT[:, :, :], xT[:, :, :], col(BO1), None, ALU.add).then_inc(s["x_ready"], 1)

            def operands8():
                dve.wait_ge(s["z_ready"], 4)
                then(dve.tensor_copy(z8[:, :, :], z))
                to_float8(z8[:, :, :], z8[:, :, :], stat[:, 5:6], t1, t2).then_inc(s["f8_ready"], 1)

            def output8():
                dve.wait_ge(s["f8_done"], 1)
                then(dve.tensor_scalar(z8[:, :, :], ps[:, 0:2, :], stat[:, 7:8], None, ALU.mult))
                then(dve.tensor_scalar(z8[:, :, :], z8[:, :, :], bias8[:, 0:1], None, ALU.add))
                dve.tensor_tensor(xT[:, :, :], xT[:, :, :], z8[:, :, :], ALU.add).then_inc(s["x_ready"], 1)

            def out3():
                ln_out(3)
                operands8()

            keys8(1, 2, {0: lambda: ln_center(3), 1: lambda: ln_rec(3), 2: out3, 4: output8,
                         5: lambda: ln_center(4), 6: lambda: ln_rec(4), 7: lambda: ln_out(4),
                         9: lambda: queries8(1, 2), 11: lambda: query_norms8(1)})
            dve.wait_ge(s["norm_qmax"], 2)
            attention8(1, 2, BO2)
            dve.wait_ge(s["cmean_ready"], 1)
            dve.tensor_copy(cmean, ps[:, 5, 0:C]).then_inc(s["cmean_copied"], 1)
            layernorm(5)
            dve.wait_ge(s["z_ready"], 6)
            then(dve.tensor_tensor(xT[:, :, :], xT[:, :, :], z, ALU.add))
            then(dve.tensor_scalar(rb1[:, 0, :], b1c[:, 1, :], 0.0, None, ALU.max))
            dve.tensor_tensor(rb1[:, 1, :], b1c[:, 1, :], rb1[:, 0, :], ALU.subtract)
            then(dve.tensor_scalar(rb1[:, 2, :], rb1[:, 0, :], -1.0, None, ALU.mult))
            then(dve.reduce_sum(stat[:, 24:25], b2c[:, 1, :], AX.X))
            layernorm(6)
            dve.wait_ge(s["g_proj"], 2)
            logits = ps[:, 6, 0:NT * E16].rearrange("p (t e) -> p t e", t=NT)[:, :, 0:E8]
            then(dve.tensor_tensor(r8(0), logits, brow[:, :].unsqueeze(1).to_broadcast([P, NT, E8]), ALU.add))
            then(dve.reduce_max(tokens(1), r8(0), AX.X))
            dve.tensor_tensor(r8(1), r8(0), per_token(1, E8), ALU.subtract).then_inc(s["route_in"], 1)
            dve.wait_ge(s["route_act"], 3)
            then(dve.reduce_sum(tokens(2), r8(2), AX.X))
            then(dve.reciprocal(tokens(2), tokens(2)))
            then(dve.tensor_tensor(r8(6), r8(2), per_token(2, E8), ALU.mult))
            sel = best(r8(6), E8, 2)
            then(dve.tensor_tensor(r8(7), r8(6), sel, ALU.mult))
            then(dve.reduce_sum(stat[:, 16:16 + NT], r8(7), AX.X))
            dve.memset(stat[:, 13:14], 0.0).then_inc(s["rb_ready"], 1)
            dve.memset(stat[:, 29:30], 0.0).then_inc(s["comb_ready"], 1)
            experts8(1)
            dve.wait_ge(s["sum_ready"], 1)
            then(dve.reduce_sum(stat[:, 25:26], ps[:, 7, 0:E8], AX.X))
            then(dve.tensor_tensor(stat[:, 25:26], stat[:, 25:26], stat[:, 24:25], ALU.add))
            then(dve.scalar_tensor_tensor(out=t2, in0=ps[:, 0:2, :], scalar=stat[:, 25:26], in1=t2, op0=ALU.mult, op1=ALU.add))
            dve.tensor_tensor(xT[:, :, :], xT[:, :, :], t2, ALU.add).then_inc(s["x_ready"], 1)

            dve.wait_ge(s["cov_ready"], 1)
            dve.tensor_scalar(cov[0:C, 0:C], ps[0:C, 2, 0:C], 1.0 / S, None, ALU.mult).then_inc(s["cov_copied"], 1)
            layernorm(7)
            dve.wait_ge(s["q3_proj"], 1)
            dve.tensor_copy(t1, ps[:, 0:2, :]).then_inc(s["q3_ready"], 1)
            dve.wait_ge(s["q3_proj"], 2)
            dve.tensor_copy(z, ps[:, 2:4, :]).then_inc(s["q3_ready"], 1)
            dve.wait_ge(s["q3_ready"], 2)
            dve.wait_ge(s["q3_proj"], 3)
            then(dve.tensor_tensor(t2, ps[:, 0:2, :], z, ALU.mult))
            dve.reduce_sum(stat[:, 1:2], t2, AX.XY).then_inc(s["q3_next"], 1)
            then(dve.reduce_sum(stat[:, 8:9], ps[:, 4:6, :], AX.XY))
            then(dve.tensor_scalar(stat[:, 8:9], stat[:, 8:9], 1.0 / T, None, ALU.mult))
            then(dve.tensor_scalar(t2, ps[:, 4:6, :], stat[:, 8:9], None, ALU.subtract))
            then(dve.tensor_tensor(t2, t2, t2, ALU.mult))
            then(dve.reduce_sum(stat[:, 9:10], t2, AX.XY))
            then(dve.tensor_scalar(stat[:, 9:10], stat[:, 9:10], 1.0 / T, None, ALU.mult))
            dve.wait_ge(s["q3_score"], 1)
            dve.scalar_tensor_tensor(out=stat[:, 10:11], in0=ps[:, 2, 0:1], scalar=D / T, in1=stat[:, 9:10],
                                     op0=ALU.mult, op1=ALU.add).then_inc(s["s3_ready"], 1)
            dve.wait_ge(s["s3_root"], 1)
            dve.reciprocal(stat[:, 12:13], stat[:, 11:12]).then_inc(s["s3_ready"], 1)
            dve.tensor_tensor(t2b, z, z, ALU.mult).then_inc(s["b1_prod"], 1)
            dve.wait_ge(s["b1_sum"], NP + 1)
            then(dve.reduce_max(stat[:, 19:20], ps[:, 0:2, :], AX.XY))
            then(dve.tensor_tensor(stat[:, 18:19], stat[:, 12:13], stat[:, 12:13], ALU.mult))
            then(dve.tensor_tensor(stat[:, 18:19], stat[:, 18:19], cpeak[:, 1:2], ALU.mult))
            dve.tensor_tensor(bnd[:, 6:7], stat[:, 19:20], stat[:, 18:19], ALU.mult).then_inc(s["bound_in"], 1)
            set_mode(3, LIMIT ** 2)
            mode3 = mode_of(dve, 3)
            sums_of(3, 0, 0, mode3)
            dve.wait_ge(s["den_ready"], H + 2)
            dve.reciprocal(ccol[:, 1, :], ps[:, 0, 0:NT]).then_inc(s["rec_ready"], 1)
            dve.wait_ge(s["av_done"], TILES[3] + RING + ST)
            then(dve.tensor_copy(t1, ps[:, 6:8, :]))
            dve.wait_ge(s["den8"], 4 * NG + 1)
            dve.tensor_tensor(t1, t1, ps[:, 2:4, :], ALU.mult).then_inc(s["o_done"], 1)
            dve.wait_ge(s["wo_ready"], WOUT[3] + 1)
            dve.tensor_tensor(xT[:, :, :], xT[:, :, :], ps[:, 2:4, :], ALU.add).then_inc(s["x_ready"], 1)

            layernorm(8)

            def turned16(n, b):
                dve.wait_ge(s["wt_turned"], n + 2)
                dve.wait_ge(s["y_ready"], n)
                dve.tensor_copy(turned[b][:, :, :], ps[:, 0, 0:3 * P].rearrange("p (m n) -> p m n", m=3)).then_inc(s["wt_copied"], 1)

            def expert16(n, gated):
                dve.wait_ge(s["hg_act"], n + 1)
                dve.wait_ge(s["hg_ready"], n * 2 + 2)
                dve.wait_ge(s["y_ready"], n + 1)
                if gated:
                    dve.tensor_tensor(t1, t2, ps[:, 2:4, :], ALU.mult).then_inc(s["hm_ready"], 1)
                    dve.wait_ge(s["hm_ready"], n)
                    dve.wait_ge(s["cb_ready"], n + 4 * E8)
                    dve.tensor_tensor(t1, t1, ps[:, 6:8, :], ALU.mult).then_inc(s["hd_ready"], 1)
                else:
                    dve.tensor_tensor(t1, t2, ps[:, 2:4, :], ALU.mult).then_inc(s["hd_ready"], 1)

            dve.wait_ge(s["wt_turned"], 2)
            dve.tensor_copy(turned[0][:, :, :], ps[:, 0, 0:3 * P].rearrange("p (m n) -> p m n", m=3)).then_inc(s["wt_copied"], 1)
            dve.wait_ge(s["route_act"], 4)
            then(dve.tensor_tensor(r16(0), r16(1), ebrow[:, :].unsqueeze(1).to_broadcast([P, NT, E16]), ALU.add))
            sel = best(r16(0), E16, 8)
            turned16(1, 1)
            expert16(0, False)
            then(dve.tensor_tensor(r16(2), r16(1), sel, ALU.mult))
            then(dve.reduce_sum(tokens(2), r16(2), AX.X))
            then(dve.reciprocal(tokens(2), tokens(2)))
            then(dve.tensor_tensor(r16(2), r16(2), per_token(2, E16), ALU.mult))
            dve.tensor_scalar(r16(7), r16(2), ROUTE_SCALE, None, ALU.mult).then_inc(s["comb_ready"], 1)
            dve.wait_ge(s["turned"], 4)
            dve.tensor_copy(shares[0:E16], ps[0:E16, 6:8, :]).then_inc(s["w_copied"], 1)
            dve.wait_ge(s["w_copied"], 2)
            dve.tensor_tensor(shares[32:32 + E16], ps[0:E16, 6:8, :], shares[0:E16].bitcast(F32), ALU.subtract)\
                .then_inc(s["w_copied"], 1)

            with dve.Fori(0, E16 // 2 - 1) as i:
                for u in range(2):
                    turned16(i * 2 + u + 2, u)
                    expert16(i * 2 + u + 1, True)
            turned16(E16, 0)
            expert16(E16 - 1, True)
            expert16(E16, True)
            dve.wait_ge(s["y_ready"], E16 + 2)
            dve.tensor_tensor(xT[:, :, :], xT[:, :, :], ps[:, 4:6, :], ALU.add).then_inc(s["x_ready"], 1)
            dve.wait_ge(s["turned"], 5)
            dve.tensor_copy(probs[:, 0, 0:T].rearrange("p (h n) -> p h n", h=2), ps[:, 0:2, :]).then_inc(s["out_ready"], 1)

        @block.sync
        def _(sp):
            x_rows = a["x"].rearrange("o (p t) d -> (o p) t d", t=NT)
            rows = a["ctx_768"].rearrange("o s c -> (o s) c")
            half = VG[NVG // 2][0]
            whole = rows[0:SF * P, :].rearrange("(p t) c -> p t c", t=SF)
            sp.dma_start(xn, x_rows).then_inc(s["in_x"], 16)
            sp.dma_start(cn[:, 0:half, :], whole[:, 0:half, :]).then_inc(s["in_ctx0"], 16)
            sp.dma_start(cn[:, half:SF, :], whole[:, half:SF, :]).then_inc(s["in_ctx1"], 16)
            sp.wait_ge(s["zeros_set"], 2)
            sp.dma_start(cn[0:TAIL, SF, :], rows[SF * P:S, :]).then_inc(s["in_ctx1"], 16)

            def weights8(n, l, bias):
                into = s["in_w2" if n else "in_w0"]
                for m, (w, b) in enumerate((("Wk", "bk"), ("Wv", "bv"))):
                    sp.dma_start(w8[0:C, n, 1 + m, :], a[l + w]).then_inc(into, 16)
                    sp.dma_start(w8[C:C + 1, n, 1 + m, :], a[l + b].rearrange("(o n) -> o n", o=1)).then_inc(into, 16)
                sp.dma_start(w8[:, n, 0, :], a[l + "Wq"]).then_inc(into, 16)
                sp.dma_start(col(bias), a[l + "bq"].rearrange("(p o) -> p o", o=1)).then_inc(into, 16)
                for j in range(G):
                    sp.dma_start(w8[32 * j:32 * j + HD8, n, 3:3 + NG, :],
                                 a[l + "Wo"].rearrange("(g j d) n -> d j g n", g=NG, j=G)[:, j]).then_inc(into, 16)

            weights8(0, "L0_xattn_", BQ0)
            for m, (name, n, w) in enumerate((("L0_ffn_Wp", P, P), ("L3_xattn_Wq", P, P), ("L3_xattn_Wo", P, P),
                                              ("L3_xattn_Wv", P, C), ("L3_ffn_gate_w", E16, P),
                                              ("L0_ffn_sim_matrix", E8, P))):
                sp.dma_start(wn[0:n, m, 0:w], a[name]).then_inc(s["in_nat"], 16)

            def context_pieces():
                sp.wait_ge(s["norm_mm"], NC)
                sp.dma_start(rest, rows[SF * P:S, :]).then_inc(s["in_piece"], 16)
                for n, (t0, end) in enumerate(PIECES):
                    if n == 2:
                        sp.wait_ge(s["piece_used"], 1)
                    sp.dma_start(pieces[n], whole[:, t0:end, :]).then_inc(s["in_piece"], 16)

            def later_loads():
                weights8(1, "L2_xattn_", BQ2)
                sp.wait_ge(s["zeros_set"], 9)
                sp.dma_start(wk3[:, 0:C], a["L3_xattn_Wk"]).then_inc(s["in_cols"], 16)
                for n, name in ((BO0, "L0_xattn_bo"), (BO2, "L2_xattn_bo"), (BO1, "L1_xattn_bo"), (GAM, "L2_ffn_gamma"),
                                (BET, "L2_ffn_beta")):
                    sp.dma_start(col(n), a[name].rearrange("(p o) -> p o", o=1)).then_inc(s["in_cols"], 16)
                for n, name in ((TEMP, "L0_ffn_temperature"), (SIN, "L1_ffn_input_scale"), (SK, "L1_ffn_kernel_scale")):
                    sp.dma_start(col(n), a[name].rearrange("(p o) -> p o", o=1).to_broadcast([P, 1])).then_inc(s["in_cols"], 16)
                sp.dma_start(bias8[:, :], a["L1_ffn_bias"].rearrange("(p o) -> p o", o=1)).then_inc(s["in_cols"], 16)
                sp.dma_start(kernel8[:, :], a["L1_ffn_kernel"]).then_inc(s["in_cols"], 16)
                sp.dma_start(wr2[:, :], a["L2_ffn_Wr"]).then_inc(s["in_cols"], 16)
                sp.dma_start(brow[:, :], a["L2_ffn_br"].rearrange("(o e) -> o e", o=1).to_broadcast([P, E8])).then_inc(s["in_cols"], 16)
                sp.dma_start(ebrow[:, :], a["L3_ffn_expert_bias"].rearrange("(o e) -> o e", o=1).to_broadcast([P, E16]))\
                    .then_inc(s["in_cols"], 16)
                for m, l in enumerate(("L0", "L2")):
                    sp.dma_start(b1c[:, m, :].rearrange("p (e f) -> p e f", f=NF),
                                 a[l + "_ffn_b1"].rearrange("e (f p) -> p e f", p=P), allow_slow_non_contiguous=True).then_inc(s["in_cols"], 16)
                    sp.dma_start(b2c[:, m, :], a[l + "_ffn_b2"].rearrange("e d -> d e"), allow_slow_non_contiguous=True).then_inc(s["in_cols"], 16)

            def attention8(n, layer):
                for c, (c0, wd) in enumerate(CHUNKS):
                    sp.wait_ge(s["k_split"], CHUNKED[layer] + c + 1)
                    sp.dma_start(kscr[n].rearrange("l p n -> p l n")[:, :, c0:c0 + wd],
                                 klo[:, c % 2, :].rearrange("p (l n) -> p l n", l=2)[:, :, 0:wd])\
                        .then_inc(s[f"k_scr{c % 2}"], 16)
                    if c == (10 if n else 6):
                        sp.wait_ge(s["q_split"], QSPLIT[layer] + 3)
                        sp.dma_start(qscr[n].rearrange("l p n -> p l n"), qs[:, :, :]).then_inc(s["q_scr"], 16)
                sp.wait_ge(s["k_scr0"], 16 * ((NC + 1) // 2) * (n + 1))
                sp.wait_ge(s["k_scr1"], 16 * (NC // 2) * (n + 1))
                for g in range(NG):
                    if n == 0 and g == 2:
                        later_loads()
                    if g >= 2:
                        sp.wait_ge(s["av_done"], TILES[layer] + RING + ST * 2 * (g - 1))
                    for j in range(G):
                        h8 = slice((g * G + j) * HD8, (g * G + j + 1) * HD8)
                        for l in range(2):
                            at = 32 * j + 2 * HD8 * l
                            sp.dma_start(kb[at:at + 2 * HD8, g % 2, :].bitcast(F32),
                                         kscr[n, l, h8, :].unsqueeze(0).to_broadcast([2, HD8, SP]))\
                                .then_inc(s[f"k_in{g % 2}"], 16)
                    if n == 0 and g == 1:
                        context_pieces()
                    if g == 0:
                        sp.wait_ge(s["q_scr"], 16 * (n + 1))
                        sp.wait_ge(s["q_zeroed"], n + 1)
                    for half in range(2):
                        if g:
                            sp.wait_ge(s["av_done"], TILES[layer] + RING + ST * (2 * (g - 1) + half + 1))
                        for j in range(G):
                            h8 = slice((g * G + j) * HD8, (g * G + j + 1) * HD8)
                            for c in range(2):
                                at = 32 * j + 2 * HD8 * c
                                sp.dma_start(qh[at:at + 2 * HD8, half, j, :].bitcast(F32),
                                             qscr[n, :, h8, half * HT:(half + 1) * HT]).then_inc(s[f"q_in{half}"], 16)

            def experts8(m, l, free):
                sp.wait_ge(s["x_ready"], free)
                if m == 1:
                    sp.dma_start(cn2[:, 0:SF, :], whole).then_inc(s["in_ctx2"], 16)
                    sp.dma_start(cn2[0:TAIL, SF, :], rows[SF * P:S, :]).then_inc(s["in_ctx2"], 16)
                with sp.Fori(0, E8 // 2) as i:
                    for u in range(2):
                        e = i * 2 + u
                        sp.wait_ge(s["eo_ready"], e + E8 * m + 1)
                        slot = vbuf[:, u * 2 * F:(u + 1) * 2 * F]
                        sp.dma_start(slot[:, 0:F], a[l + "W1"][bass.ds(e, 1), :, :].rearrange("o d f -> (o d) f"))\
                            .then_inc(s[f"moe_w{u}"], 16)
                        sp.dma_start(slot[:, F:2 * F].rearrange("p (f d) -> p f d", f=NF),
                                     a[l + "W2"][bass.ds(e, 1), :, :].rearrange("o (f p) d -> p (o f) d", p=P))\
                            .then_inc(s[f"moe_w{u}"], 16)

            attention8(0, 0)
            experts8(0, "L0_ffn_", 2)
            sp.wait_ge(s["x_ready"], 3)
            for m, (name, n) in enumerate((("Wk", C), ("Wq", D))):
                sp.dma_start(wqk1[0:n, m, :], a["L1_xattn_" + name]).then_inc(s["in_qk1"], 16)
            with sp.Fori(0, NP) as p:
                cut = bass.ds(p * P, P)
                sp.wait_ge(s["q_proj"], p * 2 + QPROJ[1])
                for e in range(2):
                    sp.dma_start(w64[:, e, :].rearrange("p (c n) -> p c n", c=2),
                                 a["L1_xattn_Wq"][:, bass.ds(p * P + e * HD64, HD64)].unsqueeze(1).to_broadcast([P, 2, HD64]))\
                        .then_inc(s["in_wq1"], 16)
                sp.wait_ge(s["v_proj"], p * NC + CHUNKED[1])
                sp.dma_start(w64[0:C, 2, :], a["L1_xattn_Wk"][:, cut]).then_inc(s["in_wkv1"], 16)
                sp.dma_start(w64[0:C, 3, :], a["L1_xattn_Wv"][:, cut]).then_inc(s["in_wkv1"], 16)
                sp.wait_ge(s["wo_ready"], p + WOUT[1])
                for e in range(2):
                    sp.dma_start(w64[HD64 * e:HD64 * (e + 1), 4:6, :],
                                 a["L1_xattn_Wo"][cut, :].rearrange("(e d) n -> d e n", e=2)).then_inc(s["in_wo1"], 16)
            attention8(1, 2)
            experts8(1, "L2_ffn_", 6)
            sp.wait_ge(s["x_ready"], 8)
            for m, name in enumerate(("gate", "up", "down")):
                sp.dma_start(shared[:, m, :], a[f"L3_ffn_shared_{name}_w"]).then_inc(s["in_shared"], 16)
            with sp.Fori(0, E16 // 2) as i:
                for u in range(2):
                    e = i * 2 + u
                    sp.wait_ge(s["wt_turned"], e + 1)
                    for m, name in enumerate(("gate", "up", "down")):
                        sp.dma_start(ex_w[u][:, m, :], a[f"L3_ffn_w_{name}"][bass.ds(e, 1), :, :].rearrange("o i d -> (o i) d"))\
                            .then_inc(s[f"ex_w{u}"], 16)
            sp.wait_ge(s["out_ready"], 1)
            sp.dma_start(a["out"].rearrange("o (p t) d -> (o p) t d", t=NT), xn).then_inc(s["out_stored"], 16)
            sp.wait_ge(s["out_stored"], 16)


INPUTS = [
    "x", "ctx_768",
    "L0_xattn_Wq", "L0_xattn_bq", "L0_xattn_Wk", "L0_xattn_bk", "L0_xattn_Wv", "L0_xattn_bv", "L0_xattn_Wo", "L0_xattn_bo",
    "L0_ffn_Wp", "L0_ffn_sim_matrix", "L0_ffn_temperature", "L0_ffn_W1", "L0_ffn_b1", "L0_ffn_W2", "L0_ffn_b2",
    "L1_xattn_Wq", "L1_xattn_Wk", "L1_xattn_Wv", "L1_xattn_Wo", "L1_xattn_bo",
    "L1_ffn_kernel", "L1_ffn_input_scale", "L1_ffn_kernel_scale", "L1_ffn_bias",
    "L2_xattn_Wq", "L2_xattn_bq", "L2_xattn_Wk", "L2_xattn_bk", "L2_xattn_Wv", "L2_xattn_bv", "L2_xattn_Wo", "L2_xattn_bo",
    "L2_ffn_gamma", "L2_ffn_beta", "L2_ffn_Wr", "L2_ffn_br", "L2_ffn_W1", "L2_ffn_b1", "L2_ffn_W2", "L2_ffn_b2",
    "L3_xattn_Wq", "L3_xattn_Wk", "L3_xattn_Wv", "L3_xattn_Wo",
    "L3_ffn_gate_w", "L3_ffn_expert_bias", "L3_ffn_w_gate", "L3_ffn_w_up", "L3_ffn_w_down",
    "L3_ffn_shared_gate_w", "L3_ffn_shared_up_w", "L3_ffn_shared_down_w",
]


def kernel(**inputs):
    import numpy as np
    import concourse.bacc as bacc
    from concourse.bass_utils import run_bass_kernel_spmd

    nc = bacc.Bacc("TRN2", target_bir_lowering=False, num_devices=1)
    arrays, dram = {}, {}
    for name in INPUTS:
        array = np.atleast_1d(np.ascontiguousarray(inputs[name]))
        arrays[f"in_{name}"] = array
        dram[name] = nc.dram_tensor(f"in_{name}", array.shape, mybir.dt.from_np(array.dtype), kind="ExternalInput").ap()
    dram["out"] = nc.dram_tensor("out_x", (1, T, D), F32, kind="ExternalOutput").ap()
    build_program(nc, dram)
    result = run_bass_kernel_spmd(nc, [arrays], core_ids=[0])
    return result.results[0]["out_x"]
```
